# Optimizing a Trainium2 kernel written in Bass

```python
import numpy as np
import jax
import jax.numpy as jnp

def _softmax(x, axis=-1):
    return jax.nn.softmax(x, axis=axis)

def _gelu(x):
    return jax.nn.gelu(x, approximate=True)

def _silu(x):
    return jax.nn.silu(x)

def _sigmoid(x):
    return jax.nn.sigmoid(x)

def _layernorm(x, axis=-1, eps=1e-05):
    m = jnp.mean(x, axis=axis, keepdims=True)
    v = jnp.var(x, axis=axis, keepdims=True)
    return (x - m) / jnp.sqrt(v + eps)

def _scatter_add(tgt, idx, src, axis=0):
    return tgt.at[idx].add(src)

def _segment_sum(src, seg, n):
    return jax.ops.segment_sum(src, seg, n)
kernel_name = 'mk_macaron_d2_jaxref_r8_4b9b11'

def setup_inputs(seed: int=0):
    np.random.seed(seed)
    _w = jnp.asarray

    def _L0_attn_setup():
        import jax, jax.numpy as jnp
        import numpy as np
        B, S, D = (4, 256, 128)
        H = 3 * D

        def _layernorm(x, g, b, eps=1e-05):
            m = jnp.mean(x, axis=-1, keepdims=True)
            v = jnp.mean(jnp.square(x - m), axis=-1, keepdims=True)
            return (x - m) * jax.lax.rsqrt(v + eps) * g + b
        key = jax.random.key(seed)
        ks = jax.random.split(key, 12)
        s = 1.0 / np.sqrt(D)
        n = lambda k, shape, sc: jax.random.normal(k, shape, jnp.float32) * sc
        return {'x': n(ks[0], (B, S, D), 1.0), 'ln1_g': jnp.ones((D,), jnp.float32), 'ln1_b': jnp.zeros((D,), jnp.float32), 'ln2_g': jnp.ones((D,), jnp.float32), 'ln2_b': jnp.zeros((D,), jnp.float32), 'Wq': n(ks[1], (D, D), s), 'bq': jnp.zeros((D,), jnp.float32), 'Wk': n(ks[2], (D, D), s), 'bk': jnp.zeros((D,), jnp.float32), 'Wv': n(ks[3], (D, D), s), 'bv': jnp.zeros((D,), jnp.float32), 'Wi': n(ks[4], (D, 1), s), 'bi': jnp.zeros((1,), jnp.float32), 'Wf': n(ks[5], (D, 1), s), 'bf': jnp.zeros((1,), jnp.float32), 'Wo': n(ks[6], (D, D), s), 'bo': jnp.zeros((D,), jnp.float32), 'W1': n(ks[7], (D, H), s), 'b1': jnp.zeros((H,), jnp.float32), 'W2': n(ks[8], (H, D), 1.0 / np.sqrt(H)), 'b2': jnp.zeros((D,), jnp.float32)}
    _L0_attn_in = _L0_attn_setup()

    def _L0_ffn_setup():
        import jax, jax.numpy as jnp
        import numpy as np
        B, S, D, F, E, R, K = (1, 64, 128, 512, 8, 16, 2)
        SCALING = 32.0 / 16.0
        EPS = 1e-06

        def _forward(x, norm_w, w1, w3, w2, gate_w, a1, b1, a3, b3, a2, b2):
            Bq, Sq, Dq = x.shape
            nx = x * jax.lax.rsqrt(jnp.mean(x * x, axis=-1, keepdims=True) + EPS) * norm_w
            t = nx.reshape(-1, Dq)
            probs = jax.nn.softmax(t @ gate_w.T, axis=-1)
            topw, topi = jax.lax.top_k(probs, K)
            topw = topw / jnp.sum(topw, axis=-1, keepdims=True)
            weights = jnp.sum(jax.nn.one_hot(topi, E, dtype=t.dtype) * topw[..., None], axis=1)
            base1 = t @ w1.T
            base3 = t @ w3.T
            h1 = base1[None] + SCALING * jnp.einsum('etr,efr->etf', jnp.einsum('td,erd->etr', t, a1), b1)
            h3 = base3[None] + SCALING * jnp.einsum('etr,efr->etf', jnp.einsum('td,erd->etr', t, a3), b3)
            act = jax.nn.silu(h1) * h3
            out_e = jnp.einsum('etf,df->etd', act, w2) + SCALING * jnp.einsum('etr,edr->etd', jnp.einsum('etf,erf->etr', act, a2), b2)
            out = jnp.einsum('te,etd->td', weights, out_e)
            return out.reshape(Bq, Sq, Dq)
        key = jax.random.key(seed)
        ks = jax.random.split(key, 12)
        w = lambda k, shape: jax.random.normal(k, shape, dtype=jnp.float32) * 0.02
        return {'x': jax.random.normal(ks[0], (B, S, D), dtype=jnp.float32), 'norm_w': jnp.ones((D,), jnp.float32), 'w1': w(ks[1], (F, D)), 'w3': w(ks[2], (F, D)), 'w2': w(ks[3], (D, F)), 'gate_w': w(ks[4], (E, D)), 'a1': w(ks[5], (E, R, D)), 'b1': w(ks[6], (E, F, R)), 'a3': w(ks[7], (E, R, D)), 'b3': w(ks[8], (E, F, R)), 'a2': w(ks[9], (E, R, F)), 'b2': w(ks[10], (E, D, R))}
    _L0_ffn_in = _L0_ffn_setup()

    def _L1_attn_setup():
        import jax, jax.numpy as jnp
        import numpy as np
        B, S, D_IN = (4, 256, 128)
        D_Q = D_K = D_V = 128
        key = jax.random.key(seed)
        ks = jax.random.split(key, 6)
        s = lambda d: 1.0 / np.sqrt(d)
        return {'x': jax.random.normal(ks[0], (B, S, D_IN), dtype=jnp.float32), 'Wk': jax.random.normal(ks[1], (D_K, D_IN), dtype=jnp.float32) * s(D_IN), 'Wq': jax.random.normal(ks[2], (D_Q, D_IN), dtype=jnp.float32) * s(D_IN), 'Wv': jax.random.normal(ks[3], (D_V, D_IN), dtype=jnp.float32) * s(D_IN), 'Wa': jax.random.normal(ks[4], (D_Q, D_K), dtype=jnp.float32) * s(D_K), 'Wb': jax.random.normal(ks[5], (D_V, D_V), dtype=jnp.float32) * s(D_V)}
    _L1_attn_in = _L1_attn_setup()

    def _L1_ffn_setup():
        import jax, jax.numpy as jnp
        import numpy as np
        B, S, D, F, E = (8, 128, 128, 512, 8)
        EPS = 1e-05
        key = jax.random.key(seed)
        ks = jax.random.split(key, 4)
        s = 0.02
        return {'input_features': jax.random.normal(ks[0], (B, S, D), jnp.float32), 'centroids': jax.random.normal(ks[1], (E, D), jnp.float32) * 0.1, 'ln_g': jnp.ones((E, D), jnp.float32), 'ln_b': jnp.zeros((E, D), jnp.float32), 'w1': jax.random.normal(ks[2], (E, D, F), jnp.float32) * s, 'b1': jnp.zeros((E, F), jnp.float32), 'w2': jax.random.normal(ks[3], (E, F, D), jnp.float32) * s, 'b2': jnp.zeros((E, D), jnp.float32)}
    _L1_ffn_in = _L1_ffn_setup()
    _d = {'L0_attn_x': _L0_attn_in['x'], 'L0_attn_ln1_g': _L0_attn_in['ln1_g'], 'L0_attn_ln1_b': _L0_attn_in['ln1_b'], 'L0_attn_ln2_g': _L0_attn_in['ln2_g'], 'L0_attn_ln2_b': _L0_attn_in['ln2_b'], 'L0_attn_Wq': _L0_attn_in['Wq'], 'L0_attn_bq': _L0_attn_in['bq'], 'L0_attn_Wk': _L0_attn_in['Wk'], 'L0_attn_bk': _L0_attn_in['bk'], 'L0_attn_Wv': _L0_attn_in['Wv'], 'L0_attn_bv': _L0_attn_in['bv'], 'L0_attn_Wi': _L0_attn_in['Wi'], 'L0_attn_bi': _L0_attn_in['bi'], 'L0_attn_Wf': _L0_attn_in['Wf'], 'L0_attn_bf': _L0_attn_in['bf'], 'L0_attn_Wo': _L0_attn_in['Wo'], 'L0_attn_bo': _L0_attn_in['bo'], 'L0_attn_W1': _L0_attn_in['W1'], 'L0_attn_b1': _L0_attn_in['b1'], 'L0_attn_W2': _L0_attn_in['W2'], 'L0_attn_b2': _L0_attn_in['b2'], 'L0_ffn_norm_w': _L0_ffn_in['norm_w'], 'L0_ffn_w1': _L0_ffn_in['w1'], 'L0_ffn_w3': _L0_ffn_in['w3'], 'L0_ffn_w2': _L0_ffn_in['w2'], 'L0_ffn_gate_w': _L0_ffn_in['gate_w'], 'L0_ffn_a1': _L0_ffn_in['a1'], 'L0_ffn_b1': _L0_ffn_in['b1'], 'L0_ffn_a3': _L0_ffn_in['a3'], 'L0_ffn_b3': _L0_ffn_in['b3'], 'L0_ffn_a2': _L0_ffn_in['a2'], 'L0_ffn_b2': _L0_ffn_in['b2'], 'L1_attn_Wk': _L1_attn_in['Wk'], 'L1_attn_Wq': _L1_attn_in['Wq'], 'L1_attn_Wv': _L1_attn_in['Wv'], 'L1_attn_Wa': _L1_attn_in['Wa'], 'L1_attn_Wb': _L1_attn_in['Wb'], 'L1_ffn_centroids': _L1_ffn_in['centroids'], 'L1_ffn_ln_g': _L1_ffn_in['ln_g'], 'L1_ffn_ln_b': _L1_ffn_in['ln_b'], 'L1_ffn_w1': _L1_ffn_in['w1'], 'L1_ffn_b1': _L1_ffn_in['b1'], 'L1_ffn_w2': _L1_ffn_in['w2'], 'L1_ffn_b2': _L1_ffn_in['b2']}
    _x0 = _d['L0_attn_x']
    _d['L0_attn_x'] = jax.random.normal(jax.random.fold_in(jax.random.key(seed), 1), (8, 512, 128), dtype=_x0.dtype)
    del _x0
    return _d

def reference(L0_attn_x, L0_attn_ln1_g, L0_attn_ln1_b, L0_attn_ln2_g, L0_attn_ln2_b, L0_attn_Wq, L0_attn_bq, L0_attn_Wk, L0_attn_bk, L0_attn_Wv, L0_attn_bv, L0_attn_Wi, L0_attn_bi, L0_attn_Wf, L0_attn_bf, L0_attn_Wo, L0_attn_bo, L0_attn_W1, L0_attn_b1, L0_attn_W2, L0_attn_b2, L0_ffn_norm_w, L0_ffn_w1, L0_ffn_w3, L0_ffn_w2, L0_ffn_gate_w, L0_ffn_a1, L0_ffn_b1, L0_ffn_a3, L0_ffn_b3, L0_ffn_a2, L0_ffn_b2, L1_attn_Wk, L1_attn_Wq, L1_attn_Wv, L1_attn_Wa, L1_attn_Wb, L1_ffn_centroids, L1_ffn_ln_g, L1_ffn_ln_b, L1_ffn_w1, L1_ffn_b1, L1_ffn_w2, L1_ffn_b2):

    def _L0_attn_ref(x, ln1_g, ln1_b, ln2_g, ln2_b, Wq, bq, Wk, bk, Wv, bv, Wi, bi, Wf, bf, Wo, bo, W1, b1, W2, b2):
        import jax, jax.numpy as jnp
        import numpy as np
        B, S, D = (4, 256, 128)
        H = 3 * D

        def _layernorm(x, g, b, eps=1e-05):
            m = jnp.mean(x, axis=-1, keepdims=True)
            v = jnp.mean(jnp.square(x - m), axis=-1, keepdims=True)
            return (x - m) * jax.lax.rsqrt(v + eps) * g + b
        seq = x.shape[1]
        h = _layernorm(x, ln1_g, ln1_b)
        q = h @ Wq + bq
        k = h @ Wk + bk
        v = h @ Wv + bv
        log_f = jax.nn.log_sigmoid(h @ Wf + bf)
        log_i = jax.nn.log_sigmoid(h @ Wi + bi)
        o = jax.nn.sigmoid(h @ Wo + bo)
        log_f_cum = jnp.cumsum(log_f, axis=1)
        log_scores = jnp.swapaxes(log_i, 1, 2) + log_f_cum - jnp.swapaxes(log_f_cum, 1, 2)
        causal = jnp.triu(jnp.full((seq, seq), -1000000000.0, jnp.float32), k=1)
        scores = jnp.exp(log_scores + causal[None])
        scores = scores / (jnp.sum(scores, axis=-1, keepdims=True) + 1e-06)
        attn = scores @ v
        x = x + o * attn
        h2 = _layernorm(x, ln2_g, ln2_b)
        m = h2 @ W1 + b1
        m = jnp.square(jnp.where(m > 0, m, 0.01 * m))
        x = x + m @ W2 + b2
        return x

    def _L0_ffn_ref(x, norm_w, w1, w3, w2, gate_w, a1, b1, a3, b3, a2, b2):
        import jax, jax.numpy as jnp
        import numpy as np
        B, S, D, F, E, R, K = (1, 64, 128, 512, 8, 16, 2)
        SCALING = 32.0 / 16.0
        EPS = 1e-06

        def _forward(x, norm_w, w1, w3, w2, gate_w, a1, b1, a3, b3, a2, b2):
            Bq, Sq, Dq = x.shape
            nx = x * jax.lax.rsqrt(jnp.mean(x * x, axis=-1, keepdims=True) + EPS) * norm_w
            t = nx.reshape(-1, Dq)
            probs = jax.nn.softmax(t @ gate_w.T, axis=-1)
            topw, topi = jax.lax.top_k(probs, K)
            topw = topw / jnp.sum(topw, axis=-1, keepdims=True)
            weights = jnp.sum(jax.nn.one_hot(topi, E, dtype=t.dtype) * topw[..., None], axis=1)
            base1 = t @ w1.T
            base3 = t @ w3.T
            h1 = base1[None] + SCALING * jnp.einsum('etr,efr->etf', jnp.einsum('td,erd->etr', t, a1), b1)
            h3 = base3[None] + SCALING * jnp.einsum('etr,efr->etf', jnp.einsum('td,erd->etr', t, a3), b3)
            act = jax.nn.silu(h1) * h3
            out_e = jnp.einsum('etf,df->etd', act, w2) + SCALING * jnp.einsum('etr,edr->etd', jnp.einsum('etf,erf->etr', act, a2), b2)
            out = jnp.einsum('te,etd->td', weights, out_e)
            return out.reshape(Bq, Sq, Dq)
        return _forward(x, norm_w, w1, w3, w2, gate_w, a1, b1, a3, b3, a2, b2)

    def _L1_attn_ref(x, Wk, Wq, Wv, Wa, Wb):
        import jax, jax.numpy as jnp
        import numpy as np
        B, S, D_IN = (4, 256, 128)
        D_Q = D_K = D_V = 128
        k = jnp.einsum('bsd,kd->bsk', x, Wk)
        q = jnp.einsum('bsd,qd->bsq', x, Wq)
        v = jnp.einsum('bsd,vd->bsv', x, Wv)
        ak = jnp.einsum('bsk,qk->bsq', k, Wa)
        e = jnp.einsum('biq,bjq->bij', q, ak)
        alpha = jax.nn.softmax(e, axis=-1)
        u = jnp.einsum('bsv,wv->bsw', v, Wb)
        out = jnp.einsum('bij,bjv->biv', alpha, u)
        return out

    def _L1_ffn_ref(input_features, centroids, ln_g, ln_b, w1, b1, w2, b2):
        import jax, jax.numpy as jnp
        import numpy as np
        B, S, D, F, E = (8, 128, 128, 512, 8)
        EPS = 1e-05
        x = input_features.reshape(-1, D)
        aff = jax.lax.stop_gradient(x @ centroids.T)
        eid = jnp.argmax(aff, axis=-1)
        alpha = jax.nn.sigmoid(jnp.sum(x * centroids[eid], axis=-1, keepdims=True))
        mu = jnp.mean(x, axis=-1, keepdims=True)
        var = jnp.mean((x - mu) ** 2, axis=-1, keepdims=True)
        xn = (x - mu) * jax.lax.rsqrt(var + EPS)
        xln = xn * ln_g[eid] + ln_b[eid]
        onehot = jax.nn.one_hot(eid, E, dtype=x.dtype)
        ffn = jnp.zeros_like(x)
        for e in range(E):
            h = jax.nn.relu(xln @ w1[e] + b1[e])
            ffn = ffn + onehot[:, e:e + 1] * (h @ w2[e] + b2[e])
        out = x + alpha * ffn
        return out.reshape(input_features.shape)
    x = L0_attn_x
    x = x + 0.5 * _L0_ffn_ref(_layernorm(x, axis=-1), L0_ffn_norm_w, L0_ffn_w1, L0_ffn_w3, L0_ffn_w2, L0_ffn_gate_w, L0_ffn_a1, L0_ffn_b1, L0_ffn_a3, L0_ffn_b3, L0_ffn_a2, L0_ffn_b2)
    x = x + _L0_attn_ref(_layernorm(x, axis=-1), L0_attn_ln1_g, L0_attn_ln1_b, L0_attn_ln2_g, L0_attn_ln2_b, L0_attn_Wq, L0_attn_bq, L0_attn_Wk, L0_attn_bk, L0_attn_Wv, L0_attn_bv, L0_attn_Wi, L0_attn_bi, L0_attn_Wf, L0_attn_bf, L0_attn_Wo, L0_attn_bo, L0_attn_W1, L0_attn_b1, L0_attn_W2, L0_attn_b2)
    x = x + 0.5 * _L0_ffn_ref(_layernorm(x, axis=-1), L0_ffn_norm_w, L0_ffn_w1, L0_ffn_w3, L0_ffn_w2, L0_ffn_gate_w, L0_ffn_a1, L0_ffn_b1, L0_ffn_a3, L0_ffn_b3, L0_ffn_a2, L0_ffn_b2)
    x = x + 0.5 * _L1_ffn_ref(_layernorm(x, axis=-1), L1_ffn_centroids, L1_ffn_ln_g, L1_ffn_ln_b, L1_ffn_w1, L1_ffn_b1, L1_ffn_w2, L1_ffn_b2)
    x = x + _L1_attn_ref(_layernorm(x, axis=-1), L1_attn_Wk, L1_attn_Wq, L1_attn_Wv, L1_attn_Wa, L1_attn_Wb)
    x = x + 0.5 * _L1_ffn_ref(_layernorm(x, axis=-1), L1_ffn_centroids, L1_ffn_ln_g, L1_ffn_ln_b, L1_ffn_w1, L1_ffn_b1, L1_ffn_w2, L1_ffn_b2)
    return x

_drawn_inputs = setup_inputs


def setup_inputs(seed=0):
    import zlib

    import numpy as np

    out = dict(_drawn_inputs(seed))
    spreads = {'L0_attn_ln1_g': (1.0, 0.2),
     'L0_attn_ln1_b': (0.0, 0.393),
     'L0_attn_ln2_g': (1.0, 0.2),
     'L0_attn_ln2_b': (0.0, 0.1),
     'L0_attn_bq': (0.0, 0.1),
     'L0_attn_bk': (0.0, 0.1),
     'L0_attn_bv': (0.0, 0.428),
     'L0_attn_bo': (0.0, 0.468),
     'L0_attn_b1': (0.0, 0.1),
     'L0_attn_b2': (0.0, 0.327),
     'L0_ffn_norm_w': (1.0, 0.6),
     'L1_ffn_ln_g': (1.0, 0.6),
     'L1_ffn_ln_b': (0.0, 2.0),
     'L1_ffn_b1': (0.0, 2.0),
     'L1_ffn_b2': (0.0, 2.0)}
    factors = {'L0_ffn_w1': 3.893,
     'L0_ffn_w3': 3.728,
     'L0_ffn_w2': 3.746,
     'L0_ffn_gate_w': 8.0,
     'L0_ffn_a1': 8.0,
     'L0_ffn_b1': 8.0,
     'L0_ffn_a3': 8.0,
     'L0_ffn_b3': 8.0,
     'L0_ffn_a2': 8.0,
     'L0_ffn_b2': 8.0,
     'L1_ffn_w1': 20.382,
     'L1_ffn_centroids': 4.28,
     'L1_ffn_w2': 4.851}
    for name, (base, spread) in spreads.items():
        noise = np.random.default_rng([zlib.crc32(name.encode()), seed]).standard_normal(out[name].shape)
        drawn = base * np.exp(spread * noise) if base else spread * noise
        out[name] = jnp.asarray(drawn.astype(out[name].dtype))
    for name, factor in factors.items():
        out[name] = (out[name] * factor).astype(out[name].dtype)
    return out
```

```python
from contextlib import ExitStack

import numpy as np
import concourse.bass as bass
from concourse import mybir

F32 = mybir.dt.float32
ALU = mybir.AluOpType
ACT = mybir.ActivationFunctionType
AX = mybir.AxisListType.X

P = 128
T = 4
S = P * T
NCH = 8
E = 8
R = 16
J = 4
JM = 3
EPS_LN, EPS_RMS, EPS_DEN = 1e-5, 1e-6, 1e-6
LORA = 2.0
STAGES = [("l0f", 0), ("l0a", 0), ("l0f", 1), ("l1f", 0), ("l1a", 0), ("l1f", 1)]


class Sem:

    def __init__(self, sem, per_chunk=1):
        self.sem, self.k = sem, per_chunk

    def __call__(self, g, n=None, ago=0):
        v = g * self.k + ((self.k if n is None else n) - ago * self.k)
        return self.sem, (max(v, 0) if isinstance(v, int) else v)


class Chunk:

    def __init__(self, c, p, call, stage):
        self.c, self.p, self.g, self.gs, self.stage = c, p, c + NCH * call, c + NCH * stage, stage


def pipeline(eng, lanes, call, stage, body):
    def at(b, p):
        return [Chunk(b - n, (p - n) % 2, call, stage)
                if not isinstance(b, int) or 0 <= b - n < NCH else None for n in range(lanes)]
    first = lanes
    pairs = (NCH - first) // 2
    for b in range(first):
        body(*at(b, b % 2))
    with eng.Fori(0, pairs) as i:
        body(*at(2 * i + first, first % 2))
        body(*at(2 * i + (first + 1), (first + 1) % 2))
    for b in range(first + 2 * pairs, NCH + lanes - 1):
        body(*at(b, b % 2))


def build(nc, d, out):
    with ExitStack() as ctx:
        def sb(name, shape, dt=F32):
            return ctx.enter_context(nc.sbuf_tensor(name, shape, dt))

        def sem(name, per_chunk=1):
            return Sem(ctx.enter_context(nc.semaphore(name)), per_chunk)

        def tok(ap):
            return ap.rearrange("p (t d) -> p t d", t=T)

        bank = [ctx.enter_context(nc.psum_tensor(f"bank{i}", [P, S], F32)) for i in range(8)]

        x = sb("x", [P, NCH * T, P])
        ident = sb("ident", [P, P])
        neghalf = sb("neghalf", [P, T]); eps_ln = sb("eps_ln", [P, T]); eps_rms = sb("eps_rms", [P, T])
        pri = sb("pri", [P, T, E])
        w1 = sb("w1", [P, J * P]); w3 = sb("w3", [P, J * P]); w2 = sb("w2", [P, J, P])
        gate = sb("gate", [P, E]); normw = sb("normw", [P, 1])
        a1 = sb("a1", [P, P]); a3 = sb("a3", [P, P]); a2 = sb("a2", [P, J, P])
        b1 = sb("b1", [P, J * P]); b3 = sb("b3", [P, J * P]); b2 = sb("b2", [P, P])
        vecs = sb("vecs", [P, 8]); bif = sb("bif", [P, 2]); wif = sb("wif", [P, 2])
        wi_b = sb("wi_b", [P, P]); wf_b = sb("wf_b", [P, P])
        wv = sb("wv", [P, P]); wo = sb("wo", [P, P])
        wm1 = sb("wm1", [P, JM * P]); bm1 = sb("bm1", [P, JM]); wm2 = sb("wm2", [P, JM, P])
        wk_l1 = sb("wk_l1", [P, P]); wq_l1 = sb("wq_l1", [P, P]); wv_l1 = sb("wv_l1", [P, P])
        waT = sb("waT", [P, P]); wbT = sb("wbT", [P, P])
        wak = sb("wak", [P, P]); gmat = sb("gmat", [P, P]); wuT = sb("wuT", [P, P])
        cen = sb("cen", [P, E]); lng = sb("lng", [E, P]); lnb = sb("lnb", [E, P])
        e1 = sb("e1", [P, E, J * P]); eb1 = sb("eb1", [P, E, J]); e2 = sb("e2", [P, E, J, P]); eb2 = sb("eb2", [E, P])

        stats = sb("stats", [P, T, 6]); mv = sb("mv", [P, T, 2]); part = sb("part", [P, 4, T])
        sc = sb("sc", [P, 8, T])
        yn = [sb(f"yn{i}", [P, T, P]) for i in range(2)]
        ys = [sb(f"ys{i}", [P, T, P]) for i in range(2)]
        tT = [sb(f"tT{i}", [P, S]) for i in range(2)]
        lg = sb("lg", [P, T, E]); lg2 = sb("lg2", [P, T, E]); gt = sb("gt", [P, T, E]); pr = sb("pr", [P, T, E])
        mx = sb("mx", [P, 4, T]); dlt = sb("dlt", [P, T]); th = sb("th", [P, T]); wts = sb("wts", [P, 2, T])
        oh = [sb(f"oh{i}", [P, T, E, R]) for i in range(2)]
        mT = [[sb(f"mT{i}{k}", [P, S]) for k in range(2)] for i in range(2)]
        mdT = sb("mdT", [P, S])
        wT = [[sb(f"wT{i}{k}", [P, S]) for k in range(2)] for i in range(2)]
        ua = [[sb(f"ua{i}{k}", [P, S]) for k in range(2)] for i in range(2)]
        ud = [[sb(f"ud{i}{k}", [P, S]) for k in range(2)] for i in range(2)]
        sil = [sb(f"sil{i}", [P, S]) for i in range(2)]
        act_ = [[sb(f"act{s}{i}", [P, S]) for i in range(2)] for s in range(2)]
        gab = [[sb(f"gab{s}{i}", [P, S]) for i in range(2)] for s in range(2)]
        gsum = [sb(f"gsum{i}", [P, S]) for i in range(2)]
        r1 = sb("r1", [P, S]); r2 = sb("r2", [P, S]); rr = sb("rr", [P, S]); oT = sb("oT", [P, S])
        hT, gi, gf, go = tT, sil[0], sil[1], act_[0][0]
        iv, num, den, rden, oaT = act_[0][1], act_[1][0], act_[1][1], gab[0][0], gab[0][1]
        z, h2, h2T = sb("z", [P, T, P]), sb("h2", [P, T, P]), gab[1][0]
        mpre, mlk, msq, moT = mT[0] + mT[1][:1], wT[0] + wT[1][:1], ua[0] + ua[1][:1], oT
        stats2 = sb("stats2", [P, T, 6]); mv2 = sb("mv2", [P, T, 2]); part2 = sb("part2", [P, 4, T]); sc2 = sb("sc2", [P, 2, T])
        hid = [sb(f"hid{i}", [P, J, S]) for i in range(2)]
        xnT, xg, xln, acc = tT, r1, [ua[0][0], ua[0][1]], z
        oh1 = [sb(f"oh1{i}", [P, T, E]) for i in range(2)]; ohT = [ud[0][0], ud[0][1]]
        inv = [sb(f"inv{i}", [P, T]) for i in range(2)]; ala = sb("ala", [P, T]); alt = sb("alt", [P, T])
        al = [sb(f"al{i}", [P, T]) for i in range(2)]
        yT, zT, pr_, pT = tT, mT[0], [act_[0][0], act_[0][1]], [act_[1][0], act_[1][1]]
        vu = [z, h2]
        mxr = sb("mxr", [P, 2]); nmx = sb("nmx", [P, 2]); rs = sb("rs", [P, 2]); rsi = sb("rsi", [P, 2]); tick = sb("tick", [P, 1])
        loads = [(t[tuple([slice(None)] * len(d[n].shape))], d[n]) for n, t in (
            ("w1", w1), ("w3", w3), ("w2", w2), ("gate", gate), ("normw", normw), ("a1", a1), ("a3", a3), ("a2", a2),
            ("b1", b1), ("b3", b3), ("b2", b2), ("wif", wif), ("wv", wv), ("wo", wo), ("wm1", wm1),
            ("bm1", bm1), ("wm2", wm2), ("wk_l1", wk_l1), ("wq_l1", wq_l1), ("wv_l1", wv_l1), ("waT", waT), ("wbT", wbT),
            ("cen", cen), ("lng", lng), ("lnb", lnb), ("e1", e1), ("eb1", eb1), ("e2", e2), ("eb2", eb2))]
        loads += [(vecs[:, 0:7], d["vecs"]), (bif[:, :], d["bif"].to_broadcast([P, 2]))]

        weights_loaded, x_loaded, x_stored = sem("weights_loaded"), sem("x_loaded"), sem("x_stored")
        zeroed, constants = sem("zeroed"), sem("constants", 4 + E)
        prod_ready, prod_saved, scaled = sem("prod_ready"), sem("prod_saved"), sem("scaled")
        x_done, bn_done, stats_ready = sem("x_done"), sem("bn_done", 3), sem("stats_ready")
        scale_steps, normed, transposed = sem("scale_steps", 8), sem("normed"), sem("transposed")
        h1_ready, h3_ready, silu_done, act_done = (sem(n, 8) for n in ("h1_ready", "h3_ready", "silu_done", "act_done"))
        weighted, summed, hidden_used = sem("weighted", 8), sem("summed", 4), sem("hidden_used", 4)
        r_steps, r_ready, out_ready, outT_saved, back_ready = (
            sem("r_steps", 2), sem("r_ready"), sem("out_ready"), sem("outT_saved"), sem("back_ready"))
        t_ready, logits_ready, logits_read, top2_steps = (
            sem("t_ready"), sem("logits_ready"), sem("logits_read"), sem("top2_steps", 9))
        onehots, delta, tanh_done, slot_w = sem("onehots", 2), sem("delta"), sem("tanh_done"), sem("slot_w", 2)
        maskT_ready, maskT_saved, mdiff_ready = sem("maskT_ready", 4), sem("maskT_saved", 4), sem("mdiff_ready")
        u_ready, u_masked, masks_weighted = sem("u_ready", 2), sem("u_masked", 4), sem("masks_weighted", 2)
        hT_saved, gates_ready, gates_saved = sem("hT_saved"), sem("gates_ready", 4), sem("gates_saved", 3)
        scan_steps, oa_ready, oab_ready = sem("scan_steps", 6), sem("oa_ready"), sem("oab_ready")
        z_ready, bn2_done, stats2_ready, scale2_steps = sem("z_ready"), sem("bn2_done", 3), sem("stats2_ready"), sem("scale2_steps", 2)
        normed2, h2T_ready, h2T_saved = sem("normed2"), sem("h2T_ready"), sem("h2T_saved")
        m_ready, m_saved, m_leaky, m_squared = sem("m_ready", 3), sem("m_saved", 3), sem("m_leaky", 3), sem("m_squared", 3)
        mo_ready, moT_saved, mback_ready, z_added = sem("mo_ready"), sem("moT_saved"), sem("mback_ready"), sem("z_added")
        xnT_ready, xnT_saved, aff_ready, aff_saved = sem("xnT_ready"), sem("xnT_saved"), sem("aff_ready"), sem("aff_saved")
        top1_steps, top1_done, alpha_arg, alpha_tanh, alpha_ready = (
            sem("top1_steps", 4), sem("top1_done"), sem("alpha_arg"), sem("alpha_tanh"), sem("alpha_ready"))
        ohT_ready, ohT_saved, lnp_ready, xln_steps, xln_ready = (
            sem("ohT_ready"), sem("ohT_saved"), sem("lnp_ready", 2), sem("xln_steps", 1), sem("xln_ready"))
        e_ready, relu_done, eo_ready, eo_added, bias_ready = (
            sem("e_ready", 32), sem("relu_done", 32), sem("eo_ready", 8), sem("eo_added", 9), sem("bias_ready"))
        y_added = sem("y_added")
        yT_ready, yT_saved, zT_ready, zT_saved, v_ready, v_saved = (
            sem("yT_ready"), sem("yT_saved"), sem("zT_ready"), sem("zT_saved"), sem("v_ready"), sem("v_saved"))
        sc_ready, max_done, nmax_done, exp_done, pT_ready, pT_saved = (
            sem(n, 4) for n in ("sc_ready", "max_done", "nmax_done", "exp_done", "pT_ready", "pT_saved"))
        rsum_done, ao_ready, ao_done = sem("rsum_done", 4), sem("ao_ready", 4), sem("ao_done", 4)

        block = ctx.enter_context(nc.Block())

        STEPS = [(0, 0), (1, 0), (0, 1), (1, 1), (2, 0), (3, 0), (2, 1), (3, 1)]
        LAST = [STEPS.index((j, 1)) + 1 for j in range(J)]
        BH1, BH3, BV, BOUT, BMISC = (0, 1), (2, 3), (4, 5), 6, 7

        def xc(ch):
            return x[:, bass.ds(ch.c * T, T), :]

        def fl(ap):
            return ap.rearrange("p t d -> p (t d)")

        @block.sync
        def _(sp):
            sp.dma_start(x[:, :, :], d["x"].rearrange("(n p) d -> p n d", p=P)).then_inc(x_loaded.sem, 16)
            for dst, src in loads:
                sp.dma_start(dst, src).then_inc(weights_loaded.sem, 16)
            o = out.rearrange("a s d -> (a s) d").rearrange("(n p) d -> p n d", p=P)
            with sp.Fori(0, NCH) as c:
                sp.wait_ge(*x_done(c + NCH * (len(STAGES) - 1)))
                sp.dma_start(o[:, bass.ds(c * T, T), :], x[:, bass.ds(c * T, T), :]).then_inc(x_stored.sem, 16)
            sp.wait_ge(x_stored.sem, 16 * NCH)

        @block.tensor
        def _(pe):
            mm, tr = nc.tensor.matmul, nc.tensor.transpose

            def transpose4(dst, src):
                for t in range(T):
                    last = tr(bank[dst][:, t * P:(t + 1) * P], src(t), ident[:, :])
                return last

            pe.wait_ge(weights_loaded.sem, 16 * len(loads))
            pe.wait_ge(*constants(0))
            mm(bank[0][:, 0:P], waT[:, :], wk_l1[:, :], start=True, stop=True).then_inc(prod_ready.sem, 1)
            mm(bank[1][:, 0:P], wv_l1[:, :], wbT[:, :], start=True, stop=True).then_inc(prod_ready.sem, 1)
            pe.wait_ge(prod_saved.sem, 1)
            mm(bank[2][:, 0:P], wq_l1[:, :], wak[:, :], start=True, stop=True).then_inc(prod_ready.sem, 1)
            pe.wait_ge(prod_saved.sem, 3)
            pe.wait_ge(scaled.sem, 5)

            def l0_ffn(pre, main, tail):
                def hidden(k):
                    if main is None:
                        return
                    (j, s), g, p = STEPS[k - 1], main.g, main.p
                    f = slice(j * P, (j + 1) * P)
                    if k == 1:
                        pe.wait_ge(*u_masked(g))
                    for i, (h, base, lora, ready, read) in enumerate(((BH1, w1, b1, h1_ready, silu_done),
                                                                      (BH3, w3, b3, h3_ready, act_done))):
                        b = bank[h[j % 2]]
                        pe.wait_ge(*read(g, k - 2))
                        if s == 0:
                            mm(b[:, :], base[:, f], tT[p][:, :], start=True, stop=False)
                            mm(b[:, :], lora[:, f], ua[p][i][:, :], start=False, stop=True).then_inc(ready.sem, 1)
                        else:
                            mm(b[:, :], lora[:, f], ud[p][i][:, :], start=False, stop=True,
                               skip_group_check=True).then_inc(ready.sem, 1)

                def down(j):
                    if main is None:
                        return
                    g = main.g
                    if j == 0:
                        pe.wait_ge(*r_ready(g, ago=1))
                        pe.wait_ge(*x_done(main.gs, ago=1))
                    pe.wait_ge(*act_done(g, LAST[j]))
                    for s in range(2):
                        mm(bank[BV[s]][:, :], a2[:, j, :], act_[s][j % 2][:, :], start=j == 0, stop=j == J - 1)
                    pe.wait_ge(*summed(g, j + 1))
                    mm(bank[BOUT][:, :], w2[:, j, :], gsum[j % 2][:, :], start=j == 0, stop=False
                       ).then_inc(hidden_used.sem, 1)

                def mask(n, src):
                    if pre is None:
                        return
                    if n:
                        pe.wait_ge(*maskT_saved(pre.g, n))
                    transpose4(BMISC, src).then_inc(maskT_ready.sem, 1)

                def up(i):
                    if pre is None:
                        return
                    if i == 0:
                        pe.wait_ge(*maskT_saved(pre.g))
                    else:
                        pe.wait_ge(*u_masked(pre.g, 2))
                    mm(bank[BMISC][:, :], (a1, a3)[i][:, :], tT[pre.p][:, :], start=True, stop=True).then_inc(u_ready.sem, 1)

                hidden(1)
                if tail is not None:
                    pe.wait_ge(*r_ready(tail.g))
                    mm(bank[BOUT][:, :], b2[:, :], rr[:, :], start=False, stop=True).then_inc(out_ready.sem, 1)
                if pre is not None:
                    pe.wait_ge(*normed(pre.gs))
                    pe.wait_ge(*u_masked(pre.g, ago=1))
                    transpose4(BMISC, lambda t: yn[pre.p][:, t, :]).then_inc(transposed.sem, 1)
                hidden(2)
                if tail is not None:
                    pe.wait_ge(*outT_saved(tail.g))
                    transpose4(BOUT, lambda t: oT[:, t * P:(t + 1) * P]).then_inc(back_ready.sem, 1)
                hidden(3)
                if pre is not None:
                    pe.wait_ge(*t_ready(pre.g))
                    for t in range(T):
                        last = mm(bank[BMISC][:, t * E:(t + 1) * E], tT[pre.p][:, t * P:(t + 1) * P], gate[:, :],
                                  start=True, stop=True)
                    last.then_inc(logits_ready.sem, 1)
                hidden(4)
                hidden(5)
                down(0)
                if pre is not None:
                    pe.wait_ge(*onehots(pre.g))
                mask(0, lambda t: oh[0][:, t, :, :].rearrange("p e r -> p (e r)"))
                hidden(6)
                mask(1, lambda t: oh[1][:, t, :, :].rearrange("p e r -> p (e r)"))
                down(1)
                if pre is not None:
                    pe.wait_ge(*slot_w(pre.g))
                mask(2, lambda t: wts[:, 0, t:t + 1].to_broadcast([P, P]))
                hidden(7)
                mask(3, lambda t: wts[:, 1, t:t + 1].to_broadcast([P, P]))
                hidden(8)
                up(0)
                down(2)
                up(1)
                down(3)

            def l0_attn(pre, gat, mlp):
                if mlp is not None:
                    pe.wait_ge(*oa_ready(mlp.g))
                    pe.wait_ge(*x_done(mlp.gs, ago=1))
                    transpose4(4, lambda t: oaT[:, t * P:(t + 1) * P]).then_inc(oab_ready.sem, 1)
                if pre is not None:
                    pe.wait_ge(*normed(pre.gs))
                    pe.wait_ge(*hT_saved(pre.g, ago=1))
                    transpose4(7, lambda t: yn[pre.p][:, t, :]).then_inc(transposed.sem, 1)
                if gat is not None:
                    pe.wait_ge(*hT_saved(gat.g))
                    pe.wait_ge(*gates_saved(gat.g, ago=1))
                    pe.wait_ge(*scan_steps(gat.g, 1, ago=1))
                    for b, w in ((1, wi_b), (2, wf_b), (3, wo), (0, wv)):
                        mm(bank[b][:, :], w[:, :], hT[gat.p][:, :], start=True, stop=True).then_inc(gates_ready.sem, 1)
                if mlp is not None:
                    g = mlp.g
                    pe.wait_ge(*normed2(g))
                    transpose4(4, lambda t: h2[:, t, :]).then_inc(h2T_ready.sem, 1)
                    pe.wait_ge(*h2T_saved(g))
                    for j in range(JM):
                        if j == 2:
                            pe.wait_ge(*m_saved(g, 1))
                        elif j == 0:
                            pe.wait_ge(*m_saved(g, 3, ago=1))
                        mm(bank[5 + j % 2][:, :], wm1[:, j * P:(j + 1) * P], h2T[:, :], start=True, stop=True
                           ).then_inc(m_ready.sem, 1)
                    for j in range(JM):
                        pe.wait_ge(*m_squared(g, j + 1))
                        last = mm(bank[4][:, :], wm2[:, j, :], msq[j][:, :], start=j == 0, stop=j == JM - 1)
                    last.then_inc(mo_ready.sem, 1)
                    pe.wait_ge(*moT_saved(g))
                    transpose4(4, lambda t: moT[:, t * P:(t + 1) * P]).then_inc(mback_ready.sem, 1)

            def l1_ffn(pre, main):
                def experts(first, last_e):
                    if main is None:
                        return
                    g, p = main.g, main.p
                    for e in range(first, last_e):
                        for j in range(J):
                            n = e * J + j + 1
                            pe.wait_ge(*relu_done(g, n - 4))
                            mm(bank[j][:, :], e1[:, e, j * P:(j + 1) * P], xln[p][:, :], start=True, stop=True
                               ).then_inc(e_ready.sem, 1)
                        if e:
                            outputs(e - 1)
                    if last_e == E:
                        outputs(E - 1)

                def outputs(e):
                    g = main.g
                    pe.wait_ge(*relu_done(g, (e + 1) * J))
                    pe.wait_ge(*eo_added(g, e) if e >= 1 else y_added(g, ago=1))
                    for t in range(T):
                        for j in range(J):
                            last = mm(bank[4 + e % 2][:, t * P:(t + 1) * P], hid[e % 2][:, j, t * P:(t + 1) * P],
                                      e2[:, e, j, :], start=j == 0, stop=j == J - 1)
                    last.then_inc(eo_ready.sem, 1)

                if main is not None:
                    pe.wait_ge(*xln_ready(main.g))
                    pe.wait_ge(*eo_added(main.g, 1, ago=1))
                    for t in range(T):
                        last = mm(bank[7][:, t * P:(t + 1) * P], ohT[main.p][0:E, t * P:(t + 1) * P], eb2[0:E, :],
                                  start=True, stop=True)
                    last.then_inc(bias_ready.sem, 1)
                experts(0, 1)
                if pre is not None:
                    pe.wait_ge(*normed(pre.gs))
                    pe.wait_ge(*xln_ready(pre.g, ago=1))
                    transpose4(6, lambda t: yn[pre.p][:, t, :]).then_inc(transposed.sem, 1)
                experts(1, 2)
                if pre is not None:
                    pe.wait_ge(*xnT_saved(pre.g))
                    for t in range(T):
                        last = mm(bank[6][:, t * E:(t + 1) * E], xnT[pre.p][:, t * P:(t + 1) * P], cen[:, :],
                                  start=True, stop=True)
                    last.then_inc(aff_ready.sem, 1)
                experts(2, 4)
                if pre is not None:
                    pe.wait_ge(*top1_done(pre.g))
                    for t in range(T):
                        last = tr(bank[6][0:E, t * P:(t + 1) * P], oh1[pre.p][:, t, :], ident[:, :])
                    last.then_inc(ohT_ready.sem, 1)
                experts(4, 5)
                if pre is not None:
                    pe.wait_ge(*ohT_saved(pre.g))
                    mm(bank[6][:, :], lng[0:E, :], ohT[pre.p][0:E, :], start=True, stop=True).then_inc(lnp_ready.sem, 1)
                experts(5, 6)
                if pre is not None:
                    pe.wait_ge(*xln_steps(pre.g))
                    mm(bank[6][:, :], lnb[0:E, :], ohT[pre.p][0:E, :], start=True, stop=True).then_inc(lnp_ready.sem, 1)
                experts(6, 8)

            def l1_attn(pre, main):
                if pre is not None:
                    pe.wait_ge(*normed(pre.gs))
                    pe.wait_ge(*v_saved(pre.g, ago=1))
                    transpose4(7, lambda t: yn[pre.p][:, t, :]).then_inc(transposed.sem, 1)
                if main is not None:
                    g, p = main.g, main.p
                    for i in range(T + 1):
                        if i < T:
                            pe.wait_ge(*exp_done(g, i - 1))
                            mm(bank[i % 2][:, :], zT[p][:, i * P:(i + 1) * P], yT[p][:, :], start=True, stop=True
                               ).then_inc(sc_ready.sem, 1)
                        if i == 0:
                            continue
                        i1 = i - 1
                        pe.wait_ge(*exp_done(g, i1 + 1))
                        pe.wait_ge(*pT_saved(g, i1 - 1))
                        transpose4(2 + i1 % 2, lambda t: pr_[i1 % 2][:, t * P:(t + 1) * P]).then_inc(pT_ready.sem, 1)
                        pe.wait_ge(*pT_saved(g, i1 + 1))
                        pe.wait_ge(*ao_done(g, i1 - 1))
                        for t in range(T):
                            last = mm(bank[4 + i1 % 2][:, 0:P], pT[i1 % 2][:, t * P:(t + 1) * P], vu[p][:, t, :],
                                      start=t == 0, stop=t == T - 1)
                        last.then_inc(ao_ready.sem, 1)
                if pre is not None:
                    pe.wait_ge(*yT_saved(pre.g))
                    mm(bank[7][:, :], gmat[:, :], yT[pre.p][:, :], start=True, stop=True).then_inc(zT_ready.sem, 1)
                    pe.wait_ge(*zT_saved(pre.g))
                    for t in range(T):
                        last = mm(bank[7][:, t * P:(t + 1) * P], yT[pre.p][:, t * P:(t + 1) * P], wuT[:, :],
                                  start=True, stop=True)
                    last.then_inc(v_ready.sem, 1)

            for stage, (kind, call) in enumerate(STAGES):
                pe.wait_ge(*x_done(NCH * stage - 1))
                lanes, body = {"l0f": (3, l0_ffn), "l0a": (3, l0_attn), "l1f": (2, l1_ffn), "l1a": (2, l1_attn)}[kind]
                pipeline(pe, lanes, call, stage, body)

        @block.scalar
        def _(act):
            af = nc.scalar.activation

            act.wait_ge(weights_loaded.sem, 16 * len(loads))
            for w in (b1, b3, b2):
                af(w[:, :], w[:, :], ACT.Copy, scale=LORA).then_inc(scaled.sem, 1)
            for n, w in enumerate((wi_b, wf_b)):
                af(w[:, :], wif[:, n:n + 1].to_broadcast([P, P]), ACT.Copy).then_inc(scaled.sem, 1)
            act.wait_ge(prod_ready.sem, 2)
            af(wak[:, :], bank[0][:, 0:P], ACT.Copy).then_inc(prod_saved.sem, 1)
            af(wuT[:, :], bank[1][:, 0:P], ACT.Copy).then_inc(prod_saved.sem, 1)
            act.wait_ge(prod_ready.sem, 3)
            af(gmat[:, :], bank[2][:, 0:P], ACT.Copy).then_inc(prod_saved.sem, 1)

            def l0_ffn(pre, main, tail):
                def silu(k):
                    if main is None:
                        return
                    g = main.g
                    act.wait_ge(*h1_ready(g, k))
                    act.wait_ge(*act_done(g, k - 2))
                    af(sil[(k - 1) % 2][:, :], bank[BH1[STEPS[k - 1][0] % 2]][:, :], ACT.Silu).then_inc(silu_done.sem, 1)

                def mask(n, dst):
                    if pre is None:
                        return
                    act.wait_ge(*maskT_ready(pre.g, n + 1))
                    if n == 0:
                        act.wait_ge(*mdiff_ready(pre.g, ago=1))
                    act.wait_ge(*r_ready(pre.g, ago=2))
                    af(dst[:, :], bank[BMISC][:, :], ACT.Copy).then_inc(maskT_saved.sem, 1)

                silu(1)
                if tail is not None:
                    act.wait_ge(*out_ready(tail.g))
                    act.wait_ge(*back_ready(tail.g, ago=1))
                    af(oT[:, :], bank[BOUT][:, :], ACT.Copy).then_inc(outT_saved.sem, 1)
                if pre is not None:
                    act.wait_ge(*transposed(pre.gs))
                    act.wait_ge(*hidden_used(pre.g, ago=2))
                    af(tT[pre.p][:, :], bank[BMISC][:, :], ACT.Copy, scale=normw[:, 0:1]).then_inc(t_ready.sem, 1)
                silu(2)
                silu(3)
                silu(4)
                if pre is not None:
                    act.wait_ge(*delta(pre.g))
                    act.wait_ge(*maskT_ready(pre.g, ago=1))
                    af(th[:, :], dlt[:, :], ACT.Tanh, scale=0.5).then_inc(tanh_done.sem, 1)
                    act.wait_ge(*tanh_done(pre.g))
                    af(wts[:, 0, :], th[:, :], ACT.Copy, scale=-0.5, bias=0.5).then_inc(slot_w.sem, 1)
                    af(wts[:, 1, :], th[:, :], ACT.Copy, scale=0.5, bias=0.5).then_inc(slot_w.sem, 1)
                silu(5)
                mask(0, mT[pre.p][0] if pre is not None else None)
                silu(6)
                mask(1, mT[pre.p][1] if pre is not None else None)
                silu(7)
                mask(2, wT[pre.p][0] if pre is not None else None)
                silu(8)
                mask(3, wT[pre.p][1] if pre is not None else None)

            def l0_attn(pre, gat, mlp):
                if pre is not None:
                    act.wait_ge(*transposed(pre.gs))
                    act.wait_ge(*gates_ready(pre.g, ago=2))
                    af(hT[pre.p][:, :], bank[7][:, :], ACT.Identity, bias=vecs[:, 1:2], scale=vecs[:, 0:1]
                       ).then_inc(hT_saved.sem, 1)
                if gat is not None:
                    g = gat.g
                    act.wait_ge(*oa_ready(g, ago=1))
                    for n, (b, dst, bias) in enumerate(((1, gi, bif[:, 0:1]), (2, gf, bif[:, 1:2]), (3, go, vecs[:, 5:6]))):
                        act.wait_ge(*gates_ready(g, n + 1))
                        af(dst[:, :], bank[b][:, :], ACT.Sigmoid, bias=bias).then_inc(gates_saved.sem, 1)
                if mlp is not None:
                    g = mlp.g
                    act.wait_ge(*h2T_ready(g))
                    af(h2T[:, :], bank[4][:, :], ACT.Identity, bias=vecs[:, 3:4], scale=vecs[:, 2:3]).then_inc(h2T_saved.sem, 1)
                    act.wait_ge(*m_leaky(g, ago=1))
                    for j in range(JM):
                        act.wait_ge(*m_ready(g, j + 1))
                        af(mpre[j][:, :], bank[5 + j % 2][:, :], ACT.Identity, bias=bm1[:, j:j + 1]).then_inc(m_saved.sem, 1)
                    for j in range(JM):
                        act.wait_ge(*m_leaky(g, j + 1))
                        af(msq[j][:, :], mlk[j][:, :], ACT.Square).then_inc(m_squared.sem, 1)
                    act.wait_ge(*mo_ready(g))
                    af(moT[:, :], bank[4][:, :], ACT.Identity, bias=vecs[:, 6:7]).then_inc(moT_saved.sem, 1)

            def l1_ffn(pre, main):
                def relu(e):
                    if main is None:
                        return
                    g = main.g
                    act.wait_ge(*eo_ready(g, e - 1))
                    for j in range(J):
                        act.wait_ge(*e_ready(g, e * J + j + 1))
                        af(hid[e % 2][:, j, :], bank[j][:, :], ACT.Relu, bias=eb1[:, e, j:j + 1]).then_inc(relu_done.sem, 1)

                relu(0)
                if pre is not None:
                    act.wait_ge(*transposed(pre.gs))
                    act.wait_ge(*xln_ready(pre.g, ago=2))
                    af(xnT[pre.p][:, :], bank[6][:, :], ACT.Copy).then_inc(xnT_saved.sem, 1)
                relu(1)
                relu(2)
                if pre is not None:
                    act.wait_ge(*alpha_arg(pre.g))
                    af(alt[:, :], ala[:, :], ACT.Tanh, scale=0.5).then_inc(alpha_tanh.sem, 1)
                for e in range(3, E):
                    relu(e)

            def l1_attn(pre, main):
                if pre is not None:
                    act.wait_ge(*transposed(pre.gs))
                    act.wait_ge(*ao_ready(pre.g, ago=2))
                    af(yT[pre.p][:, :], bank[7][:, :], ACT.Copy).then_inc(yT_saved.sem, 1)
                if main is not None:
                    g = main.g
                    for i in range(T + 1):
                        if i < T:
                            act.wait_ge(*nmax_done(g, i + 1))
                            act.wait_ge(*pT_ready(g, i - 1))
                            act.wait_ge(*rsum_done(g, i - 1))
                            af(pr_[i % 2][:, :], bank[i % 2][:, :], ACT.Exp, bias=nmx[:, i % 2:i % 2 + 1],
                               accum_out=rs[:, i % 2:i % 2 + 1]).then_inc(exp_done.sem, 1)
                        if i:
                            act.wait_ge(*pT_ready(g, i))
                            act.wait_ge(*ao_ready(g, i - 2))
                            af(pT[(i - 1) % 2][:, :], bank[2 + (i - 1) % 2][:, :], ACT.Copy).then_inc(pT_saved.sem, 1)
                if pre is not None:
                    act.wait_ge(*zT_ready(pre.g))
                    af(zT[pre.p][:, :], bank[7][:, :], ACT.Copy).then_inc(zT_saved.sem, 1)
                    act.wait_ge(*v_ready(pre.g))
                    af(fl(vu[pre.p]), bank[7][:, :], ACT.Copy).then_inc(v_saved.sem, 1)

            for stage, (kind, call) in enumerate(STAGES):
                act.wait_ge(*x_done(NCH * stage - 1))
                lanes, body = {"l0f": (3, l0_ffn), "l0a": (3, l0_attn), "l1f": (2, l1_ffn), "l1a": (2, l1_attn)}[kind]
                pipeline(act, lanes, call, stage, body)

        @block.vector
        def _(dve):
            v = nc.vector
            bc = lambda ap: ap.unsqueeze(2).to_broadcast([P, T, E])

            def aggregate(g, halves, tmp, meanvar, done, ready):
                even, odd = (lambda n: halves[:, :, n]), (lambda n: halves[:, :, 3 + n])
                dve.wait_ge(*done(g, 1))
                v.tensor_tensor(tmp[:, 0, :], even(1), odd(1), ALU.add)
                v.tensor_tensor(tmp[:, 1, :], even(1), odd(1), ALU.subtract)
                v.tensor_tensor(tmp[:, 2, :], even(2), odd(2), ALU.add).then_inc(done.sem, 1)
                dve.wait_ge(*done(g, 2))
                v.tensor_scalar(meanvar[:, :, 0], tmp[:, 0, :], 0.5, None, ALU.mult)
                v.scalar_tensor_tensor(tmp[:, 3, :], tmp[:, 1, :], 0.25, tmp[:, 1, :], ALU.mult, ALU.mult).then_inc(done.sem, 1)
                dve.wait_ge(*done(g, 3))
                v.scalar_tensor_tensor(meanvar[:, :, 1], tmp[:, 2, :], 1.0 / P, tmp[:, 3, :], ALU.mult, ALU.add
                                       ).then_inc(ready.sem, 1)

            def statistics(pre):
                if pre is None:
                    return
                if pre.stage:
                    dve.wait_ge(*x_done(pre.gs, ago=NCH))
                dve.wait_ge(*scale_steps(pre.gs, ago=1))
                for t in range(T):
                    last = v.bn_stats(stats[:, t, :], xc(pre)[:, t, :])
                last.then_inc(bn_done.sem, 1)
                aggregate(pre.gs, stats, part, mv, bn_done, stats_ready)

            def normalise(pre, row, residual, inverse=False):
                if pre is None:
                    return
                dve.wait_ge(*scale_steps(pre.gs))
                dve.wait_ge(*transposed(pre.gs, ago=2))
                if inverse:
                    v.tensor_copy(inv[pre.p][:, :], sc[:, 7, :])
                for on, dst, r in ((residual, ys, 1), (True, yn, row)):
                    for t in range(T * on):
                        last = v.tensor_scalar(dst[pre.p][:, t, :], xc(pre)[:, t, :], mv[:, t, 0:1], sc[:, r, t:t + 1],
                                               ALU.subtract, ALU.mult)
                last.then_inc(normed.sem, 1)

            def l0_ffn(pre, main, tail):
                def hidden(k):
                    if main is None:
                        return
                    (j, s), g, p = STEPS[k - 1], main.g, main.p
                    dve.wait_ge(*silu_done(g, k))
                    dve.wait_ge(*h3_ready(g, k))
                    dve.wait_ge(*hidden_used(g, j - 1))
                    a = act_[s][j % 2]
                    v.tensor_tensor(a[:, :], bank[BH3[j % 2]][:, :], sil[(k - 1) % 2][:, :], ALU.mult).then_inc(act_done.sem, 1)
                    dve.wait_ge(*act_done(g, k))
                    dve.wait_ge(*summed(g, j - 1))
                    if k == 1:
                        dve.wait_ge(*maskT_saved(g))
                    v.tensor_tensor(gab[s][j % 2][:, :], a[:, :], wT[p][s][:, :], ALU.mult).then_inc(weighted.sem, 1)

                def top2():
                    g = pre.g

                    def link(ins, n):
                        ins.then_inc(top2_steps.sem, 1)
                        dve.wait_ge(*top2_steps(g, n))

                    dve.wait_ge(*logits_ready(g))
                    dve.wait_ge(*maskT_ready(g, ago=1))
                    v.tensor_copy(lg[:, :, :].rearrange("p t e -> p (t e)"), bank[BMISC][:, 0:T * E]).then_inc(logits_read.sem, 1)
                    dve.wait_ge(*logits_read(g))
                    n = 0
                    for s, l in enumerate((lg, lg2)):
                        link(v.tensor_reduce(mx[:, 2 * s, :], l[:, :, :], AX, ALU.max), n + 1)
                        link(v.tensor_tensor(gt[:, :, :], l[:, :, :], bc(mx[:, 2 * s, :]), ALU.is_ge), n + 2)
                        link(v.tensor_tensor(pr[:, :, :], gt[:, :, :], pri[:, :, :], ALU.mult), n + 3)
                        link(v.tensor_reduce(mx[:, 2 * s + 1, :], pr[:, :, :], AX, ALU.max), n + 4)
                        for t in range(T):
                            last = v.tensor_tensor(oh[s][:, t, :, :], pr[:, t, :].unsqueeze(2).to_broadcast([P, E, R]),
                                                   mx[:, 2 * s + 1, t:t + 1].unsqueeze(2).to_broadcast([P, E, R]), ALU.is_equal)
                        last.then_inc(onehots.sem, 1)
                        if s == 0:
                            dve.wait_ge(*onehots(g, 1))
                            link(v.scalar_tensor_tensor(lg2[:, :, :], oh[0][:, :, :, 0], -3e38, lg[:, :, :],
                                                        ALU.mult, ALU.add), 5)
                            n = 5
                    dve.wait_ge(*tanh_done(g, ago=1))
                    v.tensor_tensor(dlt[:, :], mx[:, 2, :], mx[:, 0, :], ALU.subtract).then_inc(delta.sem, 1)

                def masked(i):
                    if pre is None:
                        return
                    g, p = pre.g, pre.p
                    dve.wait_ge(*u_ready(g, i + 1))
                    dve.wait_ge(*mdiff_ready(g))
                    dve.wait_ge(*h3_ready(g, ago=2))
                    v.tensor_tensor(ua[p][i][:, :], bank[BMISC][:, :], mT[p][0][:, :], ALU.mult).then_inc(u_masked.sem, 1)
                    v.tensor_tensor(ud[p][i][:, :], bank[BMISC][:, :], mdT[:, :], ALU.mult).then_inc(u_masked.sem, 1)

                statistics(pre)
                hidden(1)
                normalise(pre, 6, False)
                hidden(2)
                if tail is not None:
                    dve.wait_ge(*back_ready(tail.g))
                    v.scalar_tensor_tensor(xc(tail), tok(bank[BOUT][:, :]), 0.5, xc(tail), ALU.mult, ALU.add
                                           ).then_inc(x_done.sem, 1)
                hidden(3)
                if pre is not None:
                    top2()
                for k in range(4, 9):
                    hidden(k)
                masked(0)
                masked(1)
                if main is not None:
                    g, p = main.g, main.p
                    dve.wait_ge(*hidden_used(g))
                    dve.wait_ge(*masks_weighted(g))
                    dve.wait_ge(*out_ready(g, ago=1))
                    v.tensor_tensor(r1[:, :], bank[BV[0]][:, :], mT[p][0][:, :], ALU.mult)
                    v.tensor_tensor(r2[:, :], bank[BV[1]][:, :], mT[p][1][:, :], ALU.mult).then_inc(r_steps.sem, 2)
                    dve.wait_ge(*r_steps(g))
                    v.tensor_tensor(rr[:, :], r1[:, :], r2[:, :], ALU.add).then_inc(r_ready.sem, 1)

            def l0_attn(pre, gat, mlp):
                if mlp is not None:
                    g = mlp.g
                    dve.wait_ge(*oab_ready(g))
                    v.tensor_tensor(z[:, :, :], tok(bank[4][:, :]), ys[mlp.p][:, :, :], ALU.add).then_inc(z_ready.sem, 1)
                    dve.wait_ge(*z_ready(g))
                    for t in range(T):
                        last = v.bn_stats(stats2[:, t, :], z[:, t, :])
                    last.then_inc(bn2_done.sem, 1)
                    aggregate(g, stats2, part2, mv2, bn2_done, stats2_ready)
                    v.tensor_tensor(xc(mlp), xc(mlp), z[:, :, :], ALU.add).then_inc(z_added.sem, 1)
                statistics(pre)
                if mlp is not None:
                    g = mlp.g
                    dve.wait_ge(*scale2_steps(g))
                    dve.wait_ge(*h2T_ready(g, ago=1))
                    for t in range(T):
                        last = v.tensor_scalar(h2[:, t, :], z[:, t, :], mv2[:, t, 0:1], sc2[:, 1, t:t + 1],
                                               ALU.subtract, ALU.mult)
                    last.then_inc(normed2.sem, 1)
                normalise(pre, 6, True)
                if gat is not None:
                    g = gat.g
                    dve.wait_ge(*gates_saved(g))
                    dve.wait_ge(*gates_ready(g))
                    v.scalar_tensor_tensor(iv[:, :], bank[0][:, :], vecs[:, 4:5], gi[:, :], ALU.add, ALU.mult
                                           ).then_inc(scan_steps.sem, 1)
                    v.tensor_tensor_scan(den[:, :], gf[:, :], gi[:, :], 0.0, ALU.mult, ALU.add).then_inc(scan_steps.sem, 1)
                    dve.wait_ge(*scan_steps(g, 1))
                    v.tensor_tensor_scan(num[:, :], gf[:, :], iv[:, :], 0.0, ALU.mult, ALU.add).then_inc(scan_steps.sem, 1)
                    dve.wait_ge(*scan_steps(g, 2))
                    v.tensor_scalar(den[:, :], den[:, :], EPS_DEN, None, ALU.add).then_inc(scan_steps.sem, 1)
                    dve.wait_ge(*scan_steps(g, 4))
                    v.reciprocal(rden[:, :], den[:, :]).then_inc(scan_steps.sem, 1)
                    v.tensor_tensor(num[:, :], num[:, :], go[:, :], ALU.mult).then_inc(scan_steps.sem, 1)
                    dve.wait_ge(*scan_steps(g, 6))
                    dve.wait_ge(*oab_ready(g, ago=1))
                    v.tensor_tensor(oaT[:, :], num[:, :], rden[:, :], ALU.mult).then_inc(oa_ready.sem, 1)
                if mlp is not None:
                    g = mlp.g
                    for j in range(JM):
                        dve.wait_ge(*m_saved(g, j + 1))
                        dve.wait_ge(*m_squared(g, ago=1))
                        v.scalar_tensor_tensor(mlk[j][:, :], mpre[j][:, :], 0.01, mpre[j][:, :], ALU.mult, ALU.max
                                               ).then_inc(m_leaky.sem, 1)
                    dve.wait_ge(*mback_ready(g))
                    dve.wait_ge(*z_added(g))
                    v.tensor_tensor(xc(mlp), tok(bank[4][:, :]), xc(mlp), ALU.add).then_inc(x_done.sem, 1)

            def l1_ffn(pre, main):
                def add(first, last_e):
                    if main is None:
                        return
                    g, p = main.g, main.p
                    for e in range(first, last_e):
                        dve.wait_ge(*eo_ready(g, e + 1))
                        dve.wait_ge(*eo_added(g, e + 1))
                        for t in range(T):
                            last = v.scalar_tensor_tensor(acc[:, t, :], bank[4 + e % 2][:, t * P:(t + 1) * P],
                                                          oh1[p][:, t, e:e + 1], acc[:, t, :], ALU.mult, ALU.add)
                        last.then_inc(eo_added.sem, 1)

                if main is not None:
                    dve.wait_ge(*bias_ready(main.g))
                    dve.wait_ge(*y_added(main.g, ago=1))
                    v.tensor_copy(fl(acc), bank[7][:, :]).then_inc(eo_added.sem, 1)
                statistics(pre)
                normalise(pre, 6, True, inverse=True)
                add(0, 1)
                if pre is not None:
                    g, p = pre.g, pre.p

                    def link(ins, n):
                        ins.then_inc(top1_steps.sem, 1)
                        dve.wait_ge(*top1_steps(g, n))

                    dve.wait_ge(*aff_ready(g))
                    v.tensor_copy(lg[:, :, :].rearrange("p t e -> p (t e)"), bank[6][:, 0:T * E]).then_inc(aff_saved.sem, 1)
                    dve.wait_ge(*aff_saved(g))
                    link(v.tensor_reduce(mx[:, 0, :], lg[:, :, :], AX, ALU.max), 1)
                    dve.wait_ge(*alpha_tanh(g, ago=1))
                    v.tensor_tensor(ala[:, :], mx[:, 0, :], inv[p][:, :], ALU.mult).then_inc(alpha_arg.sem, 1)
                    link(v.tensor_tensor(gt[:, :, :], lg[:, :, :], bc(mx[:, 0, :]), ALU.is_ge), 2)
                    link(v.tensor_tensor(pr[:, :, :], gt[:, :, :], pri[:, :, :], ALU.mult), 3)
                    link(v.tensor_reduce(mx[:, 1, :], pr[:, :, :], AX, ALU.max), 4)
                    v.tensor_tensor(oh1[p][:, :, :], pr[:, :, :], bc(mx[:, 1, :]), ALU.is_equal).then_inc(top1_done.sem, 1)
                add(1, 3)
                if pre is not None:
                    g, p = pre.g, pre.p
                    dve.wait_ge(*alpha_tanh(g))
                    v.tensor_scalar(al[p][:, :], alt[:, :], 0.25, 0.25, ALU.mult, ALU.add).then_inc(alpha_ready.sem, 1)
                    dve.wait_ge(*ohT_ready(g))
                    v.tensor_copy(ohT[p][0:E, :], bank[6][0:E, :]).then_inc(ohT_saved.sem, 1)
                add(3, 4)
                if pre is not None:
                    dve.wait_ge(*lnp_ready(g, 1))
                    v.tensor_tensor(xg[:, :], bank[6][:, :], xnT[p][:, :], ALU.mult).then_inc(xln_steps.sem, 1)
                add(4, 5)
                if pre is not None:
                    dve.wait_ge(*lnp_ready(g, 2))
                    dve.wait_ge(*xln_steps(g))
                    dve.wait_ge(*e_ready(g, ago=2))
                    v.tensor_tensor(xln[p][:, :], bank[6][:, :], xg[:, :], ALU.add).then_inc(xln_ready.sem, 1)
                add(5, 8)
                if main is not None:
                    g, p = main.g, main.p
                    dve.wait_ge(*eo_added(g))
                    dve.wait_ge(*alpha_ready(g))
                    for t in range(T):
                        last = v.scalar_tensor_tensor(xc(main)[:, t, :], acc[:, t, :], al[p][:, t:t + 1], xc(main)[:, t, :],
                                                      ALU.mult, ALU.add)
                    last.then_inc(y_added.sem, 1)
                    dve.wait_ge(*y_added(g))
                    v.scalar_tensor_tensor(xc(main), ys[p][:, :, :], 0.5, xc(main), ALU.mult, ALU.add).then_inc(x_done.sem, 1)

            def l1_attn(pre, main):
                statistics(pre)
                normalise(pre, 1, False)
                if main is not None:
                    g = main.g
                    for i in range(T + 1):
                        if i < T:
                            k = slice(i % 2, i % 2 + 1)
                            dve.wait_ge(*sc_ready(g, i + 1))
                            dve.wait_ge(*exp_done(g, i - 1))
                            v.tensor_reduce(mxr[:, k], bank[i % 2][:, :], AX, ALU.max).then_inc(max_done.sem, 1)
                            dve.wait_ge(*max_done(g, i + 1))
                            v.tensor_scalar(nmx[:, k], mxr[:, k], -1.0, None, ALU.mult).then_inc(nmax_done.sem, 1)
                        if i:
                            k = slice((i - 1) % 2, (i - 1) % 2 + 1)
                            dve.wait_ge(*exp_done(g, i))
                            v.reciprocal(rsi[:, k], rs[:, k]).then_inc(rsum_done.sem, 1)
                            dve.wait_ge(*rsum_done(g, i))
                            dve.wait_ge(*ao_ready(g, i))
                            xi = xc(main)[:, i - 1, :]
                            v.scalar_tensor_tensor(xi, bank[4 + (i - 1) % 2][:, 0:P], rsi[:, k], xi, ALU.mult, ALU.add
                                                   ).then_inc(ao_done.sem, 1)
                    dve.wait_ge(*ao_done(g))
                    v.tensor_copy(tick[:, :], rsi[:, 0:1]).then_inc(x_done.sem, 1)

            dve.wait_ge(*x_loaded(0, 16))
            dve.wait_ge(*constants(0))
            for stage, (kind, call) in enumerate(STAGES):
                lanes, body = {"l0f": (3, l0_ffn), "l0a": (3, l0_attn), "l1f": (2, l1_ffn), "l1a": (2, l1_attn)}[kind]
                pipeline(dve, lanes, call, stage, body)

        @block.gpsimd
        def _(pool):
            pool.memset(ident[:, :], 0.0).then_inc(zeroed.sem, 1)
            pool.wait_ge(zeroed.sem, 1)
            pool.affine_select(out=ident[:, :], in_=ident[:, :], compare_op=ALU.not_equal, fill=1.0, base=0,
                               pattern=[[-1, P]], channel_multiplier=1).then_inc(constants.sem, 1)
            pool.memset(neghalf[:, :], -0.5).then_inc(constants.sem, 1)
            pool.memset(eps_ln[:, :], EPS_LN).then_inc(constants.sem, 1)
            pool.memset(eps_rms[:, :], EPS_RMS).then_inc(constants.sem, 1)
            for e in range(E):
                pool.memset(pri[:, :, e:e + 1], float(E - e)).then_inc(constants.sem, 1)
            pool.wait_ge(*constants(0))

            def scales(pre, eps2):
                if pre is None:
                    return
                g = pre.gs
                tt = pool.tensor_tensor
                row = lambda n: sc[:, n, :]

                def link(ins, n):
                    ins.then_inc(scale_steps.sem, 1)
                    if n < 8:
                        pool.wait_ge(*scale_steps(g, n))
                pool.wait_ge(*stats_ready(g))
                pool.wait_ge(*normed(g, ago=1))
                link(tt(row(0), mv[:, :, 1], eps_ln[:, :], ALU.add), 1)
                link(tt(row(1), row(0), neghalf[:, :], ALU.pow), 2)
                link(tt(row(2), mv[:, :, 1], row(1), ALU.mult), 3)
                link(tt(row(3), row(2), row(1), ALU.mult), 4)
                link(tt(row(4), row(3), eps2[:, :], ALU.add), 5)
                link(tt(row(5), row(4), neghalf[:, :], ALU.pow), 6)
                link(tt(row(6), row(5), row(1), ALU.mult), 7)
                link(tt(row(7), row(4), row(5), ALU.mult), 8)

            def l0_ffn(pre, main, tail):
                def total(j):
                    if main is None:
                        return
                    g = main.g
                    pool.wait_ge(*weighted(g, LAST[j]))
                    pool.wait_ge(*hidden_used(g, j - 1))
                    pool.tensor_tensor(out=gsum[j % 2][:, :], in0=gab[0][j % 2][:, :], in1=gab[1][j % 2][:, :], op=ALU.add
                                       ).then_inc(summed.sem, 1)
                scales(pre, eps_rms)
                total(0)
                total(1)
                if pre is not None:
                    pool.wait_ge(*maskT_saved(pre.g, 2))
                    pool.wait_ge(*u_masked(pre.g, ago=1))
                    pool.tensor_tensor(out=mdT[:, :], in0=mT[pre.p][1][:, :], in1=mT[pre.p][0][:, :], op=ALU.subtract
                                       ).then_inc(mdiff_ready.sem, 1)
                total(2)
                total(3)
                if pre is not None:
                    pool.wait_ge(*u_masked(pre.g))
                    pool.wait_ge(*maskT_saved(pre.g))
                    for s in range(2):
                        m = mT[pre.p][s]
                        pool.tensor_tensor(out=m[:, :], in0=m[:, :], in1=wT[pre.p][s][:, :], op=ALU.mult
                                           ).then_inc(masks_weighted.sem, 1)

            def l0_attn(pre, gat, mlp):
                if mlp is not None:
                    g = mlp.g
                    pool.wait_ge(*stats2_ready(g))
                    pool.wait_ge(*normed2(g, ago=1))
                    pool.tensor_tensor(sc2[:, 0, :], mv2[:, :, 1], eps_ln[:, :], ALU.add).then_inc(scale2_steps.sem, 1)
                    pool.wait_ge(*scale2_steps(g, 1))
                    pool.tensor_tensor(sc2[:, 1, :], sc2[:, 0, :], neghalf[:, :], ALU.pow).then_inc(scale2_steps.sem, 1)
                scales(pre, eps_ln)

            for stage, (kind, call) in enumerate(STAGES):
                lanes, body = {"l0f": (3, l0_ffn), "l0a": (3, l0_attn),
                               "l1f": (2, lambda pre, main: scales(pre, eps_ln)),
                               "l1a": (2, lambda pre, main: scales(pre, eps_ln))}[kind]
                pipeline(pool, lanes, call, stage, body)


def kernel(**inputs):
    import concourse.bacc as bacc
    from concourse.bass_utils import run_bass_kernel_spmd as run

    i = {n: np.asarray(a) for n, a in inputs.items()}
    f, a, m, t = "L0_ffn_", "L0_attn_", "L1_ffn_", "L1_attn_"
    D = P
    lay = {
        "x": i["L0_attn_x"].reshape(-1, D),
        "w1": i[f + "w1"].T, "w3": i[f + "w3"].T,
        "w2": i[f + "w2"].T.reshape(J, P, D).transpose(1, 0, 2),
        "gate": i[f + "gate_w"].T, "normw": i[f + "norm_w"].reshape(D, 1),
        "a1": i[f + "a1"].reshape(E * R, D).T, "a3": i[f + "a3"].reshape(E * R, D).T,
        "a2": i[f + "a2"].reshape(E * R, J, P).transpose(2, 1, 0),
        "b1": i[f + "b1"].transpose(0, 2, 1).reshape(E * R, J * P),
        "b3": i[f + "b3"].transpose(0, 2, 1).reshape(E * R, J * P),
        "b2": i[f + "b2"].transpose(0, 2, 1).reshape(E * R, D),
        "vecs": np.stack([i[a + n] for n in ("ln1_g", "ln1_b", "ln2_g", "ln2_b", "bv", "bo", "b2")], axis=1),
        "bif": np.stack([i[a + "bi"], i[a + "bf"]], axis=1),
        "wif": np.concatenate([i[a + "Wi"], i[a + "Wf"]], axis=1),
        "wv": i[a + "Wv"], "wo": i[a + "Wo"], "wm1": i[a + "W1"],
        "bm1": i[a + "b1"].reshape(JM, P).T, "wm2": i[a + "W2"].reshape(JM, P, D).transpose(1, 0, 2),
        "wk_l1": i[t + "Wk"], "wq_l1": i[t + "Wq"], "wv_l1": i[t + "Wv"], "waT": i[t + "Wa"].T, "wbT": i[t + "Wb"].T,
        "cen": i[m + "centroids"].T, "lng": i[m + "ln_g"], "lnb": i[m + "ln_b"],
        "e1": i[m + "w1"].transpose(1, 0, 2), "eb1": i[m + "b1"].reshape(E, J, P).transpose(2, 0, 1),
        "e2": i[m + "w2"].reshape(E, J, P, D).transpose(2, 0, 1, 3), "eb2": i[m + "b2"],
    }
    lay = {n: np.ascontiguousarray(w) for n, w in lay.items()}
    nc = bacc.Bacc("TRN2", target_bir_lowering=False, num_devices=1)
    d = {n: nc.dram_tensor(n + "_dram", w.shape, mybir.dt.from_np(w.dtype), kind="ExternalInput").ap() for n, w in lay.items()}
    out = nc.dram_tensor("out", i["L0_attn_x"].shape, F32, kind="ExternalOutput").ap()
    build(nc, d, out)
    r = run(nc, [{n + "_dram": w for n, w in lay.items()}], core_ids=[0])
    return r.results[0]["out"]
```

```python
from contextlib import ExitStack

import numpy as np
import concourse.bass as bass
from concourse import mybir

F32 = mybir.dt.float32
I32 = mybir.dt.int32
ALU = mybir.AluOpType
ACT = mybir.ActivationFunctionType
AX = mybir.AxisListType.X

P = 128
T = 4
S = P * T
NCH = 8
E = 8
R = 16
J = 4
JM = 3
EPS_LN, EPS_RMS, EPS_DEN = 1e-5, 1e-6, 1e-6
LORA = 2.0
REGION = NCH * S + P
NT = NCH * S // P + E
EXTRA = E * REGION
NROWS = EXTRA + E * P
STAGES = [("l0f", 0), ("l0a", 0), ("l0f", 1), ("l1f", 0), ("l1a", 0), ("l1f", 1)]


class Sem:

    def __init__(self, sem, per_chunk=1):
        self.sem, self.k = sem, per_chunk

    def __call__(self, g, n=None, ago=0):
        v = g * self.k + ((self.k if n is None else n) - ago * self.k)
        return self.sem, (max(v, 0) if isinstance(v, int) else v)


class Item:

    def __init__(self, c, p, q, count, unit, call, stage):
        self.c, self.p, self.g, self.h = c, p, c + count * call, q + count // unit * call
        self.gs, self.stage = c + count * stage, stage


def pipeline(eng, count, unit, lanes, call, stage, body):
    def item(s, i=None):
        if i is None:
            return Item(s, s % unit, s // unit, count, unit, call, stage) if 0 <= s < count else None
        return Item(unit * i + s, s % unit, i + s // unit, count, unit, call, stage)
    first = max(lanes, unit)
    rounds = (count - first) // unit
    for s in range(first):
        body(*[item(s - n) for n in range(lanes)])
    with eng.Fori(0, rounds) as i:
        for s in range(first, first + unit):
            body(*[item(s - n, i) for n in range(lanes)])
    for s in range(first + unit * rounds, count + lanes - 1):
        body(*[item(s - n) for n in range(lanes)])


def build(nc, d, out):
    with ExitStack() as ctx:
        def sb(name, shape, dt=F32):
            return ctx.enter_context(nc.sbuf_tensor(name, shape, dt))

        def sem(name, per_chunk=1):
            return Sem(ctx.enter_context(nc.semaphore(name)), per_chunk)

        def tok(ap):
            return ap.rearrange("p (t d) -> p t d", t=T)

        bank = [ctx.enter_context(nc.psum_tensor(f"bank{i}", [P, S], F32)) for i in range(8)]

        x = sb("x", [P, NCH * T, P])
        ident = sb("ident", [P, P])
        neghalf = sb("neghalf", [P, T]); eps_ln = sb("eps_ln", [P, T]); eps_rms = sb("eps_rms", [P, T])
        pri = sb("pri", [P, T, E])
        w1 = sb("w1", [P, J * P]); w3 = sb("w3", [P, J * P]); w2 = sb("w2", [P, J, P])
        gate = sb("gate", [P, E]); normw = sb("normw", [P, 1])
        a1 = sb("a1", [P, P]); a3 = sb("a3", [P, P]); a2 = sb("a2", [P, J, P])
        b1 = sb("b1", [P, J * P]); b3 = sb("b3", [P, J * P]); b2 = sb("b2", [P, P])
        vecs = sb("vecs", [P, 8]); bif = sb("bif", [P, 2]); wif = sb("wif", [P, 2])
        wi_b = sb("wi_b", [P, P]); wf_b = sb("wf_b", [P, P])
        wv = sb("wv", [P, P]); wo = sb("wo", [P, P])
        wm1 = sb("wm1", [P, JM * P]); bm1 = sb("bm1", [P, JM]); wm2 = sb("wm2", [P, JM, P])
        wk_l1 = sb("wk_l1", [P, P]); wq_l1 = sb("wq_l1", [P, P]); wv_l1 = sb("wv_l1", [P, P])
        waT = sb("waT", [P, P]); wbT = sb("wbT", [P, P])
        wak = sb("wak", [P, P]); gmat = sb("gmat", [P, P]); wuT = sb("wuT", [P, P])
        cen = sb("cen", [P, E]); lng = sb("lng", [P, E]); lnb = sb("lnb", [P, E])
        e1 = sb("e1", [P, E, J * P]); e2 = sb("e2", [P, E, J, P])

        stats = sb("stats", [P, T, 6]); mv = sb("mv", [P, T, 2]); part = sb("part", [P, 4, T])
        sc = sb("sc", [P, 8, T])
        yn = [sb(f"yn{i}", [P, T, P]) for i in range(2)]
        ys = [sb(f"ys{i}", [P, T, P]) for i in range(2)]
        tT = [sb(f"tT{i}", [P, S]) for i in range(2)]
        lg = sb("lg", [P, T, E]); lg2 = sb("lg2", [P, T, E]); gt = sb("gt", [P, T, E]); pr = sb("pr", [P, T, E])
        mx = sb("mx", [P, 4, T]); dlt = sb("dlt", [P, T]); th = sb("th", [P, T]); wts = sb("wts", [P, 2, T])
        oh = [sb(f"oh{i}", [P, T, E, R]) for i in range(2)]
        mT = [[sb(f"mT{i}{k}", [P, S]) for k in range(2)] for i in range(2)]
        mdT = sb("mdT", [P, S])
        wT = [[sb(f"wT{i}{k}", [P, S]) for k in range(2)] for i in range(2)]
        ua = [[sb(f"ua{i}{k}", [P, S]) for k in range(2)] for i in range(2)]
        ud = [[sb(f"ud{i}{k}", [P, S]) for k in range(2)] for i in range(2)]
        sil = [sb(f"sil{i}", [P, S]) for i in range(2)]
        act_ = [[sb(f"act{s}{i}", [P, S]) for i in range(2)] for s in range(2)]
        gab = [[sb(f"gab{s}{i}", [P, S]) for i in range(2)] for s in range(2)]
        gsum = [sb(f"gsum{i}", [P, S]) for i in range(2)]
        r1 = sb("r1", [P, S]); r2 = sb("r2", [P, S]); rr = sb("rr", [P, S]); oT = sb("oT", [P, S])
        hT, gi, gf, go = tT, sil[0], sil[1], act_[0][0]
        iv, num, den, rden, oaT = act_[0][1], act_[1][0], act_[1][1], gab[0][0], gab[0][1]
        z, h2, h2T = sb("z", [P, T, P]), sb("h2", [P, T, P]), gab[1][0]
        mpre, mlk, msq, moT = mT[0] + mT[1][:1], wT[0] + wT[1][:1], ua[0] + ua[1][:1], oT
        stats2 = sb("stats2", [P, T, 6]); mv2 = sb("mv2", [P, T, 2]); part2 = sb("part2", [P, 4, T]); sc2 = sb("sc2", [P, 2, T])
        lower = sb("lower", [P, P]); ones = sb("ones", [P, P]); zrow = sb("zrow", [P, P])
        region = sb("region", [P, E]); one8 = sb("one8", [P, E]); tile_i = sb("tile_i", [P, NT], I32)
        tile_no = sb("tile_no", [P, NT])
        xnT = tT
        oh1 = [sb(f"oh1{i}", [P, T, E]) for i in range(2)]
        inv = [sb(f"inv{i}", [P, T]) for i in range(2)]; ala = sb("ala", [P, T]); alt = sb("alt", [P, T])
        alpha = sb("alpha", [P, NCH * T])
        nxt = sb("nxt", [P, E])
        pos = sb("pos", [P, T, E]); slot = sb("slot", [P, T]); slot_i = [sb(f"slot_i{i}", [P, T], I32) for i in range(2)]
        slots = sb("slots", [P, NCH * T]); oh_all = sb("oh_all", [P, NCH * T, E]); shift = sb("shift", [P, E])
        moved = sb("moved", [P, NCH * T, E]); offs = sb("offs", [P, NCH * T]); out_rows = sb("out_rows", [P, NCH * T], I32)
        cnt = sb("cnt", [P, E]); cnt_i = sb("cnt_i", [P, E], I32); nt_i = sb("nt_i", [P, E], I32); ntf = sb("ntf", [P, E])
        ends = sb("ends", [P, E]); jump = sb("jump", [P, E]); past = sb("past", [P, NT, E]); hop = sb("hop", [P, NT, E])
        tab = sb("tab", [P, 2, NT]); tab_e = sb("tab_e", [P, NT], I32); tab_row = sb("tab_row", [P, NT], I32)
        pad_i = sb("pad_i", [P, E], I32)
        eb1b = sb("eb1b", [P, E, J * P]); eb2b = sb("eb2b", [P, E, P])
        xin = [sb(f"xin{i}", [P, P]) for i in range(4)]
        xlT = [sb(f"xlT{i}", [P, P]) for i in range(2)]
        hb, hbT = sil, [act_[0][0], act_[0][1]]
        ob = [sb(f"ob{i}", [P, P]) for i in range(4)]
        gslot = [sb(f"gslot{i}", [P, T], I32) for i in range(2)]
        got = [sb(f"got{i}", [P, T, P]) for i in range(2)]
        rows_in = nc.dram_tensor("rows_in", [NROWS, P], F32, kind="Internal").ap()
        rows_out = nc.dram_tensor("rows_out", [NT * P, P], F32, kind="Internal").ap()
        yT, zT, pr_, pT = tT, mT[0], [act_[0][0], act_[0][1]], [act_[1][0], act_[1][1]]
        vu = [z, h2]
        mxr = sb("mxr", [P, 2]); nmx = sb("nmx", [P, 2]); rs = sb("rs", [P, 2]); rsi = sb("rsi", [P, 2]); tick = sb("tick", [P, 1]); held = sb("held", [P, 3])
        loads = [(t[tuple([slice(None)] * len(d[n].shape))], d[n]) for n, t in (
            ("w1", w1), ("w3", w3), ("w2", w2), ("gate", gate), ("normw", normw), ("a1", a1), ("a3", a3), ("a2", a2),
            ("b1", b1), ("b3", b3), ("b2", b2), ("wif", wif), ("wv", wv), ("wo", wo), ("wm1", wm1),
            ("bm1", bm1), ("wm2", wm2), ("wk_l1", wk_l1), ("wq_l1", wq_l1), ("wv_l1", wv_l1), ("waT", waT), ("wbT", wbT),
            ("cen", cen), ("lng", lng), ("lnb", lnb), ("e1", e1), ("e2", e2))]
        loads += [(vecs[:, 0:7], d["vecs"]), (bif[:, :], d["bif"].to_broadcast([P, 2])),
                  (eb1b[:, :, :].rearrange("p e f -> p (e f)"), d["eb1"].to_broadcast([P, E * J * P])),
                  (eb2b[:, :, :].rearrange("p e d -> p (e d)"), d["eb2"].to_broadcast([P, E * P]))]

        weights_loaded, x_loaded, x_stored = sem("weights_loaded"), sem("x_loaded"), sem("x_stored")
        zeroed, constants = sem("zeroed"), sem("constants", 9 + 2 * E)
        prod_ready, prod_saved, scaled = sem("prod_ready"), sem("prod_saved"), sem("scaled")
        x_done, bn_done, stats_ready = sem("x_done"), sem("bn_done", 3), sem("stats_ready")
        scale_steps, normed, transposed = sem("scale_steps", 8), sem("normed"), sem("transposed")
        h1_ready, h3_ready, silu_done, act_done = (sem(n, 8) for n in ("h1_ready", "h3_ready", "silu_done", "act_done"))
        weighted, summed, hidden_used = sem("weighted", 8), sem("summed", 4), sem("hidden_used", 4)
        r_steps, r_ready, out_ready, outT_saved, back_ready = (
            sem("r_steps", 2), sem("r_ready"), sem("out_ready"), sem("outT_saved"), sem("back_ready"))
        t_ready, logits_ready, logits_read, top2_steps = (
            sem("t_ready"), sem("logits_ready"), sem("logits_read"), sem("top2_steps", 9))
        onehots, delta, tanh_done, slot_w = sem("onehots", 2), sem("delta"), sem("tanh_done"), sem("slot_w", 2)
        maskT_ready, maskT_saved, mdiff_ready = sem("maskT_ready", 4), sem("maskT_saved", 4), sem("mdiff_ready")
        u_ready, u_masked, masks_weighted = sem("u_ready", 2), sem("u_masked", 4), sem("masks_weighted", 2)
        hT_saved, gates_ready, gates_saved = sem("hT_saved"), sem("gates_ready", 4), sem("gates_saved", 3)
        scan_steps, oa_ready, oab_ready = sem("scan_steps", 6), sem("oa_ready"), sem("oab_ready")
        z_ready, bn2_done, stats2_ready, scale2_steps = sem("z_ready"), sem("bn2_done", 3), sem("stats2_ready"), sem("scale2_steps", 2)
        normed2, h2T_ready, h2T_saved = sem("normed2"), sem("h2T_ready"), sem("h2T_saved")
        m_ready, m_saved, m_leaky, m_squared = sem("m_ready", 3), sem("m_saved", 3), sem("m_leaky", 3), sem("m_squared", 3)
        mo_ready, moT_saved, mback_ready, z_added = sem("mo_ready"), sem("moT_saved"), sem("mback_ready"), sem("z_added")
        xnT_saved, aff_ready, aff_saved = sem("xnT_saved"), sem("aff_ready"), sem("aff_saved")
        top1_steps, top1_done, alpha_arg, alpha_tanh, alpha_ready = (
            sem("top1_steps", 4), sem("top1_done"), sem("alpha_arg"), sem("alpha_tanh"), sem("alpha_ready"))
        rank_ready, rank_read, row_steps, rows_ready = (
            sem("rank_ready"), sem("rank_read"), sem("row_steps", 3), sem("rows_ready"))
        scattered = [sem(f"scattered{i}", 16 * T) for i in range(2)]
        gslot_ready, gathered = sem("gslot_ready"), [sem(f"gathered{i}", 16 * T) for i in range(2)]
        arrived = sem("arrived")
        carried_s, carried_g = sem("carried_s"), sem("carried_g")
        routing_reset = sem("routing_reset")
        tab_steps, tabs_ready, extra_zeroed, padded = sem("tab_steps", 12), sem("tabs_ready"), sem("extra_zeroed", 16), sem("padded", 16 * E)
        tile_in = [sem(f"tile_in{i}", 16) for i in range(4)]
        tile_T, xlT_saved, hid_ready, hb_ready, hbT_ready, hbT_saved, o_ready, ob_ready = (
            sem(n) for n in ("tile_T", "xlT_saved", "hid_ready", "hb_ready", "hbT_ready", "hbT_saved", "o_ready", "ob_ready"))
        tile_out = [sem(f"tile_out{i}", 16) for i in range(4)]
        yT_ready, yT_saved, zT_ready, zT_saved, v_ready, v_saved = (
            sem("yT_ready"), sem("yT_saved"), sem("zT_ready"), sem("zT_saved"), sem("v_ready"), sem("v_saved"))
        sc_ready, max_done, nmax_done, exp_done, pT_ready, pT_saved = (
            sem(n, 4) for n in ("sc_ready", "max_done", "nmax_done", "exp_done", "pT_ready", "pT_saved"))
        rsum_done, ao_ready, ao_done = sem("rsum_done", 4), sem("ao_ready", 4), sem("ao_done", 4)

        block = ctx.enter_context(nc.Block())

        STEPS = [(0, 0), (1, 0), (0, 1), (1, 1), (2, 0), (3, 0), (2, 1), (3, 1)]
        LAST = [STEPS.index((j, 1)) + 1 for j in range(J)]
        BH1, BH3, BV, BOUT, BMISC = (0, 1), (2, 3), (4, 5), 6, 7

        zeros8 = zrow[:, :].unsqueeze(1).to_broadcast([P, E, P])
        CALLS = sum(kind == "l1f" for kind, _ in STAGES)
        AFTER = {n + 1 for n, (kind, _) in enumerate(STAGES) if kind == "l1f"}

        def expert_of(eng, tile):
            return eng.value_load(tab_e[0:1, bass.ds(tile.c, 1)], min_val=0, max_val=E - 1)

        def before_stage(eng, stage):
            if stage in AFTER:
                eng.wait_ge(*ob_ready(NT * (STAGES[stage - 1][1] + 1), ago=1))
            else:
                eng.wait_ge(*x_done(NCH * stage, ago=1))

        def xc(ch):
            return x[:, bass.ds(ch.c * T, T), :]

        def fl(ap):
            return ap.rearrange("p t d -> p (t d)")

        @block.sync
        def _(sp):
            sp.dma_start(x[:, :, :], d["x"].rearrange("(n p) d -> p n d", p=P)).then_inc(x_loaded.sem, 16)
            for dst, src in loads:
                sp.dma_start(dst, src).then_inc(weights_loaded.sem, 16)
            sp.wait_ge(*constants(0))
            sp.dma_start(rows_in[EXTRA:, :].rearrange("(n p) d -> p n d", p=P), zeros8).then_inc(extra_zeroed.sem, 16)
            for call in range(CALLS):
                sp.wait_ge(*tabs_ready(call))
                for e in range(E):
                    r = sp.value_load(pad_i[0:1, e:e + 1], min_val=0, max_val=EXTRA - P)
                    sp.dma_start(rows_in[bass.ds(r, P), :], zrow[:, :]).then_inc(padded.sem, 16)
                sp.wait_ge(*padded(call))
                for i in range(2):
                    sp.wait_ge(*scattered[i](NCH // 2 * (call + 1), ago=1))
                if call == 0:
                    sp.wait_ge(*extra_zeroed(0))

                def load(t, b):
                    r = sp.value_load(tab_row[0:1, bass.ds(t, 1)], min_val=0, max_val=NROWS - P)
                    sp.dma_start(xin[b][:, :], rows_in[bass.ds(r, P), :]).then_inc(tile_in[b].sem, 16)

                def store(t, b):
                    sp.wait_ge(*ob_ready(t + NT * call))
                    sp.dma_start(rows_out[bass.ds(t * P, P), :], ob[b][:, :]).then_inc(tile_out[b].sem, 16)

                for b in range(4):
                    load(b, b)
                with sp.Fori(0, NT // 4 - 1) as i:
                    for b in range(4):
                        store(4 * i + b, b)
                        load(4 * i + (b + 4), b)
                for b in range(4):
                    store(NT - 4 + b, b)
            o = out.rearrange("a s d -> (a s) d").rearrange("(n p) d -> p n d", p=P)
            with sp.Fori(0, NCH) as c:
                sp.wait_ge(*(arrived(c + NCH * (CALLS - 1)) if STAGES[-1][0] == "l1f" else x_done(c + NCH * (len(STAGES) - 1))))
                sp.dma_start(o[:, bass.ds(c * T, T), :], x[:, bass.ds(c * T, T), :]).then_inc(x_stored.sem, 16)
            sp.wait_ge(x_stored.sem, 16 * NCH)

        @block.tensor
        def _(pe):
            mm, tr = nc.tensor.matmul, nc.tensor.transpose

            def transpose4(dst, src):
                for t in range(T):
                    last = tr(bank[dst][:, t * P:(t + 1) * P], src(t), ident[:, :])
                return last

            pe.wait_ge(weights_loaded.sem, 16 * len(loads))
            pe.wait_ge(*constants(0))
            mm(bank[0][:, 0:P], waT[:, :], wk_l1[:, :], start=True, stop=True).then_inc(prod_ready.sem, 1)
            mm(bank[1][:, 0:P], wv_l1[:, :], wbT[:, :], start=True, stop=True).then_inc(prod_ready.sem, 1)
            pe.wait_ge(prod_saved.sem, 1)
            mm(bank[2][:, 0:P], wq_l1[:, :], wak[:, :], start=True, stop=True).then_inc(prod_ready.sem, 1)
            pe.wait_ge(prod_saved.sem, 3)
            pe.wait_ge(scaled.sem, 5)

            def l0_ffn(pre, main, tail):
                def hidden(k):
                    if main is None:
                        return
                    (j, s), g, p = STEPS[k - 1], main.g, main.p
                    f = slice(j * P, (j + 1) * P)
                    if k == 1:
                        pe.wait_ge(*u_masked(g))
                    for i, (h, base, lora, ready, read) in enumerate(((BH1, w1, b1, h1_ready, silu_done),
                                                                      (BH3, w3, b3, h3_ready, act_done))):
                        b = bank[h[j % 2]]
                        pe.wait_ge(*read(g, k - 2))
                        if s == 0:
                            mm(b[:, :], base[:, f], tT[p][:, :], start=True, stop=False)
                            mm(b[:, :], lora[:, f], ua[p][i][:, :], start=False, stop=True).then_inc(ready.sem, 1)
                        else:
                            mm(b[:, :], lora[:, f], ud[p][i][:, :], start=False, stop=True,
                               skip_group_check=True).then_inc(ready.sem, 1)

                def down(j):
                    if main is None:
                        return
                    g = main.g
                    if j == 0:
                        pe.wait_ge(*r_ready(g, ago=1))
                        pe.wait_ge(*x_done(main.gs, ago=1))
                    pe.wait_ge(*act_done(g, LAST[j]))
                    for s in range(2):
                        mm(bank[BV[s]][:, :], a2[:, j, :], act_[s][j % 2][:, :], start=j == 0, stop=j == J - 1)
                    pe.wait_ge(*summed(g, j + 1))
                    mm(bank[BOUT][:, :], w2[:, j, :], gsum[j % 2][:, :], start=j == 0, stop=False
                       ).then_inc(hidden_used.sem, 1)

                def mask(n, src):
                    if pre is None:
                        return
                    if n:
                        pe.wait_ge(*maskT_saved(pre.g, n))
                    transpose4(BMISC, src).then_inc(maskT_ready.sem, 1)

                def up(i):
                    if pre is None:
                        return
                    if i == 0:
                        pe.wait_ge(*maskT_saved(pre.g))
                    else:
                        pe.wait_ge(*u_masked(pre.g, 2))
                    mm(bank[BMISC][:, :], (a1, a3)[i][:, :], tT[pre.p][:, :], start=True, stop=True).then_inc(u_ready.sem, 1)

                hidden(1)
                if tail is not None:
                    pe.wait_ge(*r_ready(tail.g))
                    mm(bank[BOUT][:, :], b2[:, :], rr[:, :], start=False, stop=True).then_inc(out_ready.sem, 1)
                if pre is not None:
                    pe.wait_ge(*normed(pre.gs))
                    pe.wait_ge(*u_masked(pre.g, ago=1))
                    transpose4(BMISC, lambda t: yn[pre.p][:, t, :]).then_inc(transposed.sem, 1)
                hidden(2)
                if tail is not None:
                    pe.wait_ge(*outT_saved(tail.g))
                    transpose4(BOUT, lambda t: oT[:, t * P:(t + 1) * P]).then_inc(back_ready.sem, 1)
                hidden(3)
                if pre is not None:
                    pe.wait_ge(*t_ready(pre.g))
                    for t in range(T):
                        last = mm(bank[BMISC][:, t * E:(t + 1) * E], tT[pre.p][:, t * P:(t + 1) * P], gate[:, :],
                                  start=True, stop=True)
                    last.then_inc(logits_ready.sem, 1)
                hidden(4)
                hidden(5)
                down(0)
                if pre is not None:
                    pe.wait_ge(*onehots(pre.g))
                mask(0, lambda t: oh[0][:, t, :, :].rearrange("p e r -> p (e r)"))
                hidden(6)
                mask(1, lambda t: oh[1][:, t, :, :].rearrange("p e r -> p (e r)"))
                down(1)
                if pre is not None:
                    pe.wait_ge(*slot_w(pre.g))
                mask(2, lambda t: wts[:, 0, t:t + 1].to_broadcast([P, P]))
                hidden(7)
                mask(3, lambda t: wts[:, 1, t:t + 1].to_broadcast([P, P]))
                hidden(8)
                up(0)
                down(2)
                up(1)
                down(3)

            def l0_attn(pre, gat, mlp):
                if mlp is not None:
                    pe.wait_ge(*oa_ready(mlp.g))
                    pe.wait_ge(*x_done(mlp.gs, ago=1))
                    transpose4(4, lambda t: oaT[:, t * P:(t + 1) * P]).then_inc(oab_ready.sem, 1)
                if pre is not None:
                    pe.wait_ge(*normed(pre.gs))
                    pe.wait_ge(*hT_saved(pre.g, ago=1))
                    transpose4(7, lambda t: yn[pre.p][:, t, :]).then_inc(transposed.sem, 1)
                if gat is not None:
                    pe.wait_ge(*hT_saved(gat.g))
                    pe.wait_ge(*gates_saved(gat.g, ago=1))
                    pe.wait_ge(*scan_steps(gat.g, 1, ago=1))
                    for b, w in ((1, wi_b), (2, wf_b), (3, wo), (0, wv)):
                        mm(bank[b][:, :], w[:, :], hT[gat.p][:, :], start=True, stop=True).then_inc(gates_ready.sem, 1)
                if mlp is not None:
                    g = mlp.g
                    pe.wait_ge(*normed2(g))
                    transpose4(4, lambda t: h2[:, t, :]).then_inc(h2T_ready.sem, 1)
                    pe.wait_ge(*h2T_saved(g))
                    for j in range(JM):
                        if j == 2:
                            pe.wait_ge(*m_saved(g, 1))
                        elif j == 0:
                            pe.wait_ge(*m_saved(g, 3, ago=1))
                        mm(bank[5 + j % 2][:, :], wm1[:, j * P:(j + 1) * P], h2T[:, :], start=True, stop=True
                           ).then_inc(m_ready.sem, 1)
                    for j in range(JM):
                        pe.wait_ge(*m_squared(g, j + 1))
                        last = mm(bank[4][:, :], wm2[:, j, :], msq[j][:, :], start=j == 0, stop=j == JM - 1)
                    last.then_inc(mo_ready.sem, 1)
                    pe.wait_ge(*moT_saved(g))
                    transpose4(4, lambda t: moT[:, t * P:(t + 1) * P]).then_inc(mback_ready.sem, 1)

            def route(pre, srt):
                if srt is not None:
                    g, p = srt.g, srt.p
                    pe.wait_ge(*xnT_saved(g))
                    pe.wait_ge(*aff_saved(g, ago=1))
                    for t in range(T):
                        last = mm(bank[7][:, t * E:(t + 1) * E], xnT[p][:, t * P:(t + 1) * P], cen[:, :],
                                  start=True, stop=True)
                    last.then_inc(aff_ready.sem, 1)
                if pre is not None:
                    pe.wait_ge(*normed(pre.gs))
                    pe.wait_ge(*xnT_saved(pre.g, ago=1))
                    transpose4(6, lambda t: yn[pre.p][:, t, :]).then_inc(transposed.sem, 1)
                if srt is not None:
                    pe.wait_ge(*top1_done(g))
                    pe.wait_ge(*rank_read(g, ago=1))
                    for t in range(T + 1):
                        for u in range(min(t + 1, T)):
                            last = mm(bank[5][:, t * E:(t + 1) * E], (lower if u == t else ones)[:, :], oh1[p][:, u, :],
                                      start=u == 0, stop=u == min(t, T - 1))
                    last.then_inc(rank_ready.sem, 1)

            def expert(n0, n1, n2):
                if n2 is not None:
                    p = n2.p % 2
                    pe.wait_ge(*hb_ready(n2.g))
                    pe.wait_ge(*hbT_saved(n2.g, ago=2))
                    for j in range(J):
                        last = tr(bank[2 + p][:, j * P:(j + 1) * P], hb[p][:, j * P:(j + 1) * P], ident[:, :])
                    last.then_inc(hbT_ready.sem, 1)
                if n1 is not None:
                    p, e = n1.p % 2, expert_of(pe, n1)
                    pe.wait_ge(*xlT_saved(n1.g))
                    pe.wait_ge(*hb_ready(n1.g, ago=2))
                    mm(bank[p][:, :], xlT[p][:, :], e1[:, bass.ds(e, 1), :].rearrange("p a f -> p (a f)"),
                       start=True, stop=True).then_inc(hid_ready.sem, 1)
                if n0 is not None:
                    pe.wait_ge(*tile_in[n0.p](n0.h))
                    pe.wait_ge(*xlT_saved(n0.g, ago=2))
                    tr(bank[4 + n0.p % 2][:, 0:P], xin[n0.p][:, :], ident[:, :]).then_inc(tile_T.sem, 1)
                if n2 is not None:
                    p, e = n2.p % 2, expert_of(pe, n2)
                    pe.wait_ge(*hbT_saved(n2.g))
                    pe.wait_ge(*ob_ready(n2.g, ago=2))
                    for j in range(J):
                        last = mm(bank[6 + p][:, 0:P], hbT[p][:, j * P:(j + 1) * P],
                                  e2[:, bass.ds(e, 1), j, :].rearrange("p a d -> p (a d)"), start=j == 0, stop=j == J - 1)
                    last.then_inc(o_ready.sem, 1)

            def l1_attn(_, pre, main):
                if pre is not None:
                    pe.wait_ge(*normed(pre.gs))
                    pe.wait_ge(*v_saved(pre.g, ago=1))
                    transpose4(7, lambda t: yn[pre.p][:, t, :]).then_inc(transposed.sem, 1)
                if main is not None:
                    g, p = main.g, main.p
                    for i in range(T + 1):
                        if i < T:
                            pe.wait_ge(*exp_done(g, i - 1))
                            mm(bank[i % 2][:, :], zT[p][:, i * P:(i + 1) * P], yT[p][:, :], start=True, stop=True
                               ).then_inc(sc_ready.sem, 1)
                        if i == 0:
                            continue
                        i1 = i - 1
                        pe.wait_ge(*exp_done(g, i1 + 1))
                        pe.wait_ge(*pT_saved(g, i1 - 1))
                        transpose4(2 + i1 % 2, lambda t: pr_[i1 % 2][:, t * P:(t + 1) * P]).then_inc(pT_ready.sem, 1)
                        pe.wait_ge(*pT_saved(g, i1 + 1))
                        pe.wait_ge(*ao_done(g, i1 - 1))
                        for t in range(T):
                            last = mm(bank[4 + i1 % 2][:, 0:P], pT[i1 % 2][:, t * P:(t + 1) * P], vu[p][:, t, :],
                                      start=t == 0, stop=t == T - 1)
                        last.then_inc(ao_ready.sem, 1)
                if pre is not None:
                    pe.wait_ge(*yT_saved(pre.g))
                    mm(bank[7][:, :], gmat[:, :], yT[pre.p][:, :], start=True, stop=True).then_inc(zT_ready.sem, 1)
                    pe.wait_ge(*zT_saved(pre.g))
                    for t in range(T):
                        last = mm(bank[7][:, t * P:(t + 1) * P], yT[pre.p][:, t * P:(t + 1) * P], wuT[:, :],
                                  start=True, stop=True)
                    last.then_inc(v_ready.sem, 1)

            for stage, (kind, call) in enumerate(STAGES):
                before_stage(pe, stage)
                lanes, body = {"l0f": (3, l0_ffn), "l0a": (3, l0_attn), "l1f": (2, route), "l1a": (3, l1_attn)}[kind]
                pipeline(pe, NCH, 2, lanes, call, stage, body)
                if kind == "l1f":
                    pe.wait_ge(*tabs_ready(call))
                    pipeline(pe, NT, 4, 3, call, stage, expert)

        @block.scalar
        def _(act):
            af = nc.scalar.activation

            act.wait_ge(weights_loaded.sem, 16 * len(loads))
            for w in (b1, b3, b2):
                af(w[:, :], w[:, :], ACT.Copy, scale=LORA).then_inc(scaled.sem, 1)
            for n, w in enumerate((wi_b, wf_b)):
                af(w[:, :], wif[:, n:n + 1].to_broadcast([P, P]), ACT.Copy).then_inc(scaled.sem, 1)
            act.wait_ge(prod_ready.sem, 2)
            af(wak[:, :], bank[0][:, 0:P], ACT.Copy).then_inc(prod_saved.sem, 1)
            af(wuT[:, :], bank[1][:, 0:P], ACT.Copy).then_inc(prod_saved.sem, 1)
            act.wait_ge(prod_ready.sem, 3)
            af(gmat[:, :], bank[2][:, 0:P], ACT.Copy).then_inc(prod_saved.sem, 1)

            def l0_ffn(pre, main, tail):
                def silu(k):
                    if main is None:
                        return
                    g = main.g
                    act.wait_ge(*h1_ready(g, k))
                    act.wait_ge(*act_done(g, k - 2))
                    af(sil[(k - 1) % 2][:, :], bank[BH1[STEPS[k - 1][0] % 2]][:, :], ACT.Silu).then_inc(silu_done.sem, 1)

                def mask(n, dst):
                    if pre is None:
                        return
                    act.wait_ge(*maskT_ready(pre.g, n + 1))
                    if n == 0:
                        act.wait_ge(*mdiff_ready(pre.g, ago=1))
                    act.wait_ge(*r_ready(pre.g, ago=2))
                    af(dst[:, :], bank[BMISC][:, :], ACT.Copy).then_inc(maskT_saved.sem, 1)

                silu(1)
                if tail is not None:
                    act.wait_ge(*out_ready(tail.g))
                    act.wait_ge(*back_ready(tail.g, ago=1))
                    af(oT[:, :], bank[BOUT][:, :], ACT.Copy).then_inc(outT_saved.sem, 1)
                if pre is not None:
                    act.wait_ge(*transposed(pre.gs))
                    act.wait_ge(*hidden_used(pre.g, ago=2))
                    af(tT[pre.p][:, :], bank[BMISC][:, :], ACT.Copy, scale=normw[:, 0:1]).then_inc(t_ready.sem, 1)
                silu(2)
                silu(3)
                silu(4)
                if pre is not None:
                    act.wait_ge(*delta(pre.g))
                    act.wait_ge(*maskT_ready(pre.g, ago=1))
                    af(th[:, :], dlt[:, :], ACT.Tanh, scale=0.5).then_inc(tanh_done.sem, 1)
                    act.wait_ge(*tanh_done(pre.g))
                    af(wts[:, 0, :], th[:, :], ACT.Copy, scale=-0.5, bias=0.5).then_inc(slot_w.sem, 1)
                    af(wts[:, 1, :], th[:, :], ACT.Copy, scale=0.5, bias=0.5).then_inc(slot_w.sem, 1)
                silu(5)
                mask(0, mT[pre.p][0] if pre is not None else None)
                silu(6)
                mask(1, mT[pre.p][1] if pre is not None else None)
                silu(7)
                mask(2, wT[pre.p][0] if pre is not None else None)
                silu(8)
                mask(3, wT[pre.p][1] if pre is not None else None)

            def l0_attn(pre, gat, mlp):
                if pre is not None:
                    act.wait_ge(*transposed(pre.gs))
                    act.wait_ge(*gates_ready(pre.g, ago=2))
                    af(hT[pre.p][:, :], bank[7][:, :], ACT.Identity, bias=vecs[:, 1:2], scale=vecs[:, 0:1]
                       ).then_inc(hT_saved.sem, 1)
                if gat is not None:
                    g = gat.g
                    act.wait_ge(*oa_ready(g, ago=1))
                    for n, (b, dst, bias) in enumerate(((1, gi, bif[:, 0:1]), (2, gf, bif[:, 1:2]), (3, go, vecs[:, 5:6]))):
                        act.wait_ge(*gates_ready(g, n + 1))
                        af(dst[:, :], bank[b][:, :], ACT.Sigmoid, bias=bias).then_inc(gates_saved.sem, 1)
                if mlp is not None:
                    g = mlp.g
                    act.wait_ge(*h2T_ready(g))
                    af(h2T[:, :], bank[4][:, :], ACT.Identity, bias=vecs[:, 3:4], scale=vecs[:, 2:3]).then_inc(h2T_saved.sem, 1)
                    act.wait_ge(*m_leaky(g, ago=1))
                    for j in range(JM):
                        act.wait_ge(*m_ready(g, j + 1))
                        af(mpre[j][:, :], bank[5 + j % 2][:, :], ACT.Identity, bias=bm1[:, j:j + 1]).then_inc(m_saved.sem, 1)
                    for j in range(JM):
                        act.wait_ge(*m_leaky(g, j + 1))
                        af(msq[j][:, :], mlk[j][:, :], ACT.Square).then_inc(m_squared.sem, 1)
                    act.wait_ge(*mo_ready(g))
                    af(moT[:, :], bank[4][:, :], ACT.Identity, bias=vecs[:, 6:7]).then_inc(moT_saved.sem, 1)

            def route(pre, srt):
                if pre is not None:
                    act.wait_ge(*transposed(pre.gs))
                    act.wait_ge(*aff_ready(pre.g, ago=2))
                    af(xnT[pre.p][:, :], bank[6][:, :], ACT.Copy).then_inc(xnT_saved.sem, 1)
                if srt is not None:
                    act.wait_ge(*alpha_arg(srt.g))
                    act.wait_ge(*alpha_ready(srt.g, ago=1))
                    af(alt[:, :], ala[:, :], ACT.Tanh, scale=0.5).then_inc(alpha_tanh.sem, 1)

            def expert(n0, n1, n2):
                if n2 is not None:
                    p = n2.p % 2
                    act.wait_ge(*hbT_ready(n2.g))
                    act.wait_ge(*o_ready(n2.g, ago=2))
                    af(hbT[p][:, :], bank[2 + p][:, :], ACT.Relu).then_inc(hbT_saved.sem, 1)
                if n0 is not None:
                    p, e = n0.p % 2, expert_of(act, n0)
                    act.wait_ge(*tile_T(n0.g))
                    act.wait_ge(*hid_ready(n0.g, ago=2))
                    af(xlT[p][:, :], bank[4 + p][:, 0:P], ACT.Identity, bias=lnb[:, bass.ds(e, 1)], scale=lng[:, bass.ds(e, 1)]
                       ).then_inc(xlT_saved.sem, 1)

            def l1_attn(_, pre, main):
                if pre is not None:
                    act.wait_ge(*transposed(pre.gs))
                    act.wait_ge(*ao_ready(pre.g, ago=2))
                    af(yT[pre.p][:, :], bank[7][:, :], ACT.Copy).then_inc(yT_saved.sem, 1)
                if main is not None:
                    g = main.g
                    for i in range(T + 1):
                        if i < T:
                            act.wait_ge(*nmax_done(g, i + 1))
                            act.wait_ge(*pT_ready(g, i - 1))
                            act.wait_ge(*rsum_done(g, i - 1))
                            af(pr_[i % 2][:, :], bank[i % 2][:, :], ACT.Exp, bias=nmx[:, i % 2:i % 2 + 1],
                               accum_out=rs[:, i % 2:i % 2 + 1]).then_inc(exp_done.sem, 1)
                        if i:
                            act.wait_ge(*pT_ready(g, i))
                            act.wait_ge(*ao_ready(g, i - 2))
                            af(pT[(i - 1) % 2][:, :], bank[2 + (i - 1) % 2][:, :], ACT.Copy).then_inc(pT_saved.sem, 1)
                if pre is not None:
                    act.wait_ge(*zT_ready(pre.g))
                    af(zT[pre.p][:, :], bank[7][:, :], ACT.Copy).then_inc(zT_saved.sem, 1)
                    act.wait_ge(*v_ready(pre.g))
                    af(fl(vu[pre.p]), bank[7][:, :], ACT.Copy).then_inc(v_saved.sem, 1)

            for stage, (kind, call) in enumerate(STAGES):
                before_stage(act, stage)
                lanes, body = {"l0f": (3, l0_ffn), "l0a": (3, l0_attn), "l1f": (2, route), "l1a": (3, l1_attn)}[kind]
                pipeline(act, NCH, 2, lanes, call, stage, body)
                if kind == "l1f":
                    act.wait_ge(*tabs_ready(call))
                    pipeline(act, NT, 4, 3, call, stage, expert)

        @block.vector
        def _(dve):
            v = nc.vector
            bc = lambda ap: ap.unsqueeze(2).to_broadcast([P, T, E])

            def aggregate(g, halves, tmp, meanvar, done, ready):
                even, odd = (lambda n: halves[:, :, n]), (lambda n: halves[:, :, 3 + n])
                dve.wait_ge(*done(g, 1))
                v.tensor_tensor(tmp[:, 0, :], even(1), odd(1), ALU.add)
                v.tensor_tensor(tmp[:, 1, :], even(1), odd(1), ALU.subtract)
                v.tensor_tensor(tmp[:, 2, :], even(2), odd(2), ALU.add).then_inc(done.sem, 1)
                dve.wait_ge(*done(g, 2))
                v.tensor_scalar(meanvar[:, :, 0], tmp[:, 0, :], 0.5, None, ALU.mult)
                v.scalar_tensor_tensor(tmp[:, 3, :], tmp[:, 1, :], 0.25, tmp[:, 1, :], ALU.mult, ALU.mult).then_inc(done.sem, 1)
                dve.wait_ge(*done(g, 3))
                v.scalar_tensor_tensor(meanvar[:, :, 1], tmp[:, 2, :], 1.0 / P, tmp[:, 3, :], ALU.mult, ALU.add
                                       ).then_inc(ready.sem, 1)

            def statistics(pre):
                if pre is None:
                    return
                if pre.stage:
                    dve.wait_ge(*x_done(pre.gs, ago=NCH))
                dve.wait_ge(*scale_steps(pre.gs, ago=1))
                v.memset(held[:, 0:1], 0.0)
                for t in range(T):
                    last = v.bn_stats(stats[:, t, :], xc(pre)[:, t, :])
                last.then_inc(bn_done.sem, 1)
                aggregate(pre.gs, stats, part, mv, bn_done, stats_ready)

            def normalise(pre, row, residual, inverse=False):
                if pre is None:
                    return
                dve.wait_ge(*scale_steps(pre.gs))
                dve.wait_ge(*transposed(pre.gs, ago=2))
                if inverse:
                    dve.wait_ge(*scattered[pre.p](pre.h, ago=1))
                    v.tensor_copy(inv[pre.p][:, :], sc[:, 7, :])
                for on, dst, r in ((residual, ys, 1), (True, yn, row)):
                    for t in range(T * on):
                        last = v.tensor_scalar(dst[pre.p][:, t, :], xc(pre)[:, t, :], mv[:, t, 0:1], sc[:, r, t:t + 1],
                                               ALU.subtract, ALU.mult)
                last.then_inc(normed.sem, 1)

            def l0_ffn(pre, main, tail):
                def hidden(k):
                    if main is None:
                        return
                    (j, s), g, p = STEPS[k - 1], main.g, main.p
                    dve.wait_ge(*silu_done(g, k))
                    dve.wait_ge(*h3_ready(g, k))
                    dve.wait_ge(*hidden_used(g, j - 1))
                    a = act_[s][j % 2]
                    v.tensor_tensor(a[:, :], bank[BH3[j % 2]][:, :], sil[(k - 1) % 2][:, :], ALU.mult).then_inc(act_done.sem, 1)
                    dve.wait_ge(*act_done(g, k))
                    dve.wait_ge(*summed(g, j - 1))
                    if k == 1:
                        dve.wait_ge(*maskT_saved(g))
                    v.tensor_tensor(gab[s][j % 2][:, :], a[:, :], wT[p][s][:, :], ALU.mult).then_inc(weighted.sem, 1)

                def top2():
                    g = pre.g

                    def link(ins, n):
                        ins.then_inc(top2_steps.sem, 1)
                        dve.wait_ge(*top2_steps(g, n))

                    dve.wait_ge(*logits_ready(g))
                    dve.wait_ge(*maskT_ready(g, ago=1))
                    v.tensor_copy(lg[:, :, :].rearrange("p t e -> p (t e)"), bank[BMISC][:, 0:T * E]).then_inc(logits_read.sem, 1)
                    dve.wait_ge(*logits_read(g))
                    n = 0
                    for s, l in enumerate((lg, lg2)):
                        link(v.tensor_reduce(mx[:, 2 * s, :], l[:, :, :], AX, ALU.max), n + 1)
                        link(v.tensor_tensor(gt[:, :, :], l[:, :, :], bc(mx[:, 2 * s, :]), ALU.is_ge), n + 2)
                        link(v.tensor_tensor(pr[:, :, :], gt[:, :, :], pri[:, :, :], ALU.mult), n + 3)
                        link(v.tensor_reduce(mx[:, 2 * s + 1, :], pr[:, :, :], AX, ALU.max), n + 4)
                        for t in range(T):
                            last = v.tensor_tensor(oh[s][:, t, :, :], pr[:, t, :].unsqueeze(2).to_broadcast([P, E, R]),
                                                   mx[:, 2 * s + 1, t:t + 1].unsqueeze(2).to_broadcast([P, E, R]), ALU.is_equal)
                        last.then_inc(onehots.sem, 1)
                        if s == 0:
                            dve.wait_ge(*onehots(g, 1))
                            link(v.scalar_tensor_tensor(lg2[:, :, :], oh[0][:, :, :, 0], -3e38, lg[:, :, :],
                                                        ALU.mult, ALU.add), 5)
                            n = 5
                    dve.wait_ge(*tanh_done(g, ago=1))
                    v.tensor_tensor(dlt[:, :], mx[:, 2, :], mx[:, 0, :], ALU.subtract).then_inc(delta.sem, 1)

                def masked(i):
                    if pre is None:
                        return
                    g, p = pre.g, pre.p
                    dve.wait_ge(*u_ready(g, i + 1))
                    dve.wait_ge(*mdiff_ready(g))
                    dve.wait_ge(*h3_ready(g, ago=2))
                    v.tensor_tensor(ua[p][i][:, :], bank[BMISC][:, :], mT[p][0][:, :], ALU.mult).then_inc(u_masked.sem, 1)
                    v.tensor_tensor(ud[p][i][:, :], bank[BMISC][:, :], mdT[:, :], ALU.mult).then_inc(u_masked.sem, 1)

                statistics(pre)
                hidden(1)
                normalise(pre, 6, False)
                hidden(2)
                if tail is not None:
                    dve.wait_ge(*back_ready(tail.g))
                    v.scalar_tensor_tensor(xc(tail), tok(bank[BOUT][:, :]), 0.5, xc(tail), ALU.mult, ALU.add
                                           ).then_inc(x_done.sem, 1)
                hidden(3)
                if pre is not None:
                    top2()
                for k in range(4, 9):
                    hidden(k)
                masked(0)
                masked(1)
                if main is not None:
                    g, p = main.g, main.p
                    dve.wait_ge(*hidden_used(g))
                    dve.wait_ge(*masks_weighted(g))
                    dve.wait_ge(*out_ready(g, ago=1))
                    v.tensor_tensor(r1[:, :], bank[BV[0]][:, :], mT[p][0][:, :], ALU.mult)
                    v.tensor_tensor(r2[:, :], bank[BV[1]][:, :], mT[p][1][:, :], ALU.mult).then_inc(r_steps.sem, 2)
                    dve.wait_ge(*r_steps(g))
                    v.tensor_tensor(rr[:, :], r1[:, :], r2[:, :], ALU.add).then_inc(r_ready.sem, 1)

            def l0_attn(pre, gat, mlp):
                if mlp is not None:
                    g = mlp.g
                    dve.wait_ge(*oab_ready(g))
                    v.tensor_tensor(z[:, :, :], tok(bank[4][:, :]), ys[mlp.p][:, :, :], ALU.add).then_inc(z_ready.sem, 1)
                    dve.wait_ge(*z_ready(g))
                    for t in range(T):
                        last = v.bn_stats(stats2[:, t, :], z[:, t, :])
                    last.then_inc(bn2_done.sem, 1)
                    aggregate(g, stats2, part2, mv2, bn2_done, stats2_ready)
                    v.tensor_tensor(xc(mlp), xc(mlp), z[:, :, :], ALU.add).then_inc(z_added.sem, 1)
                statistics(pre)
                if mlp is not None:
                    g = mlp.g
                    dve.wait_ge(*scale2_steps(g))
                    dve.wait_ge(*h2T_ready(g, ago=1))
                    for t in range(T):
                        last = v.tensor_scalar(h2[:, t, :], z[:, t, :], mv2[:, t, 0:1], sc2[:, 1, t:t + 1],
                                               ALU.subtract, ALU.mult)
                    last.then_inc(normed2.sem, 1)
                normalise(pre, 6, True)
                if gat is not None:
                    g = gat.g
                    dve.wait_ge(*gates_saved(g))
                    dve.wait_ge(*gates_ready(g))
                    v.scalar_tensor_tensor(iv[:, :], bank[0][:, :], vecs[:, 4:5], gi[:, :], ALU.add, ALU.mult
                                           ).then_inc(scan_steps.sem, 1)
                    v.tensor_tensor_scan(den[:, :], gf[:, :], gi[:, :], 0.0, ALU.mult, ALU.add).then_inc(scan_steps.sem, 1)
                    dve.wait_ge(*scan_steps(g, 1))
                    v.tensor_tensor_scan(num[:, :], gf[:, :], iv[:, :], 0.0, ALU.mult, ALU.add).then_inc(scan_steps.sem, 1)
                    dve.wait_ge(*scan_steps(g, 2))
                    v.tensor_scalar(den[:, :], den[:, :], EPS_DEN, None, ALU.add).then_inc(scan_steps.sem, 1)
                    dve.wait_ge(*scan_steps(g, 4))
                    v.reciprocal(rden[:, :], den[:, :]).then_inc(scan_steps.sem, 1)
                    v.tensor_tensor(num[:, :], num[:, :], go[:, :], ALU.mult).then_inc(scan_steps.sem, 1)
                    dve.wait_ge(*scan_steps(g, 6))
                    dve.wait_ge(*oab_ready(g, ago=1))
                    v.tensor_tensor(oaT[:, :], num[:, :], rden[:, :], ALU.mult).then_inc(oa_ready.sem, 1)
                if mlp is not None:
                    g = mlp.g
                    for j in range(JM):
                        dve.wait_ge(*m_saved(g, j + 1))
                        dve.wait_ge(*m_squared(g, ago=1))
                        v.scalar_tensor_tensor(mlk[j][:, :], mpre[j][:, :], 0.01, mpre[j][:, :], ALU.mult, ALU.max
                                               ).then_inc(m_leaky.sem, 1)
                    dve.wait_ge(*mback_ready(g))
                    dve.wait_ge(*z_added(g))
                    v.tensor_tensor(xc(mlp), tok(bank[4][:, :]), xc(mlp), ALU.add).then_inc(x_done.sem, 1)

            def route(pre, srt):
                statistics(pre)
                if srt is not None:
                    g, p = srt.g, srt.p

                    def link(ins, n):
                        ins.then_inc(top1_steps.sem, 1)
                        dve.wait_ge(*top1_steps(g, n))

                    dve.wait_ge(*aff_ready(g))
                    dve.wait_ge(*rank_ready(g, ago=2))
                    v.tensor_copy(lg[:, :, :].rearrange("p t e -> p (t e)"), bank[7][:, 0:T * E]).then_inc(aff_saved.sem, 1)
                    dve.wait_ge(*aff_saved(g))
                    link(v.tensor_reduce(mx[:, 0, :], lg[:, :, :], AX, ALU.max), 1)
                    dve.wait_ge(*alpha_tanh(g, ago=1))
                    v.tensor_tensor(ala[:, :], mx[:, 0, :], inv[p][:, :], ALU.mult).then_inc(alpha_arg.sem, 1)
                    link(v.tensor_tensor(gt[:, :, :], lg[:, :, :], bc(mx[:, 0, :]), ALU.is_ge), 2)
                    link(v.tensor_tensor(pr[:, :, :], gt[:, :, :], pri[:, :, :], ALU.mult), 3)
                    link(v.tensor_reduce(mx[:, 1, :], pr[:, :, :], AX, ALU.max), 4)
                    v.tensor_tensor(oh1[p][:, :, :], pr[:, :, :], bc(mx[:, 1, :]), ALU.is_equal).then_inc(top1_done.sem, 1)
                normalise(pre, 6, True, inverse=True)
                if srt is not None:
                    dve.wait_ge(*rank_ready(g))
                    dve.wait_ge(*top1_done(g))
                    v.tensor_tensor(pos[:, :, :], bank[5][:, 0:T * E].rearrange("p (t e) -> p t e", t=T),
                                    nxt[:, :].unsqueeze(1).to_broadcast([P, T, E]), ALU.add).then_inc(row_steps.sem, 1)
                    dve.wait_ge(*row_steps(g, 1))
                    v.tensor_tensor(nxt[:, :], bank[5][:, T * E:T * E + E], nxt[:, :], ALU.add).then_inc(rank_read.sem, 1)
                    v.tensor_tensor(pos[:, :, :], pos[:, :, :], oh1[p][:, :, :], ALU.mult).then_inc(row_steps.sem, 1)
                    dve.wait_ge(*row_steps(g, 2))
                    v.tensor_reduce(slot[:, :], pos[:, :, :], AX, ALU.add).then_inc(row_steps.sem, 1)
                    dve.wait_ge(*row_steps(g, 3))
                    dve.wait_ge(*scattered[p](srt.h, ago=1))
                    v.tensor_copy(slot_i[p][:, :], slot[:, :]).then_inc(rows_ready.sem, 1)
                    v.tensor_copy(slots[:, bass.ds(srt.c * T, T)], slot[:, :])
                    v.tensor_copy(oh_all[:, bass.ds(srt.c * T, T), :], oh1[p][:, :, :])
                    dve.wait_ge(*alpha_tanh(g))
                    v.tensor_scalar(alpha[:, bass.ds(srt.c * T, T)], alt[:, :], 0.25, 0.25, ALU.mult, ALU.add
                                    ).then_inc(alpha_ready.sem, 1)
                if pre is not None:
                    dve.wait_ge(*normed(pre.gs))
                    v.scalar_tensor_tensor(xc(pre), ys[pre.p][:, :, :], 0.5, xc(pre), ALU.mult, ALU.add).then_inc(x_done.sem, 1)

            def tables(call):
                def link(ins, n):
                    ins.then_inc(tab_steps.sem, 1)
                    dve.wait_ge(*tab_steps(call, n))

                dve.wait_ge(*alpha_ready(NCH * call + NCH - 1))
                v.tensor_copy(pad_i[:, :], nxt[:, :])
                link(v.tensor_tensor(cnt[:, :], nxt[:, :], region[:, :], ALU.subtract), 1)
                link(v.tensor_scalar(cnt_i[:, :], cnt[:, :], float(P - 1), None, ALU.add), 2)
                link(v.tensor_scalar(nt_i[:, :], cnt_i[:, :], P.bit_length() - 1, None, ALU.arith_shift_right), 3)
                link(v.tensor_copy(ntf[:, :], nt_i[:, :]), 4)
                v.tensor_scalar(jump[:, :], ntf[:, :], float(-P), float(REGION), ALU.mult, ALU.add)
                link(v.tensor_tensor_scan(ends[:, :], one8[:, :], ntf[:, :], 0.0, ALU.mult, ALU.add), 5)
                over_e = lambda ap, n=NT: ap.unsqueeze(1).to_broadcast([P, n, E])
                link(v.tensor_tensor(past[:, :, :], tile_no[:, :].unsqueeze(2).to_broadcast([P, NT, E]), over_e(ends[:, :]),
                                     ALU.is_ge), 6)
                v.tensor_reduce(tab[:, 0, :], past[:, :, :], AX, ALU.add)
                link(v.tensor_tensor(hop[:, :, :], past[:, :, :], over_e(jump[:, :]), ALU.mult), 7)
                link(v.tensor_reduce(tab[:, 1, :], hop[:, :, :], AX, ALU.add), 8)
                link(v.tensor_tensor(shift[:, :], ends[:, :], ntf[:, :], ALU.subtract), 9)
                link(v.scalar_tensor_tensor(shift[:, :], shift[:, :], float(P), region[:, :], ALU.mult, ALU.subtract), 10)
                link(v.tensor_tensor(moved[:, :, :], oh_all[:, :, :], over_e(shift[:, :], NCH * T), ALU.mult), 11)
                link(v.tensor_reduce(offs[:, :], moved[:, :, :], AX, ALU.add), 12)
                v.tensor_tensor(out_rows[:, :], slots[:, :], offs[:, :], ALU.add)
                v.tensor_scalar(tab_e[:, :], tab[:, 0, :], float(E - 1), None, ALU.min)
                v.scalar_tensor_tensor(tab_row[:, :], tile_no[:, :], float(P), tab[:, 1, :], ALU.mult, ALU.add
                                       ).then_inc(tabs_ready.sem, 1)

            def expert(n0, n1, n2):
                if n1 is not None:
                    p, e = n1.p % 2, expert_of(dve, n1)
                    dve.wait_ge(*hid_ready(n1.g))
                    dve.wait_ge(*hbT_ready(n1.g, ago=2))
                    v.tensor_tensor(hb[p][:, :], bank[p][:, :], eb1b[:, bass.ds(e, 1), :].rearrange("p a f -> p (a f)"), ALU.add
                                    ).then_inc(hb_ready.sem, 1)
                if n2 is not None:
                    p, e = n2.p % 2, expert_of(dve, n2)
                    dve.wait_ge(*o_ready(n2.g))
                    dve.wait_ge(*tile_out[n2.p](n2.h, ago=1))
                    v.tensor_tensor(ob[n2.p][:, :], bank[6 + p][:, 0:P], eb2b[:, bass.ds(e, 1), :].rearrange("p a d -> p (a d)"), ALU.add
                                    ).then_inc(ob_ready.sem, 1)

            def fetch(nx):
                if nx is None:
                    return
                dve.wait_ge(*gathered[nx.p](nx.h, ago=1))
                v.tensor_copy(gslot[nx.p][:, :], out_rows[:, bass.ds(nx.c * T, T)]).then_inc(gslot_ready.sem, 1)

            def arrive(ch):
                if ch is None:
                    return
                dve.wait_ge(*gathered[ch.p](ch.h))
                for t in range(T):
                    xt = xc(ch)[:, t, :]
                    last = v.scalar_tensor_tensor(xt, got[ch.p][:, t, :], alpha[:, bass.ds(ch.c * T + t, 1)], xt,
                                                  ALU.mult, ALU.add)
                last.then_inc(arrived.sem, 1)
                dve.wait_ge(*arrived(ch.g))

            def l1_attn(nx, pre, main):
                fetch(nx)
                arrive(pre)
                statistics(pre)
                normalise(pre, 1, False)
                if main is not None:
                    g = main.g
                    for i in range(T + 1):
                        if i < T:
                            k = slice(i % 2, i % 2 + 1)
                            dve.wait_ge(*sc_ready(g, i + 1))
                            dve.wait_ge(*exp_done(g, i - 1))
                            v.tensor_reduce(mxr[:, k], bank[i % 2][:, :], AX, ALU.max).then_inc(max_done.sem, 1)
                            dve.wait_ge(*max_done(g, i + 1))
                            v.tensor_scalar(nmx[:, k], mxr[:, k], -1.0, None, ALU.mult).then_inc(nmax_done.sem, 1)
                        if i:
                            k = slice((i - 1) % 2, (i - 1) % 2 + 1)
                            dve.wait_ge(*exp_done(g, i))
                            v.reciprocal(rsi[:, k], rs[:, k]).then_inc(rsum_done.sem, 1)
                            dve.wait_ge(*rsum_done(g, i))
                            dve.wait_ge(*ao_ready(g, i))
                            xi = xc(main)[:, i - 1, :]
                            v.scalar_tensor_tensor(xi, bank[4 + (i - 1) % 2][:, 0:P], rsi[:, k], xi, ALU.mult, ALU.add
                                                   ).then_inc(ao_done.sem, 1)
                    dve.wait_ge(*ao_done(g))
                    v.tensor_copy(tick[:, :], rsi[:, 0:1]).then_inc(x_done.sem, 1)

            dve.wait_ge(*x_loaded(0, 16))
            dve.wait_ge(*constants(0))
            for stage, (kind, call) in enumerate(STAGES):
                if kind == "l1f":
                    v.tensor_copy(nxt[:, :], region[:, :]).then_inc(routing_reset.sem, 1)
                    dve.wait_ge(*routing_reset(call))
                lanes, body = {"l0f": (3, l0_ffn), "l0a": (3, l0_attn), "l1f": (2, route), "l1a": (3, l1_attn)}[kind]
                pipeline(dve, NCH, 2, lanes, call, stage, body)
                if kind == "l1f":
                    tables(call)
                    dve.wait_ge(*tabs_ready(call))
                    pipeline(dve, NT, 4, 3, call, stage, expert)
            if STAGES[-1][0] == "l1f":
                def last_chunks(nx, ch):
                    fetch(nx)
                    arrive(ch)
                pipeline(dve, NCH, 2, 2, CALLS - 1, stage, last_chunks)

        @block.gpsimd
        def _(pool):
            pool.memset(ident[:, :], 0.0).then_inc(zeroed.sem, 1)
            pool.wait_ge(zeroed.sem, 1)
            pool.affine_select(out=ident[:, :], in_=ident[:, :], compare_op=ALU.not_equal, fill=1.0, base=0,
                               pattern=[[-1, P]], channel_multiplier=1).then_inc(constants.sem, 1)
            pool.memset(neghalf[:, :], -0.5).then_inc(constants.sem, 1)
            pool.memset(eps_ln[:, :], EPS_LN).then_inc(constants.sem, 1)
            pool.memset(eps_rms[:, :], EPS_RMS).then_inc(constants.sem, 1)
            for e in range(E):
                pool.memset(pri[:, :, e:e + 1], float(E - e)).then_inc(constants.sem, 1)
            for e in range(E):
                pool.memset(region[:, e:e + 1], float(e * REGION)).then_inc(constants.sem, 1)
            pool.memset(one8[:, :], 1.0).then_inc(constants.sem, 1)
            pool.memset(zrow[:, :], 0.0).then_inc(constants.sem, 1)
            pool.memset(ones[:, :], 1.0).then_inc(constants.sem, 1)
            pool.memset(lower[:, :], 1.0).then_inc(zeroed.sem, 1)
            pool.wait_ge(zeroed.sem, 2)
            pool.affine_select(out=lower[:, :], in_=lower[:, :], compare_op=ALU.is_gt, fill=0.0, base=0,
                               pattern=[[1, P]], channel_multiplier=-1).then_inc(constants.sem, 1)
            pool.iota(tile_i[:, :], pattern=[[1, NT]], base=0, channel_multiplier=0).then_inc(zeroed.sem, 1)
            pool.wait_ge(zeroed.sem, 3)
            pool.tensor_copy(tile_no[:, :], tile_i[:, :]).then_inc(constants.sem, 1)
            pool.wait_ge(*constants(0))

            def scales(pre, eps2):
                if pre is None:
                    return
                g = pre.gs
                tt = pool.tensor_tensor
                row = lambda n: sc[:, n, :]

                def link(ins, n):
                    ins.then_inc(scale_steps.sem, 1)
                    if n < 8:
                        pool.wait_ge(*scale_steps(g, n))
                pool.wait_ge(*stats_ready(g))
                pool.wait_ge(*normed(g, ago=1))
                link(tt(row(0), mv[:, :, 1], eps_ln[:, :], ALU.add), 1)
                link(tt(row(1), row(0), neghalf[:, :], ALU.pow), 2)
                link(tt(row(2), mv[:, :, 1], row(1), ALU.mult), 3)
                link(tt(row(3), row(2), row(1), ALU.mult), 4)
                link(tt(row(4), row(3), eps2[:, :], ALU.add), 5)
                link(tt(row(5), row(4), neghalf[:, :], ALU.pow), 6)
                link(tt(row(6), row(5), row(1), ALU.mult), 7)
                link(tt(row(7), row(4), row(5), ALU.mult), 8)

            def l0_ffn(pre, main, tail):
                def total(j):
                    if main is None:
                        return
                    g = main.g
                    pool.wait_ge(*weighted(g, LAST[j]))
                    pool.wait_ge(*hidden_used(g, j - 1))
                    pool.tensor_tensor(out=gsum[j % 2][:, :], in0=gab[0][j % 2][:, :], in1=gab[1][j % 2][:, :], op=ALU.add
                                       ).then_inc(summed.sem, 1)
                scales(pre, eps_rms)
                total(0)
                total(1)
                if pre is not None:
                    pool.wait_ge(*maskT_saved(pre.g, 2))
                    pool.wait_ge(*u_masked(pre.g, ago=1))
                    pool.tensor_tensor(out=mdT[:, :], in0=mT[pre.p][1][:, :], in1=mT[pre.p][0][:, :], op=ALU.subtract
                                       ).then_inc(mdiff_ready.sem, 1)
                total(2)
                total(3)
                if pre is not None:
                    pool.wait_ge(*u_masked(pre.g))
                    pool.wait_ge(*maskT_saved(pre.g))
                    for s in range(2):
                        m = mT[pre.p][s]
                        pool.tensor_tensor(out=m[:, :], in0=m[:, :], in1=wT[pre.p][s][:, :], op=ALU.mult
                                           ).then_inc(masks_weighted.sem, 1)

            def l0_attn(pre, gat, mlp):
                if mlp is not None:
                    g = mlp.g
                    pool.wait_ge(*stats2_ready(g))
                    pool.wait_ge(*normed2(g, ago=1))
                    pool.tensor_tensor(sc2[:, 0, :], mv2[:, :, 1], eps_ln[:, :], ALU.add).then_inc(scale2_steps.sem, 1)
                    pool.wait_ge(*scale2_steps(g, 1))
                    pool.tensor_tensor(sc2[:, 1, :], sc2[:, 0, :], neghalf[:, :], ALU.pow).then_inc(scale2_steps.sem, 1)
                scales(pre, eps_ln)

            def carry_wait(ready, g, done, n):
                pool.wait_ge(*done(g, ago=1))
                pool.wait_ge(*ready(g))
                pool.tensor_tensor(out=held[:, n:n + 1], in0=one8[:, 0:1], in1=one8[:, 0:1], op=ALU.mult).then_inc(done.sem, 1)

            def route(pre, srt):
                scales(pre, eps_ln)
                if srt is not None:
                    carry_wait(rows_ready, srt.g, carried_s, 1)
                    for t in range(T):
                        pool.indirect_dma_start(rows_in[:, :], bass.IndirectOffsetOnAxis(slot_i[srt.p][:, t:t + 1], 0),
                                                yn[srt.p][:, t, :], None).then_inc(scattered[srt.p].sem, 16)

            def gather(nx):
                if nx is None:
                    return
                carry_wait(gslot_ready, nx.g, carried_g, 2)
                for t in range(T):
                    pool.indirect_dma_start(got[nx.p][:, t, :], None, rows_out[:, :],
                                            bass.IndirectOffsetOnAxis(gslot[nx.p][:, t:t + 1], 0)).then_inc(gathered[nx.p].sem, 16)

            def l1_attn(nx, pre, main):
                gather(nx)
                scales(pre, eps_ln)

            for stage, (kind, call) in enumerate(STAGES):
                lanes, body = {"l0f": (3, l0_ffn), "l0a": (3, l0_attn), "l1f": (2, route), "l1a": (3, l1_attn)}[kind]
                pipeline(pool, NCH, 2, lanes, call, stage, body)
                if kind == "l1f":
                    for b in range(4):
                        pool.wait_ge(*tile_out[b](NT // 4 * (call + 1), ago=1))
            if STAGES[-1][0] == "l1f":
                pipeline(pool, NCH, 2, 2, CALLS - 1, stage, lambda nx, ch: gather(nx))


def kernel(**inputs):
    import concourse.bacc as bacc
    from concourse.bass_utils import run_bass_kernel_spmd as run

    i = {n: np.asarray(a) for n, a in inputs.items()}
    f, a, m, t = "L0_ffn_", "L0_attn_", "L1_ffn_", "L1_attn_"
    D = P
    lay = {
        "x": i["L0_attn_x"].reshape(-1, D),
        "w1": i[f + "w1"].T, "w3": i[f + "w3"].T,
        "w2": i[f + "w2"].T.reshape(J, P, D).transpose(1, 0, 2),
        "gate": i[f + "gate_w"].T, "normw": i[f + "norm_w"].reshape(D, 1),
        "a1": i[f + "a1"].reshape(E * R, D).T, "a3": i[f + "a3"].reshape(E * R, D).T,
        "a2": i[f + "a2"].reshape(E * R, J, P).transpose(2, 1, 0),
        "b1": i[f + "b1"].transpose(0, 2, 1).reshape(E * R, J * P),
        "b3": i[f + "b3"].transpose(0, 2, 1).reshape(E * R, J * P),
        "b2": i[f + "b2"].transpose(0, 2, 1).reshape(E * R, D),
        "vecs": np.stack([i[a + n] for n in ("ln1_g", "ln1_b", "ln2_g", "ln2_b", "bv", "bo", "b2")], axis=1),
        "bif": np.stack([i[a + "bi"], i[a + "bf"]], axis=1),
        "wif": np.concatenate([i[a + "Wi"], i[a + "Wf"]], axis=1),
        "wv": i[a + "Wv"], "wo": i[a + "Wo"], "wm1": i[a + "W1"],
        "bm1": i[a + "b1"].reshape(JM, P).T, "wm2": i[a + "W2"].reshape(JM, P, D).transpose(1, 0, 2),
        "wk_l1": i[t + "Wk"], "wq_l1": i[t + "Wq"], "wv_l1": i[t + "Wv"], "waT": i[t + "Wa"].T, "wbT": i[t + "Wb"].T,
        "cen": i[m + "centroids"].T, "lng": i[m + "ln_g"].T, "lnb": i[m + "ln_b"].T,
        "e1": i[m + "w1"].transpose(1, 0, 2), "eb1": i[m + "b1"].reshape(1, -1),
        "e2": i[m + "w2"].reshape(E, J, P, D).transpose(2, 0, 1, 3), "eb2": i[m + "b2"].reshape(1, -1),
    }
    lay = {n: np.ascontiguousarray(w) for n, w in lay.items()}
    nc = bacc.Bacc("TRN2", target_bir_lowering=False, num_devices=1)
    d = {n: nc.dram_tensor(n + "_dram", w.shape, mybir.dt.from_np(w.dtype), kind="ExternalInput").ap() for n, w in lay.items()}
    out = nc.dram_tensor("out", i["L0_attn_x"].shape, F32, kind="ExternalOutput").ap()
    build(nc, d, out)
    r = run(nc, [{n + "_dram": w for n, w in lay.items()}], core_ids=[0])
    return r.results[0]["out"]
```

```python
from contextlib import ExitStack

import numpy as np
import concourse.bass as bass
from concourse import mybir

F32 = mybir.dt.float32
F32R = mybir.dt.float32r
BF16 = mybir.dt.bfloat16
I32 = mybir.dt.int32
ALU = mybir.AluOpType
ACT = mybir.ActivationFunctionType
AX = mybir.AxisListType.X

P = 128
T = 4
S = P * T
NCH = 8
E = 8
R = 16
J = 4
JM = 3
EPS_LN, EPS_RMS, EPS_DEN = 1e-5, 1e-6, 1e-6
LORA, LEAK = 2.0, 0.01
REGION = NCH * S + P
NT = NCH * S // P + E
EXTRA = E * REGION
NROWS = EXTRA + E * P
W = P + 1
STAGES = [("l0f", 0), ("l0a", 0), ("l0f", 1), ("l1f", 0), ("l1a", 0), ("l1f", 1)]


class Sem:

    def __init__(self, sem, per_chunk=1):
        self.sem, self.k = sem, per_chunk

    def __call__(self, g, n=None, ago=0):
        v = g * self.k + ((self.k if n is None else n) - ago * self.k)
        return self.sem, (max(v, 0) if isinstance(v, int) else v)


class Item:

    def __init__(self, c, p, q, count, unit, call, stage):
        self.c, self.p, self.g, self.h = c, p, c + count * call, q + count // unit * call
        self.gs, self.stage = c + count * stage, stage


def step(s, count, unit, lanes, call, stage, body, i=None):
    def item(s):
        if i is None:
            return Item(s, s % unit, s // unit, count, unit, call, stage) if 0 <= s < count else None
        return Item(unit * i + s, s % unit, i + s // unit, count, unit, call, stage)
    body(*[item(s - n) for n in range(lanes)])


def pipeline(eng, count, unit, lanes, call, stage, body, first=0, skip=0, early=()):
    args = (count, unit, lanes, call, stage, body)
    first = max(lanes, unit, first)
    rounds = (count - first) // unit
    for s in range(skip, first):
        step(s, *args)
    with eng.Fori(0, rounds) as i:
        for s in range(first, first + unit):
            step(s, *args, i)
    for s in range(first + unit * rounds, count + lanes - 1):
        for at, run in early:
            if at == s:
                run()
        step(s, *args)


def build(nc, d, out):
    with ExitStack() as ctx:
        def sb(name, shape, dt=F32):
            return ctx.enter_context(nc.sbuf_tensor(name, shape, dt))

        def sem(name, per_chunk=1):
            return Sem(ctx.enter_context(nc.semaphore(name)), per_chunk)

        def tok(ap):
            return ap.rearrange("p (t d) -> p t d", t=T)

        bank = [ctx.enter_context(nc.psum_tensor(f"bank{i}", [P, S], F32)) for i in range(8)]

        x = sb("x", [P, NCH * T, P])
        ident = sb("ident", [P, P]); ident_bf = sb("ident_bf", [P, P], BF16)
        neghalf = sb("neghalf", [P, T]);
        pri = sb("pri", [P, T, E])
        w2 = sb("w2", [P, J, P])
        gate = sb("gate", [P, E]); normw = sb("normw", [P, 1])
        a1 = sb("a1", [P, P]); a3 = sb("a3", [P, P]); a2 = sb("a2", [P, J, P])
        b2 = sb("b2", [P, P])
        vecs = sb("vecs", [P, 8]); bif = sb("bif", [P, 2]); wif = sb("wif", [P, 2])
        wi_b = sb("wi_b", [P, P]); wf_b = sb("wf_b", [P, P])
        wv = sb("wv", [P, P]); wo = sb("wo", [P, P])
        wm1 = sb("wm1", [P, JM * P]); bm1 = sb("bm1", [P, JM]); wm2 = sb("wm2", [P, JM, P])
        wk_l1 = sb("wk_l1", [P, P]); wq_l1 = sb("wq_l1", [P, P]); wv_l1 = sb("wv_l1", [P, P])
        waT = sb("waT", [P, P]); wbT = sb("wbT", [P, P])
        wak = sb("wak", [P, P]); gmat = sb("gmat", [P, P]); wuT = sb("wuT", [P, P])
        cen = sb("cen", [P, E]); lng = sb("lng", [P, E]); lnb = sb("lnb", [P, E])

        stats = sb("stats", [P, T, 6]); part = sb("part", [P, 4, T]); mv = [sb(f"mv{i}", [P, T, 2]) for i in range(2)]
        sc = [sb(f"sc{i}", [P, 4, T]) for i in range(2)]
        yw = [sb(f"yw{i}", [P, T, W]) for i in range(4)]
        yn4 = [w[:, :, 0:P] for w in yw]
        yn = yn4[:2]
        ys = [sb(f"ys{i}", [P, T, P]) for i in range(2)]
        tT = [sb(f"tT{i}", [P, S]) for i in range(2)]
        lg = sb("lg", [P, T, E]); lg2 = sb("lg2", [P, T, E]); gt = sb("gt", [P, T, E]); pr = sb("pr", [P, T, E])
        mx = sb("mx", [P, 4, T]); dlt = sb("dlt", [P, T]); th = sb("th", [P, T]); wts = sb("wts", [P, T])
        oh = [sb(f"oh{i}", [P, T, E, R], BF16) for i in range(2)]
        mT = [[sb(f"mT{i}{k}", [P, S]) for k in range(2)] for i in range(2)]
        mdT = sb("mdT", [P, S])
        wT = [[sb(f"wT{i}{k}", [P, S]) for k in range(2)] for i in range(2)]
        ua, ud = [sb(f"ua{k}", [P, S]) for k in range(2)], [sb(f"ud{k}", [P, S]) for k in range(2)]
        sil = [sb(f"sil{i}", [P, S]) for i in range(2)]
        act_ = [[sb(f"act{s}{i}", [P, S]) for i in range(2)] for s in range(2)]
        gab = [[sb(f"gab{s}{i}", [P, S]) for i in range(2)] for s in range(2)]
        (w1, w3), (b1, b3) = gab
        gsum = [sb(f"gsum{i}", [P, S]) for i in range(2)]
        r1 = sb("r1", [P, S]); r2 = sb("r2", [P, S]); rr = sb("rr", [P, S]); oT = sb("oT", [P, S])
        hT, gi, gf, go = tT, sil[0], sil[1], act_[0][0]
        iv, num, den, oaT = act_[0][1], act_[1][0], act_[1][1], gab[0][1]
        denc = sb("denc", [P, 2, T])
        z, h2, h2T = sb("z", [P, T, P]), sb("h2", [P, T, P]), gab[1][0]
        mpre, mlk, msq, moT = mT[0] + mT[1][:1], wT[0] + wT[1][:1], ua + ud[:1], oT
        stats2 = sb("stats2", [P, T, 6]); mv2 = sb("mv2", [P, T, 2]); part2 = sb("part2", [P, 4, T]); sc2 = sb("sc2", [P, 2, T])
        lower = sb("lower", [P, P]); ones = sb("ones", [P, P]); zrow = sb("zrow", [P, 2 * E, W]); token_i = sb("token_i", [P, NCH * T + 2 * E], I32); token = sb("token", [P, NCH * T + 2 * E])
        region = sb("region", [P, E]); one8 = sb("one8", [P, E]); tile_i = sb("tile_i", [P, NT], I32)
        tile_no = sb("tile_no", [P, NT])
        xnT = tT
        oh1 = [sb(f"oh1{i}", [P, T, E]) for i in range(2)]
        inv = [sb(f"inv{i}", [P, T]) for i in range(2)]; invs = sb("invs", [P, T]); ala = sb("ala", [P, T]); alt = sb("alt", [P, T])
        alpha = sb("alpha", [P, NCH * T])
        nxt = sb("nxt", [P, E])
        pos = sb("pos", [P, T, E]); slot = sb("slot", [P, T]); slot_i = [sb(f"slot_i{i}", [P, T], I32) for i in range(4)]
        cnt = sb("cnt", [P, E]); cnt_i = sb("cnt_i", [P, E], I32); nt_i = sb("nt_i", [P, E], I32); ntf = sb("ntf", [P, E])
        ends = sb("ends", [P, E]); jump = sb("jump", [P, E]); past = sb("past", [P, NT, E]); hop = sb("hop", [P, NT, E])
        tab = sb("tab", [P, 2, NT]); tab_e = sb("tab_e", [P, NT], I32); tab_row = sb("tab_row", [P, NT], I32)
        pad_i = sb("pad_i", [P, E], I32)
        eb2b = sb("eb2b", [P, E, P])
        xin = [sb(f"xin{i}", [P, W]) for i in range(4)]
        xlT = [sb(f"xlT{i}", [P, P]) for i in range(2)]
        hb, hbT = sil, [act_[0][0], act_[0][1]]
        ob = [sb(f"ob{i}", [P, P]) for i in range(4)]
        ids = [sb(f"ids{i}", [P, 1], I32) for i in range(4)]
        got = [yn4[2], yn4[3]]
        rows_in = nc.dram_tensor("rows_in", [NROWS, W], F32, kind="Internal").ap()
        rows_out = nc.dram_tensor("rows_out", [NCH * S + 2 * E * P, P], F32, kind="Internal").ap()
        yT, zT, pr_, pT = tT, mT[0], [act_[0][0], act_[0][1]], [act_[1][0], act_[1][1]]
        vu = [z, h2]
        mxr = sb("mxr", [P, 2]); nmx = sb("nmx", [P, 2]); rs = sb("rs", [P, 2]); rsi = sb("rsi", [P, T]); tick = sb("tick", [P, 1]); held = sb("held", [P, 3])
        with nc.sbuf_tensor("split", [P, 29 * S], F32R) as split:
            def parts(n, width=S):
                return tuple(split[:, (n + k) * S:(n + k) * S + width] for k in range(2))
            w1s, w3s, b1s, b3s = parts(0), parts(2), parts(4), parts(6)
            a1s, a3s = (tuple(split[:, 8 * S + (k + i) * P:8 * S + (k + i + 1) * P] for k in range(2)) for i in (0, 2))
            ts = [parts(9), parts(11)]
            uas = [[parts(13 + 8 * p + 2 * i) for i in range(2)] for p in range(2)]
            uds = [[parts(17 + 8 * p + 2 * i) for i in range(2)] for p in range(2)]
        e1 = sb("e1", [P, E, J * P]); e2 = sb("e2", [P, E, J, P]); eb1b = sb("eb1b", [P, E, J * P])
        whole = lambda *pairs: [(t[tuple([slice(None)] * len(d[n].shape))], d[n]) for n, t in pairs]
        ffn_loads = whole(("normw", normw), ("gate", gate), ("a1", a1), ("a3", a3), ("b1", b1), ("w1", w1), ("b3", b3),
                          ("w3", w3), ("a2", a2), ("w2", w2), ("b2", b2))
        loads = whole(
            ("wif", wif), ("wv", wv), ("wo", wo), ("wm1", wm1),
            ("bm1", bm1), ("wm2", wm2), ("wk_l1", wk_l1), ("wq_l1", wq_l1), ("wv_l1", wv_l1), ("waT", waT), ("wbT", wbT),
            ("cen", cen), ("lng", lng), ("lnb", lnb))
        loads += [(vecs[:, 0:7], d["vecs"]), (bif[:, :], d["bif"].to_broadcast([P, 2])),
                  (eb2b[:, :, :].rearrange("p e d -> p (e d)"), d["eb2"].to_broadcast([P, E * P]))]

        late_loads = whole(("e1", e1), ("e2", e2)) + [(eb1b[:, :, :].rearrange("p e f -> p (e f)"), d["eb1"].to_broadcast([P, E * J * P]))]

        late_loaded, ffn_loaded, weights_loaded, x0_loaded, x_loaded, x_stored = sem("late_loaded"), sem("ffn_loaded"), sem("weights_loaded"), sem("x0_loaded"), sem("x_loaded"), sem("x_stored")
        zeroed, constants = sem("zeroed"), sem("constants", 10 + 2 * E)
        prod_ready, prod_saved, scaled, spread, weight_high, weight_low = (
            sem("prod_ready"), sem("prod_saved"), sem("scaled"), sem("spread"), sem("weight_high"), sem("weight_low"))
        x_done, bn_done, stats_ready = sem("x_done"), sem("bn_done", 4), sem("stats_ready")
        scale_steps, normed, transposed = sem("scale_steps", 2), sem("normed"), sem("transposed")
        h1_ready, h3_ready, silu_done, act_done = (sem(n, 8) for n in ("h1_ready", "h3_ready", "silu_done", "act_done"))
        weighted, summed, hidden_used = sem("weighted", 8), sem("summed", 4), sem("hidden_used", 4)
        r_steps, r_ready, out_ready, outT_saved, back_ready = (
            sem("r_steps", 2), sem("r_ready"), sem("out_ready"), sem("outT_saved"), sem("back_ready"))
        t_ready, logits_ready, logits_read, top2_steps = (
            sem("t_ready"), sem("logits_ready"), sem("logits_read"), sem("top2_steps", 9))
        onehots, delta, tanh_done, slot_w = sem("onehots", 2), sem("delta"), sem("tanh_done"), sem("slot_w")
        maskT_ready, maskT_saved, mdiff_ready = sem("maskT_ready", 3), sem("maskT_saved", 4), sem("mdiff_ready")
        u_ready, u_masked, masks_weighted = sem("u_ready", 2), sem("u_masked", 4), sem("masks_weighted", 2)
        t_low, u_high, u_low = sem("t_low"), sem("u_high", 4), sem("u_low", 4)
        hT_saved, gates_ready, gates_saved = sem("hT_saved"), sem("gates_ready", 4), sem("gates_saved", 3)
        scan_steps, oa_ready, oab_ready = sem("scan_steps", 3), sem("oa_ready"), sem("oab_ready")
        z_ready, bn2_done, stats2_ready, scale2_steps = sem("z_ready"), sem("bn2_done", 4), sem("stats2_ready"), sem("scale2_steps")
        normed2, h2T_ready, h2T_saved = sem("normed2"), sem("h2T_ready"), sem("h2T_saved")
        m_ready, m_saved, m_leaky, m_squared = sem("m_ready", 3), sem("m_saved", 3), sem("m_leaky", 3), sem("m_squared", 3)
        den_steps = sem("den_steps", 2)
        mo_ready, moT_saved, mback_ready, z_added = sem("mo_ready"), sem("moT_saved"), sem("mback_ready"), sem("z_added")
        xnT_saved, aff_ready, aff_saved = sem("xnT_saved"), sem("aff_ready"), sem("aff_saved")
        top1_steps, top1_done, alpha_arg, alpha_tanh, alpha_ready = (
            sem("top1_steps", 4), sem("top1_done"), sem("alpha_arg"), sem("alpha_tanh"), sem("alpha_ready"))
        rank_ready, rank_read, row_steps, rows_ready = (
            sem("rank_ready"), sem("rank_read"), sem("row_steps", 3), sem("rows_ready"))
        scattered = [sem(f"scattered{i}", 16 * T) for i in range(4)]
        fetched = [sem(f"fetched{i}", 16) for i in range(2)]
        arrived = sem("arrived")
        carried_s, carried_o, ids_ready = sem("carried_s"), sem("carried_o"), sem("ids_ready")
        routing_reset, inv_steps = sem("routing_reset"), sem("inv_steps", 2)
        numbered = sem("numbered")
        ends_ready, tab_steps, tabs_ready, extra_zeroed, padded = sem("ends_ready"), sem("tab_steps", 8), sem("tabs_ready"), sem("extra_zeroed", 16), sem("padded", 16 * E)
        tile_in = [sem(f"tile_in{i}", 16) for i in range(4)]
        tile_T, xlT_saved, hid_ready, hb_ready, hbT_ready, hbT_saved, o_ready, ob_ready = (
            sem(n) for n in ("tile_T", "xlT_saved", "hid_ready", "hb_ready", "hbT_ready", "hbT_saved", "o_ready", "ob_ready"))
        tile_out = [sem(f"tile_out{i}", 16) for i in range(4)]
        yT_ready, yT_saved, zT_ready, zT_saved, v_ready, v_saved = (
            sem("yT_ready"), sem("yT_saved"), sem("zT_ready"), sem("zT_saved"), sem("v_ready"), sem("v_saved"))
        sc_ready, max_done, nmax_done, exp_done, pT_ready, pT_saved = (
            sem(n, 4) for n in ("sc_ready", "max_done", "nmax_done", "exp_done", "pT_ready", "pT_saved"))
        rsum_done, ao_ready, ao_done = sem("rsum_done", 4), sem("ao_ready", 4), sem("ao_done", 4)

        block = ctx.enter_context(nc.Block())

        STEPS = [(0, 0), (1, 0), (0, 1), (1, 1), (2, 0), (3, 0), (2, 1), (3, 1)]
        LAST = [STEPS.index((j, 1)) + 1 for j in range(J)]
        BH1, BH3, BV, BOUT, BMISC = (0, 1), (2, 3), (4, 5), 6, 7

        SPLITS = [(a1s, a1, 1.0), (a3s, a3, 1.0), (w1s, w1, 1.0), (b1s, b1, LORA), (w3s, w3, 1.0), (b3s, b3, LORA)]
        CALLS = sum(kind == "l1f" for kind, _ in STAGES)
        AFTER = {n + 1 for n, (kind, _) in enumerate(STAGES) if kind == "l1f"}

        def expert_of(eng, tile):
            return eng.value_load(tab_e[0:1, bass.ds(tile.c, 1)], min_val=0, max_val=E - 1)

        LANES = {"l0f": 4, "l0a": 6, "l1f": 3, "l1a": 3}
        UNIT = {"l0f": 2, "l0a": 2, "l1f": 4, "l1a": 2}

        def steps_early(stage):
            if stage in (-1, len(STAGES) - 1) or STAGES[stage][0] == "l1f" or STAGES[stage + 1][0] == "l1a":
                return 0
            return 2 if STAGES[stage][0] == "l0f" and STAGES[stage + 1][0] == "l0a" else 1

        def run_stage(eng, stage, bodies):
            def args(n):
                kind, call = STAGES[n]
                return NCH, UNIT[kind], LANES[kind], call, n, bodies[kind]
            n = steps_early(stage)
            end = NCH + LANES[STAGES[stage][0]] - 1
            early = [(end - n + k, lambda k=k: step(k, *args(stage + 1))) for k in range(n)]
            pipeline(eng, *args(stage), skip=steps_early(stage - 1), early=early)

        def window(eng, row, first, n, most):
            return nc.values_load_multi_w_load_instructions(row[0:1, bass.ds(first, n)], engines=(eng.engine,),
                                                            min_val=0, max_val=most)[1]

        def experts(eng, kept, n0, n3, *tiles):
            if n0 is None or isinstance(n0.c, int):
                return [expert_of(eng, t) if t is not None else None for t in tiles]
            at = (n0.p - 1) % 4
            if at == 0:
                kept[:] = window(eng, tab_e, n3.c, 7, E - 1)
            return [kept[at + {n3: 0, n0: 3}.get(t, 2)] for t in tiles]

        def before_stage(eng, stage):
            if stage in AFTER:
                eng.wait_ge(*ob_ready(NT * (STAGES[stage - 1][1] + 1), ago=1))
            else:
                eng.wait_ge(*x_done(NCH * stage, ago=1))

        def first_chunk(ch):
            return ch.stage == 0 and isinstance(ch.c, int) and ch.c == 0

        def xc(ch):
            return x[:, bass.ds(ch.c * T, T), :]

        def fl(ap):
            return ap.rearrange("p t d -> p (t d)")

        kept_pe, kept_act, kept_dve = [], [], []

        @block.sync
        def _(sp):
            o = out.rearrange("a s d -> (a s) d").rearrange("(n p) d -> p n d", p=P)
            xd = d["x"].rearrange("(n p) d -> p n d", p=P)
            sp.dma_start(x[:, 0:T, :], xd[:, 0:T, :]).then_inc(x0_loaded.sem, 16)
            for dst, src in ffn_loads:
                sp.dma_start(dst, src).then_inc(ffn_loaded.sem, 16)
            sp.dma_start(x[:, T:, :], xd[:, T:, :]).then_inc(x_loaded.sem, 16)
            for dst, src in loads:
                sp.dma_start(dst, src).then_inc(weights_loaded.sem, 16)
            sp.wait_ge(*constants(0))
            sp.dma_start(rows_in[EXTRA:, :].rearrange("(n p) d -> p n d", p=P), zrow[:, E:, :]).then_inc(extra_zeroed.sem, 16)
            l0_stages = [n for n, (kind, _) in enumerate(STAGES) if kind == "l0f"]
            if l0_stages:
                sp.wait_ge(*x_done(NCH * l0_stages[-1] + NCH - 1))
            for dst, src in late_loads:
                sp.dma_start(dst, src).then_inc(late_loaded.sem, 16)
            for call in range(CALLS):
                sp.wait_ge(*ends_ready(call))
                for e, r in enumerate(window(sp, pad_i, 0, E, EXTRA - P)):
                    sp.dma_start(rows_in[bass.ds(r, P), :], zrow[:, e, :]).then_inc(padded.sem, 16)
                sp.wait_ge(*tabs_ready(call))
                sp.wait_ge(*padded(call))
                for i in range(4):
                    sp.wait_ge(*scattered[i](NCH // 4 * (call + 1), ago=1))
                if call == 0:
                    sp.wait_ge(*extra_zeroed(0))

                def load(t, b, r=None):
                    if r is None:
                        r = sp.value_load(tab_row[0:1, bass.ds(t, 1)], min_val=0, max_val=NROWS - P)
                    sp.dma_start(xin[b][:, :], rows_in[bass.ds(r, P), :]).then_inc(tile_in[b].sem, 16)

                for b in range(4):
                    load(b, b)

                def next_load(t, b, r=None):
                    sp.wait_ge(*tile_T(t + NT * call))
                    sp.wait_ge(*ids_ready(t + NT * call))
                    load(t + 4, b, r)

                for b in range(4):
                    next_load(b, b)
                with sp.Fori(0, NT // 4 - 2) as i:
                    starts = window(sp, tab_row, 4 * i + 8, 4, NROWS - P)
                    for b in range(4):
                        next_load(4 * i + (4 + b), b, starts[b])

                for b in range(4):
                    sp.wait_ge(*tile_out[b](NT // 4 * (call + 1), ago=1))

                def fetch(c, p):
                    sp.dma_start(got[p], rows_out[bass.ds(c * S, S), :].rearrange("(t p) d -> p t d", p=P)
                                 ).then_inc(fetched[p].sem, 16)

                def store(c):
                    sp.dma_start(o[:, bass.ds(c * T, T), :], x[:, bass.ds(c * T, T), :]).then_inc(x_stored.sem, 16)

                final = call == CALLS - 1 and STAGES[-1][0] == "l1f"
                for p in range(2):
                    fetch(p, p)
                with sp.Fori(0, NCH // 2 - 1) as i:
                    for p in range(2):
                        sp.wait_ge(*arrived(2 * i + (p + NCH * call)))
                        fetch(2 * i + (p + 2), p)
                        if final:
                            store(2 * i + p)
                if final:
                    for c in range(NCH - 2, NCH):
                        sp.wait_ge(*arrived(c + NCH * call))
                        store(c)
            if STAGES[-1][0] != "l1f":
                for c in range(NCH):
                    sp.wait_ge(*x_done(c + NCH * (len(STAGES) - 1)))
                    store(c)
            sp.wait_ge(x_stored.sem, 16 * NCH)

        @block.tensor
        def _(pe):
            mm, tr = nc.tensor.matmul, nc.tensor.transpose

            def transpose4(dst, src):
                for t in range(T):
                    last = tr(bank[dst][:, t * P:(t + 1) * P], src(t), ident[:, :])
                return last

            pe.wait_ge(*constants(0))

            def mm3(dst, w, m, start, stop, **more):
                mm(dst, w[0], m[0], start=start, stop=False, **more)
                mm(dst, w[0], m[1], start=False, stop=False, **more)
                return mm(dst, w[1], m[0], start=False, stop=stop, **more)

            def products():
                pe.wait_ge(weights_loaded.sem, 16 * len(loads))
                mm(bank[0][:, 0:P], waT[:, :], wk_l1[:, :], start=True, stop=True).then_inc(prod_ready.sem, 1)
                mm(bank[1][:, 0:P], wv_l1[:, :], wbT[:, :], start=True, stop=True).then_inc(prod_ready.sem, 1)
                pe.wait_ge(prod_saved.sem, 1)
                mm(bank[2][:, 0:P], wq_l1[:, :], wak[:, :], start=True, stop=True).then_inc(prod_ready.sem, 1)
                pe.wait_ge(prod_saved.sem, 3)

            def l0_ffn(st, pre, main, tail):
                def hidden(k):
                    if main is None:
                        return
                    (j, s), g, p = STEPS[k - 1], main.g, main.p
                    f = slice(j * P, (j + 1) * P)
                    if k == 1:
                        pe.wait_ge(*t_low(g))
                    if k == 3:
                        pe.wait_ge(*u_low(g))
                    for i, (h, base, lora, ready, read) in enumerate(((BH1, w1s, b1s, h1_ready, silu_done),
                                                                      (BH3, w3s, b3s, h3_ready, act_done))):
                        b = bank[h[j % 2]]
                        cut = lambda w: (w[0][:, f], w[1][:, f])
                        pe.wait_ge(*read(g, k - 2))
                        if s == 0:
                            mm3(b[:, :], cut(base), ts[p], True, False)
                            if k == 1:
                                pe.wait_ge(*u_low(g, 2 * i + 1))
                            mm3(b[:, :], cut(lora), uas[p][i], False, True).then_inc(ready.sem, 1)
                        else:
                            mm3(b[:, :], cut(lora), uds[p][i], False, True, skip_group_check=True).then_inc(ready.sem, 1)

                def down(j):
                    if main is None:
                        return
                    g = main.g
                    if j == 0:
                        pe.wait_ge(*r_ready(g, ago=1))
                        pe.wait_ge(*x_done(main.gs, ago=1))
                    pe.wait_ge(*act_done(g, LAST[j]))
                    for s in range(2):
                        mm(bank[BV[s]][:, :], a2[:, j, :], act_[s][j % 2][:, :], start=j == 0, stop=j == J - 1)
                    pe.wait_ge(*summed(g, j + 1))
                    mm(bank[BOUT][:, :], w2[:, j, :], gsum[j % 2][:, :], start=j == 0, stop=False
                       ).then_inc(hidden_used.sem, 1)

                def mask(n, src):
                    if pre is None:
                        return
                    if n:
                        pe.wait_ge(*maskT_saved(pre.g, n))
                    for t in range(T):
                        if n < 2:
                            last = mm(bank[BMISC][:, t * P:(t + 1) * P], src(t), ident_bf[:, :], start=True, stop=True)
                        else:
                            last = tr(bank[BMISC][:, t * P:(t + 1) * P], src(t), ident[:, :])
                    last.then_inc(maskT_ready.sem, 1)

                def up(i):
                    if pre is None:
                        return
                    if i == 0:
                        pe.wait_ge(*maskT_saved(pre.g))
                        pe.wait_ge(*t_low(pre.g))
                        if first_chunk(pre):
                            pe.wait_ge(weight_low.sem, 6)
                            pe.wait_ge(scaled.sem, 1)
                    else:
                        pe.wait_ge(*u_masked(pre.g, 2))
                    mm3(bank[BMISC][:, :], (a1s, a3s)[i], ts[pre.p], True, True).then_inc(u_ready.sem, 1)

                hidden(1)
                hidden(2)
                if tail is not None:
                    pe.wait_ge(*r_ready(tail.g))
                    mm(bank[BOUT][:, :], b2[:, :], rr[:, :], start=False, stop=True).then_inc(out_ready.sem, 1)
                if pre is not None:
                    pe.wait_ge(*normed(pre.gs))
                    pe.wait_ge(*u_masked(pre.g, ago=1))
                    transpose4(BMISC, lambda t: yn[pre.p][:, t, :]).then_inc(transposed.sem, 1)
                hidden(3)
                if tail is not None:
                    pe.wait_ge(*outT_saved(tail.g))
                    transpose4(BOUT, lambda t: oT[:, t * P:(t + 1) * P]).then_inc(back_ready.sem, 1)
                if pre is not None:
                    pe.wait_ge(*t_ready(pre.g))
                    if first_chunk(pre):
                        pe.wait_ge(ffn_loaded.sem, 16 * len(ffn_loads))
                    for t in range(T):
                        last = mm(bank[BMISC][:, t * E:(t + 1) * E], tT[pre.p][:, t * P:(t + 1) * P], gate[:, :],
                                  start=True, stop=True)
                    last.then_inc(logits_ready.sem, 1)
                hidden(4)
                hidden(5)
                down(0)
                if pre is not None:
                    pe.wait_ge(*onehots(pre.g, 1))
                mask(0, lambda t: oh[0][:, t, :, :].rearrange("p e r -> p (e r)"))
                hidden(6)
                if pre is not None:
                    pe.wait_ge(*onehots(pre.g))
                mask(1, lambda t: oh[1][:, t, :, :].rearrange("p e r -> p (e r)"))
                down(1)
                if pre is not None:
                    pe.wait_ge(*slot_w(pre.g))
                mask(2, lambda t: wts[:, t:t + 1].to_broadcast([P, P]))
                hidden(7)
                up(0)
                hidden(8)
                down(2)
                up(1)
                down(3)

            def l0_attn(st, pre, gat, nrm, up, dn):
                if nrm is not None:
                    g = nrm.g
                    pe.wait_ge(*oa_ready(g))
                    pe.wait_ge(*m_saved(g, ago=2))
                    transpose4(5, lambda t: oaT[:, t * P:(t + 1) * P])
                    for t in range(T):
                        last = mm(bank[6][:, t:t + 1], den[0:1, t * P:(t + 1) * P], ones[0:1, 0:1], start=True, stop=True)
                    last.then_inc(oab_ready.sem, 1)
                if gat is not None:
                    pe.wait_ge(*hT_saved(gat.g))
                    pe.wait_ge(*gates_saved(gat.g, ago=1))
                    pe.wait_ge(*scan_steps(gat.g, 1, ago=1))
                    for b, w in ((1, wi_b), (2, wf_b), (3, wo), (0, wv)):
                        mm(bank[b][:, :], w[:, :], hT[gat.p][:, :], start=True, stop=True).then_inc(gates_ready.sem, 1)
                if up is not None:
                    pe.wait_ge(*normed2(up.g))
                    transpose4(7, lambda t: h2[:, t, :]).then_inc(h2T_ready.sem, 1)
                if dn is not None:
                    pe.wait_ge(*m_squared(dn.g))
                    pe.wait_ge(*x_done(dn.gs, ago=1))
                    for j in range(JM):
                        last = mm(bank[4][:, :], wm2[:, j, :], msq[j][:, :], start=j == 0, stop=j == JM - 1)
                    last.then_inc(mo_ready.sem, 1)
                if pre is not None:
                    pe.wait_ge(*normed(pre.gs))
                    if up is not None:
                        pe.wait_ge(*h2T_saved(up.g))
                    else:
                        pe.wait_ge(*hT_saved(pre.g, ago=1))
                    transpose4(7, lambda t: yn[pre.p][:, t, :]).then_inc(transposed.sem, 1)
                if up is not None:
                    g = up.g
                    pe.wait_ge(*h2T_saved(g))
                    pe.wait_ge(*m_saved(g, ago=1))
                    pe.wait_ge(*z_ready((nrm or up).g))
                    for j in range(JM):
                        if j == 2:
                            pe.wait_ge(*m_saved(g, 1))
                        mm(bank[5 + j % 2][:, :], wm1[:, j * P:(j + 1) * P], h2T[:, :], start=True, stop=True
                           ).then_inc(m_ready.sem, 1)
                if dn is not None:
                    pe.wait_ge(*moT_saved(dn.g))
                    transpose4(4, lambda t: moT[:, t * P:(t + 1) * P]).then_inc(mback_ready.sem, 1)

            def route(st, pre, srt):
                if srt is not None:
                    g, p = srt.g, srt.p % 2
                    pe.wait_ge(*xnT_saved(g))
                    pe.wait_ge(*aff_saved(g, ago=1))
                    for t in range(T):
                        last = mm(bank[7][:, t * E:(t + 1) * E], xnT[p][:, t * P:(t + 1) * P], cen[:, :],
                                  start=True, stop=True)
                    last.then_inc(aff_ready.sem, 1)
                if pre is not None:
                    pe.wait_ge(*normed(pre.gs))
                    pe.wait_ge(*xnT_saved(pre.g, ago=1))
                    transpose4(6, lambda t: yn4[pre.p][:, t, :]).then_inc(transposed.sem, 1)
                if srt is not None:
                    pe.wait_ge(*top1_done(g))
                    pe.wait_ge(*rank_read(g, ago=1))
                    for t in range(T + 1):
                        for u in range(min(t + 1, T)):
                            last = mm(bank[5][:, t * E:(t + 1) * E], (lower if u == t else ones)[:, :], oh1[p][:, u, :],
                                      start=u == 0, stop=u == min(t, T - 1))
                    last.then_inc(rank_ready.sem, 1)

            def expert(n0, n1, n2, n3):
                e_n1, e_n3 = experts(pe, kept_pe, n0, n3, n1, n3)
                if n1 is not None:
                    p, e = n1.p % 2, e_n1
                    pe.wait_ge(*xlT_saved(n1.g))
                    pe.wait_ge(*hb_ready(n1.g, ago=2))
                    mm(bank[p][:, :], xlT[p][:, :], e1[:, bass.ds(e, 1), :].rearrange("p a f -> p (a f)"),
                       start=True, stop=True).then_inc(hid_ready.sem, 1)
                if n0 is not None:
                    pe.wait_ge(*tile_in[n0.p](n0.h))
                    pe.wait_ge(*xlT_saved(n0.g, ago=2))
                    tr(bank[4 + n0.p % 2][:, 0:P], xin[n0.p][:, 0:P], ident[:, :]).then_inc(tile_T.sem, 1)
                if n2 is not None:
                    p = n2.p % 2
                    pe.wait_ge(*hb_ready(n2.g))
                    pe.wait_ge(*hbT_saved(n2.g, ago=2))
                    for j in range(J):
                        last = tr(bank[2 + p][:, j * P:(j + 1) * P], hb[p][:, j * P:(j + 1) * P], ident[:, :])
                    last.then_inc(hbT_ready.sem, 1)
                if n3 is not None:
                    p, e = n3.p % 2, e_n3
                    pe.wait_ge(*hbT_saved(n3.g))
                    pe.wait_ge(*ob_ready(n3.g, ago=2))
                    for j in range(J):
                        last = mm(bank[6 + p][:, 0:P], hbT[p][:, j * P:(j + 1) * P],
                                  e2[:, bass.ds(e, 1), j, :].rearrange("p a d -> p (a d)"), start=j == 0, stop=j == J - 1)
                    last.then_inc(o_ready.sem, 1)

            def l1_attn(st, pre, main):
                def rows(n):
                    if main is None:
                        return
                    g, p = main.g, main.p
                    if n < T:
                        pe.wait_ge(*exp_done(g, n - 1))
                        mm(bank[n % 2][:, :], zT[p][:, n * P:(n + 1) * P], yT[p][:, :], start=True, stop=True
                           ).then_inc(sc_ready.sem, 1)
                    if 1 <= n <= T:
                        k = (n - 1) % 2
                        pe.wait_ge(*exp_done(g, n))
                        pe.wait_ge(*pT_saved(g, n - 2))
                        transpose4(2 + k, lambda t: pr_[k][:, t * P:(t + 1) * P]).then_inc(pT_ready.sem, 1)
                    if n >= 2:
                        k = n % 2
                        pe.wait_ge(*pT_saved(g, n - 1))
                        pe.wait_ge(*ao_done(g, n - 3))
                        for t in range(T):
                            last = mm(bank[4 + k][:, 0:P], pT[k][:, t * P:(t + 1) * P], vu[p][:, t, :],
                                      start=t == 0, stop=t == T - 1)
                        last.then_inc(ao_ready.sem, 1)

                rows(0)
                if pre is not None:
                    pe.wait_ge(*normed(pre.gs))
                    pe.wait_ge(*v_saved(pre.g, ago=1))
                    transpose4(7, lambda t: yn[pre.p][:, t, :]).then_inc(transposed.sem, 1)
                rows(1)
                rows(2)
                rows(3)
                if pre is not None:
                    pe.wait_ge(*yT_saved(pre.g))
                    mm(bank[7][:, :], gmat[:, :], yT[pre.p][:, :], start=True, stop=True).then_inc(zT_ready.sem, 1)
                rows(4)
                if pre is not None:
                    pe.wait_ge(*zT_saved(pre.g))
                    for t in range(T):
                        last = mm(bank[7][:, t * P:(t + 1) * P], yT[pre.p][:, t * P:(t + 1) * P], wuT[:, :],
                                  start=True, stop=True)
                    last.then_inc(v_ready.sem, 1)
                rows(5)

            for stage, (kind, call) in enumerate(STAGES):
                before_stage(pe, stage)
                if kind == "l0a":
                    pe.wait_ge(spread.sem, 2)
                run_stage(pe, stage, {"l0f": l0_ffn, "l0a": l0_attn, "l1f": route, "l1a": l1_attn})
                if kind == "l1f":
                    if call == 0:
                        products()
                    pe.wait_ge(*tabs_ready(call))
                    pe.wait_ge(late_loaded.sem, 16 * len(late_loads))
                    pipeline(pe, NT, 4, 4, call, stage, expert, first=5)

        @block.scalar
        def _(act):
            af = nc.scalar.activation

            act.wait_ge(ffn_loaded.sem, 16 * len(ffn_loads))
            for dst, w, f in SPLITS:
                af(dst[0], w[:, :], ACT.Copy, scale=f).then_inc(weight_high.sem, 1)
            af(b2[:, :], b2[:, :], ACT.Copy, scale=LORA).then_inc(scaled.sem, 1)

            def products():
                act.wait_ge(weights_loaded.sem, 16 * len(loads))
                act.wait_ge(prod_ready.sem, 2)
                af(wak[:, :], bank[0][:, 0:P], ACT.Copy).then_inc(prod_saved.sem, 1)
                af(wuT[:, :], bank[1][:, 0:P], ACT.Copy).then_inc(prod_saved.sem, 1)
                act.wait_ge(prod_ready.sem, 3)
                af(gmat[:, :], bank[2][:, 0:P], ACT.Copy).then_inc(prod_saved.sem, 1)

            def l0_ffn(st, pre, main, tail):
                def silu(k):
                    if main is None:
                        return
                    g = main.g
                    act.wait_ge(*h1_ready(g, k))
                    act.wait_ge(*act_done(g, k - 2))
                    af(sil[(k - 1) % 2][:, :], bank[BH1[STEPS[k - 1][0] % 2]][:, :], ACT.Silu).then_inc(silu_done.sem, 1)

                def mask(n, dst, **affine):
                    if pre is None:
                        return
                    act.wait_ge(*maskT_ready(pre.g, min(n + 1, 3)))
                    if n == 0:
                        act.wait_ge(*mdiff_ready(pre.g, ago=1))
                    act.wait_ge(*r_ready(pre.g, ago=2))
                    af(dst[:, :], bank[BMISC][:, :], ACT.Copy, **affine).then_inc(maskT_saved.sem, 1)

                silu(1)
                silu(2)
                if tail is not None:
                    act.wait_ge(*out_ready(tail.g))
                    act.wait_ge(*back_ready(tail.g, ago=1))
                    af(oT[:, :], bank[BOUT][:, :], ACT.Copy).then_inc(outT_saved.sem, 1)
                if pre is not None:
                    act.wait_ge(*transposed(pre.gs))
                    act.wait_ge(*hidden_used(pre.g, ago=2))
                    af(tT[pre.p][:, :], bank[BMISC][:, :], ACT.Copy, scale=normw[:, 0:1])
                    af(ts[pre.p][0], bank[BMISC][:, :], ACT.Copy, scale=normw[:, 0:1]).then_inc(t_ready.sem, 1)
                silu(3)
                silu(4)
                if pre is not None:
                    act.wait_ge(*delta(pre.g))
                    act.wait_ge(*maskT_ready(pre.g, ago=1))
                    af(th[:, :], dlt[:, :], ACT.Tanh, scale=0.5).then_inc(tanh_done.sem, 1)
                    act.wait_ge(*tanh_done(pre.g))
                    af(wts[:, :], th[:, :], ACT.Copy, scale=-0.5, bias=0.5).then_inc(slot_w.sem, 1)
                silu(5)
                mask(0, mT[pre.p][0] if pre is not None else None)
                silu(6)
                mask(1, mT[pre.p][1] if pre is not None else None)
                mask(2, wT[pre.p][0] if pre is not None else None)
                mask(3, wT[pre.p][1] if pre is not None else None, scale=-1.0, bias=1.0)
                silu(7)
                silu(8)
                if pre is not None:
                    g, p = pre.g, pre.p
                    act.wait_ge(*h3_ready(g, ago=2))
                    for i in range(2):
                        for k, (dst, src) in enumerate(((uas[p][i][0], ua[i]), (uds[p][i][0], ud[i]))):
                            act.wait_ge(*u_masked(g, 2 * i + k + 1))
                            af(dst, src[:, :], ACT.Copy).then_inc(u_high.sem, 1)

            def l0_attn(st, pre, gat, nrm, up, dn):
                if gat is not None:
                    g = gat.g
                    act.wait_ge(*oa_ready(g, ago=1))
                    for n, (b, dst, bias) in enumerate(((1, gi, bif[:, 0:1]), (2, gf, bif[:, 1:2]), (3, go, vecs[:, 5:6]))):
                        act.wait_ge(*gates_ready(g, n + 1))
                        af(dst[:, :], bank[b][:, :], ACT.Sigmoid, bias=bias).then_inc(gates_saved.sem, 1)
                if up is not None:
                    act.wait_ge(*h2T_ready(up.g))
                    af(h2T[:, :], bank[7][:, :], ACT.Identity, bias=vecs[:, 3:4], scale=vecs[:, 2:3]).then_inc(h2T_saved.sem, 1)
                if dn is not None:
                    act.wait_ge(*mo_ready(dn.g))
                    act.wait_ge(*mback_ready(dn.g, ago=1))
                    af(moT[:, :], bank[4][:, :], ACT.Identity, bias=vecs[:, 6:7]).then_inc(moT_saved.sem, 1)
                if pre is not None and isinstance(pre.c, int) and pre.c == 0:
                    act.wait_ge(weights_loaded.sem, 16 * len(loads))
                    for n, w in enumerate((wi_b, wf_b)):
                        af(w[:, :], wif[:, n:n + 1].to_broadcast([P, P]), ACT.Copy).then_inc(spread.sem, 1)
                if pre is not None:
                    act.wait_ge(*transposed(pre.gs))
                    act.wait_ge(*gates_ready(pre.g, ago=2))
                    af(hT[pre.p][:, :], bank[7][:, :], ACT.Identity, bias=vecs[:, 1:2], scale=vecs[:, 0:1]
                       ).then_inc(hT_saved.sem, 1)
                if up is not None:
                    g = up.g
                    act.wait_ge(*m_leaky(g, ago=1))
                    for j in range(JM):
                        act.wait_ge(*m_ready(g, j + 1))
                        af(mpre[j][:, :], bank[5 + j % 2][:, :], ACT.Identity, bias=bm1[:, j:j + 1]).then_inc(m_saved.sem, 1)
                if up is not None:
                    act.wait_ge(*mo_ready(g, ago=1))
                    for j in range(JM):
                        act.wait_ge(*m_leaky(g, j + 1))
                        af(msq[j][:, :], mlk[j][:, :], ACT.Square).then_inc(m_squared.sem, 1)

            def route(st, pre, srt):
                if pre is not None:
                    act.wait_ge(*transposed(pre.gs))
                    act.wait_ge(*aff_ready(pre.g, ago=2))
                    af(xnT[pre.p % 2][:, :], bank[6][:, :], ACT.Copy).then_inc(xnT_saved.sem, 1)
                if srt is not None:
                    act.wait_ge(*alpha_arg(srt.g))
                    act.wait_ge(*alpha_ready(srt.g, ago=1))
                    af(alt[:, :], ala[:, :], ACT.Tanh, scale=0.5).then_inc(alpha_tanh.sem, 1)

            def expert(n0, n1, n2, n3):
                e_n0, = experts(act, kept_act, n0, n3, n0)
                if n0 is not None:
                    p, e = n0.p % 2, e_n0
                    act.wait_ge(*tile_T(n0.g))
                    act.wait_ge(*hid_ready(n0.g, ago=2))
                    af(xlT[p][:, :], bank[4 + p][:, 0:P], ACT.Identity, bias=lnb[:, bass.ds(e, 1)], scale=lng[:, bass.ds(e, 1)]
                       ).then_inc(xlT_saved.sem, 1)
                if n2 is not None:
                    p = n2.p % 2
                    act.wait_ge(*hbT_ready(n2.g))
                    act.wait_ge(*o_ready(n2.g, ago=2))
                    af(hbT[p][:, :], bank[2 + p][:, :], ACT.Relu).then_inc(hbT_saved.sem, 1)

            def l1_attn(st, pre, main):
                def rows(n):
                    if main is None:
                        return
                    g = main.g
                    if n < T:
                        k = n % 2
                        act.wait_ge(*nmax_done(g, n + 1))
                        act.wait_ge(*pT_ready(g, n - 1))
                        act.wait_ge(*rsum_done(g, n - 1))
                        af(pr_[k][:, :], bank[k][:, :], ACT.Exp, bias=nmx[:, k:k + 1], accum_out=rs[:, k:k + 1]
                           ).then_inc(exp_done.sem, 1)
                    if 1 <= n <= T:
                        k = (n - 1) % 2
                        act.wait_ge(*pT_ready(g, n))
                        act.wait_ge(*ao_ready(g, n - 2))
                        af(pT[k][:, :], bank[2 + k][:, :], ACT.Copy).then_inc(pT_saved.sem, 1)

                rows(0)
                if pre is not None:
                    act.wait_ge(*transposed(pre.gs))
                    act.wait_ge(*ao_ready(pre.g, ago=2))
                    af(yT[pre.p][:, :], bank[7][:, :], ACT.Copy).then_inc(yT_saved.sem, 1)
                rows(1)
                rows(2)
                rows(3)
                if pre is not None:
                    act.wait_ge(*zT_ready(pre.g))
                    af(zT[pre.p][:, :], bank[7][:, :], ACT.Copy).then_inc(zT_saved.sem, 1)
                rows(4)
                if pre is not None:
                    act.wait_ge(*v_ready(pre.g))
                    af(fl(vu[pre.p]), bank[7][:, :], ACT.Copy).then_inc(v_saved.sem, 1)

            for stage, (kind, call) in enumerate(STAGES):
                before_stage(act, stage)
                run_stage(act, stage, {"l0f": l0_ffn, "l0a": l0_attn, "l1f": route, "l1a": l1_attn})
                if kind == "l1f":
                    if call == 0:
                        products()
                    act.wait_ge(*tabs_ready(call))
                    pipeline(act, NT, 4, 4, call, stage, expert, first=5)

        @block.vector
        def _(dve):
            v = nc.vector
            bc = lambda ap: ap.unsqueeze(2).to_broadcast([P, T, E])

            def aggregate(g, halves, tmp, meanvar, done, ready, squares):
                even, odd = (lambda n: halves[:, :, n]), (lambda n: halves[:, :, 3 + n])
                dve.wait_ge(*done(g, 1))
                v.tensor_tensor(tmp[:, 0, :], even(1), odd(1), ALU.add)
                v.tensor_tensor(tmp[:, 1, :], even(1), odd(1), ALU.subtract)
                v.tensor_tensor(tmp[:, 2, :], even(2), odd(2), ALU.add).then_inc(done.sem, 1)
                dve.wait_ge(*done(g, 2))
                v.tensor_scalar(meanvar[:, :, 0], tmp[:, 0, :], 0.5, None, ALU.mult)
                v.scalar_tensor_tensor(tmp[:, 3, :], tmp[:, 1, :], 0.25, tmp[:, 1, :], ALU.mult, ALU.mult).then_inc(done.sem, 1)
                dve.wait_ge(*done(g, 3))
                v.scalar_tensor_tensor(meanvar[:, :, 1], tmp[:, 2, :], 1.0 / P, tmp[:, 3, :], ALU.mult, ALU.add
                                       ).then_inc(done.sem, 1)
                dve.wait_ge(*done(g, 4))
                for dst, f, c in squares:
                    last = v.tensor_scalar(dst, meanvar[:, :, 1], f, c, ALU.mult, ALU.add)
                last.then_inc(ready.sem, 1)

            def statistics(st, eps2, rows=(1, 3)):
                if st is None:
                    return
                if st.stage:
                    dve.wait_ge(*x_done(st.gs, ago=NCH))
                elif isinstance(st.c, int) and st.c == 1:
                    dve.wait_ge(x_loaded.sem, 16)
                v.memset(held[:, 0:1], 0.0)
                for t in range(T):
                    last = v.bn_stats(stats[:, t, :], xc(st)[:, t, :])
                last.then_inc(bn_done.sem, 1)
                p = st.p % 2
                aggregate(st.gs, stats, part, mv[p], bn_done, stats_ready, [
                    (sc[p][:, r - 1, :], *((1.0, EPS_LN) if r == 1 else (1.0 + eps2, eps2 * EPS_LN))) for r in rows])

            def normalise(pre, row, residual, free=None):
                if pre is None:
                    return
                p, yp = pre.p % 2, (yn4 if free else yn)[pre.p]
                dve.wait_ge(*scale_steps(pre.gs))
                dve.wait_ge(*transposed(pre.gs, ago=2))
                if free:
                    dve.wait_ge(*free)
                    v.tensor_tensor(invs[:, :], sc[p][:, 2, :], sc[p][:, 3, :], ALU.mult).then_inc(inv_steps.sem, 1)
                for on, dst, r in ((residual, ys[p], 1), (True, yp, row)):
                    for t in range(T * on):
                        last = v.tensor_scalar(dst[:, t, :], xc(pre)[:, t, :], mv[p][:, t, 0:1], sc[p][:, r, t:t + 1],
                                               ALU.subtract, ALU.mult)
                last.then_inc(normed.sem, 1)
                if free:
                    dve.wait_ge(*inv_steps(pre.g, 1))
                    v.tensor_tensor(inv[p][:, :], invs[:, :], sc[p][:, 1, :], ALU.mult).then_inc(inv_steps.sem, 1)

            def l0_ffn(st, pre, main, tail):
                def hidden(k):
                    if main is None:
                        return
                    (j, s), g, p = STEPS[k - 1], main.g, main.p
                    dve.wait_ge(*silu_done(g, k))
                    dve.wait_ge(*h3_ready(g, k))
                    dve.wait_ge(*hidden_used(g, j - 1))
                    a = act_[s][j % 2]
                    v.tensor_tensor(a[:, :], bank[BH3[j % 2]][:, :], sil[(k - 1) % 2][:, :], ALU.mult).then_inc(act_done.sem, 1)
                    dve.wait_ge(*act_done(g, k))
                    dve.wait_ge(*summed(g, j - 1))
                    if k == 1:
                        dve.wait_ge(*maskT_saved(g))
                    v.tensor_tensor(gab[s][j % 2][:, :], a[:, :], wT[p][s][:, :], ALU.mult).then_inc(weighted.sem, 1)

                def top2(s):
                    if pre is None:
                        return
                    g, n, l = pre.g, 5 * s, (lg, lg2)[s]

                    def link(ins, n):
                        ins.then_inc(top2_steps.sem, 1)
                        dve.wait_ge(*top2_steps(g, n))

                    if s == 0:
                        dve.wait_ge(*logits_ready(g))
                        dve.wait_ge(*maskT_ready(g, ago=1))
                        v.tensor_copy(lg[:, :, :].rearrange("p t e -> p (t e)"), bank[BMISC][:, 0:T * E]).then_inc(logits_read.sem, 1)
                        dve.wait_ge(*logits_read(g))
                    else:
                        dve.wait_ge(*onehots(g, 1))
                        link(v.scalar_tensor_tensor(lg2[:, :, :], oh[0][:, :, :, 0], -3e38, lg[:, :, :], ALU.mult, ALU.add), 5)
                    link(v.tensor_reduce(mx[:, 2 * s, :], l[:, :, :], AX, ALU.max), n + 1)
                    link(v.tensor_tensor(gt[:, :, :], l[:, :, :], bc(mx[:, 2 * s, :]), ALU.is_ge), n + 2)
                    link(v.tensor_tensor(pr[:, :, :], gt[:, :, :], pri[:, :, :], ALU.mult), n + 3)
                    link(v.tensor_reduce(mx[:, 2 * s + 1, :], pr[:, :, :], AX, ALU.max), n + 4)
                    for t in range(T):
                        last = v.tensor_tensor(oh[s][:, t, :, :], pr[:, t, :].unsqueeze(2).to_broadcast([P, E, R]),
                                               mx[:, 2 * s + 1, t:t + 1].unsqueeze(2).to_broadcast([P, E, R]), ALU.is_equal)
                    last.then_inc(onehots.sem, 1)
                    if s == 1:
                        dve.wait_ge(*tanh_done(g, ago=1))
                        v.tensor_tensor(dlt[:, :], mx[:, 2, :], mx[:, 0, :], ALU.subtract).then_inc(delta.sem, 1)

                def masked(i):
                    if pre is None:
                        return
                    g, p = pre.g, pre.p
                    dve.wait_ge(*u_ready(g, i + 1))
                    dve.wait_ge(*mdiff_ready(g))
                    dve.wait_ge(*u_low(g, ago=1))
                    v.tensor_tensor(ua[i][:, :], bank[BMISC][:, :], mT[p][0][:, :], ALU.mult).then_inc(u_masked.sem, 1)
                    v.tensor_tensor(ud[i][:, :], bank[BMISC][:, :], mdT[:, :], ALU.mult).then_inc(u_masked.sem, 1)

                hidden(1)
                normalise(pre, 3, False)
                hidden(2)
                if tail is not None:
                    dve.wait_ge(*back_ready(tail.g))
                    v.scalar_tensor_tensor(xc(tail), tok(bank[BOUT][:, :]), 0.5, xc(tail), ALU.mult, ALU.add
                                           ).then_inc(x_done.sem, 1)
                hidden(3)
                top2(0)
                hidden(4)
                top2(1)
                hidden(5)
                if pre is not None and first_chunk(pre):
                    for n, (dst, w, f) in enumerate(SPLITS):
                        dve.wait_ge(weight_high.sem, n + 1)
                        v.scalar_tensor_tensor(dst[1], w[:, :], f, dst[0].bitcast(F32), ALU.mult, ALU.subtract
                                               ).then_inc(weight_low.sem, 1)
                hidden(6)
                hidden(7)
                masked(0)
                hidden(8)
                masked(1)
                statistics(st, EPS_RMS, rows=(3,))
                if main is not None:
                    g, p = main.g, main.p
                    dve.wait_ge(*hidden_used(g))
                    dve.wait_ge(*masks_weighted(g))
                    dve.wait_ge(*out_ready(g, ago=1))
                    v.tensor_tensor(r1[:, :], bank[BV[0]][:, :], mT[p][0][:, :], ALU.mult)
                    v.tensor_tensor(r2[:, :], bank[BV[1]][:, :], mT[p][1][:, :], ALU.mult).then_inc(r_steps.sem, 2)
                    dve.wait_ge(*r_steps(g))
                    v.tensor_tensor(rr[:, :], r1[:, :], r2[:, :], ALU.add).then_inc(r_ready.sem, 1)

            def l0_attn(st, pre, gat, nrm, up, dn):
                if up is not None:
                    dve.wait_ge(*scale2_steps(up.g))
                    dve.wait_ge(*h2T_ready(up.g, ago=1))
                    for t in range(T):
                        last = v.tensor_scalar(h2[:, t, :], z[:, t, :], mv2[:, t, 0:1], sc2[:, 1, t:t + 1],
                                               ALU.subtract, ALU.mult)
                    last.then_inc(normed2.sem, 1)
                if nrm is not None:
                    dve.wait_ge(*z_added(nrm.g, ago=1))
                    g = nrm.g
                    dve.wait_ge(*oab_ready(g))
                    v.tensor_scalar(denc[:, 0, :], bank[6][:, 0:T], EPS_DEN, None, ALU.add).then_inc(den_steps.sem, 1)
                    dve.wait_ge(*den_steps(g, 1))
                    v.reciprocal(denc[:, 1, :], denc[:, 0, :]).then_inc(den_steps.sem, 1)
                    dve.wait_ge(*den_steps(g, 2))
                    for t in range(T):
                        last = v.scalar_tensor_tensor(z[:, t, :], bank[5][:, t * P:(t + 1) * P], denc[:, 1, t:t + 1],
                                                      ys[nrm.p][:, t, :], ALU.mult, ALU.add)
                    last.then_inc(z_ready.sem, 1)
                    dve.wait_ge(*z_ready(g))
                    v.memset(held[:, 0:1], 0.0)
                    for t in range(T):
                        last = v.bn_stats(stats2[:, t, :], z[:, t, :])
                    last.then_inc(bn2_done.sem, 1)
                normalise(pre, 3, True)
                if nrm is not None:
                    aggregate(g, stats2, part2, mv2, bn2_done, stats2_ready, [(sc2[:, 0, :], 1.0, EPS_LN)])
                if gat is not None:
                    g = gat.g
                    dve.wait_ge(*gates_saved(g))
                    dve.wait_ge(*gates_ready(g))
                    dve.wait_ge(*oab_ready(g, ago=1))
                    dve.wait_ge(*oa_ready(g, ago=1))
                    v.scalar_tensor_tensor(iv[:, :], bank[0][:, :], vecs[:, 4:5], gi[:, :], ALU.add, ALU.mult
                                           ).then_inc(scan_steps.sem, 1)
                    v.tensor_tensor_scan(den[:, :], gf[:, :], gi[:, :], 0.0, ALU.mult, ALU.add).then_inc(scan_steps.sem, 1)
                    dve.wait_ge(*scan_steps(g, 1))
                    v.tensor_tensor_scan(num[:, :], gf[:, :], iv[:, :], 0.0, ALU.mult, ALU.add).then_inc(scan_steps.sem, 1)
                if up is not None:
                    g = up.g
                    for j in range(JM):
                        dve.wait_ge(*m_saved(g, j + 1))
                        dve.wait_ge(*m_squared(g, ago=1))
                        v.scalar_tensor_tensor(mlk[j][:, :], mpre[j][:, :], LEAK, mpre[j][:, :], ALU.mult, ALU.max
                                               ).then_inc(m_leaky.sem, 1)
                if dn is not None:
                    dve.wait_ge(*mback_ready(dn.g))
                    dve.wait_ge(*z_added(dn.g))
                    v.tensor_tensor(xc(dn), tok(bank[4][:, :]), xc(dn), ALU.add).then_inc(x_done.sem, 1)
                statistics(st, EPS_LN)

            def route(st, pre, srt):
                normalise(pre, 3, True, scattered[pre.p](pre.h, ago=1) if pre is not None else None)
                if pre is not None:
                    v.tensor_copy(yw[pre.p][:, :, P:W], token[:, bass.ds(pre.c * T, T)].unsqueeze(2)).then_inc(numbered.sem, 1)
                if srt is not None:
                    g, p = srt.g, srt.p % 2

                    def link(ins, n):
                        ins.then_inc(top1_steps.sem, 1)
                        dve.wait_ge(*top1_steps(g, n))

                    dve.wait_ge(*aff_ready(g))
                    dve.wait_ge(*rank_ready(g, ago=2))
                    v.tensor_copy(lg[:, :, :].rearrange("p t e -> p (t e)"), bank[7][:, 0:T * E]).then_inc(aff_saved.sem, 1)
                    dve.wait_ge(*aff_saved(g))
                    link(v.tensor_reduce(mx[:, 0, :], lg[:, :, :], AX, ALU.max), 1)
                    dve.wait_ge(*alpha_tanh(g, ago=1))
                    dve.wait_ge(*inv_steps(g))
                    v.tensor_tensor(ala[:, :], mx[:, 0, :], inv[p][:, :], ALU.mult).then_inc(alpha_arg.sem, 1)
                    link(v.tensor_tensor(gt[:, :, :], lg[:, :, :], bc(mx[:, 0, :]), ALU.is_ge), 2)
                    link(v.tensor_tensor(pr[:, :, :], gt[:, :, :], pri[:, :, :], ALU.mult), 3)
                    link(v.tensor_reduce(mx[:, 1, :], pr[:, :, :], AX, ALU.max), 4)
                    v.tensor_tensor(oh1[p][:, :, :], pr[:, :, :], bc(mx[:, 1, :]), ALU.is_equal).then_inc(top1_done.sem, 1)
                statistics(st, EPS_LN)
                if pre is not None:
                    dve.wait_ge(*normed(pre.gs))
                    v.scalar_tensor_tensor(xc(pre), ys[pre.p % 2][:, :, :], 0.5, xc(pre), ALU.mult, ALU.add).then_inc(x_done.sem, 1)
                if srt is not None:
                    dve.wait_ge(*rank_ready(g))
                    dve.wait_ge(*top1_done(g))
                    v.tensor_tensor(pos[:, :, :], bank[5][:, 0:T * E].rearrange("p (t e) -> p t e", t=T),
                                    nxt[:, :].unsqueeze(1).to_broadcast([P, T, E]), ALU.add).then_inc(row_steps.sem, 1)
                    dve.wait_ge(*row_steps(g, 1))
                    v.tensor_tensor(nxt[:, :], bank[5][:, T * E:T * E + E], nxt[:, :], ALU.add).then_inc(rank_read.sem, 1)
                    v.tensor_tensor(pos[:, :, :], pos[:, :, :], oh1[p][:, :, :], ALU.mult).then_inc(row_steps.sem, 1)
                    dve.wait_ge(*row_steps(g, 2))
                    v.tensor_reduce(slot[:, :], pos[:, :, :], AX, ALU.add).then_inc(row_steps.sem, 1)
                    dve.wait_ge(*row_steps(g, 3))
                    dve.wait_ge(*scattered[srt.p](srt.h, ago=1))
                    v.tensor_copy(slot_i[srt.p][:, :], slot[:, :]).then_inc(rows_ready.sem, 1)
                    dve.wait_ge(*alpha_tanh(g))
                    v.tensor_scalar(alpha[:, bass.ds(srt.c * T, T)], alt[:, :], 0.25, 0.25, ALU.mult, ALU.add
                                    ).then_inc(alpha_ready.sem, 1)

            def tables(call):
                def link(ins, n):
                    ins.then_inc(tab_steps.sem, 1)
                    dve.wait_ge(*tab_steps(call, n))

                dve.wait_ge(*alpha_ready(NCH * call + NCH - 1))
                v.tensor_copy(pad_i[:, :], nxt[:, :]).then_inc(ends_ready.sem, 1)
                link(v.tensor_tensor(cnt[:, :], nxt[:, :], region[:, :], ALU.subtract), 1)
                link(v.tensor_scalar(cnt_i[:, :], cnt[:, :], float(P - 1), None, ALU.add), 2)
                link(v.tensor_scalar(nt_i[:, :], cnt_i[:, :], P.bit_length() - 1, None, ALU.arith_shift_right), 3)
                link(v.tensor_copy(ntf[:, :], nt_i[:, :]), 4)
                v.tensor_scalar(jump[:, :], ntf[:, :], float(-P), float(REGION), ALU.mult, ALU.add)
                link(v.tensor_tensor_scan(ends[:, :], one8[:, :], ntf[:, :], 0.0, ALU.mult, ALU.add), 5)
                over_e = lambda ap, n=NT: ap.unsqueeze(1).to_broadcast([P, n, E])
                link(v.tensor_tensor(past[:, :, :], tile_no[:, :].unsqueeze(2).to_broadcast([P, NT, E]), over_e(ends[:, :]),
                                     ALU.is_ge), 6)
                v.tensor_reduce(tab[:, 0, :], past[:, :, :], AX, ALU.add)
                link(v.tensor_tensor(hop[:, :, :], past[:, :, :], over_e(jump[:, :]), ALU.mult), 7)
                link(v.tensor_reduce(tab[:, 1, :], hop[:, :, :], AX, ALU.add), 8)
                v.tensor_scalar(tab_e[:, :], tab[:, 0, :], float(E - 1), None, ALU.min)
                v.scalar_tensor_tensor(tab_row[:, :], tile_no[:, :], float(P), tab[:, 1, :], ALU.mult, ALU.add
                                       ).then_inc(tabs_ready.sem, 1)

            def expert(n0, n1, n2, n3):
                e_n1, e_n3 = experts(dve, kept_dve, n0, n3, n1, n3)
                if n1 is not None:
                    dve.wait_ge(*tile_in[n1.p](n1.h))
                    dve.wait_ge(*tile_out[n1.p](n1.h, ago=1))
                    v.tensor_copy(ids[n1.p][:, :], xin[n1.p][:, P:W]).then_inc(ids_ready.sem, 1)
                    p, e = n1.p % 2, e_n1
                    dve.wait_ge(*hid_ready(n1.g))
                    dve.wait_ge(*hbT_ready(n1.g, ago=2))
                    v.tensor_tensor(hb[p][:, :], bank[p][:, :], eb1b[:, bass.ds(e, 1), :].rearrange("p a f -> p (a f)"), ALU.add
                                    ).then_inc(hb_ready.sem, 1)
                if n3 is not None:
                    p, e = n3.p % 2, e_n3
                    dve.wait_ge(*o_ready(n3.g))
                    dve.wait_ge(*tile_out[n3.p](n3.h, ago=1))
                    v.tensor_tensor(ob[n3.p][:, :], bank[6 + p][:, 0:P], eb2b[:, bass.ds(e, 1), :].rearrange("p a d -> p (a d)"), ALU.add
                                    ).then_inc(ob_ready.sem, 1)

            def arrive(ch):
                if ch is None:
                    return
                dve.wait_ge(*fetched[ch.p](ch.h))
                for t in range(T):
                    xt = xc(ch)[:, t, :]
                    last = v.scalar_tensor_tensor(xt, got[ch.p][:, t, :], alpha[:, bass.ds(ch.c * T + t, 1)], xt,
                                                  ALU.mult, ALU.add)
                last.then_inc(arrived.sem, 1)
                dve.wait_ge(*arrived(ch.g))

            def l1_attn(st, pre, main):
                def rows(n):
                    if main is None:
                        return
                    g = main.g
                    if n < T:
                        k = slice(n % 2, n % 2 + 1)
                        dve.wait_ge(*sc_ready(g, n + 1))
                        dve.wait_ge(*exp_done(g, n - 1))
                        v.tensor_reduce(mxr[:, k], bank[n % 2][:, :], AX, ALU.max).then_inc(max_done.sem, 1)
                        dve.wait_ge(*max_done(g, n + 1))
                        v.tensor_scalar(nmx[:, k], mxr[:, k], -1.0, None, ALU.mult).then_inc(nmax_done.sem, 1)
                    if 1 <= n <= T:
                        k = slice((n - 1) % 2, (n - 1) % 2 + 1)
                        dve.wait_ge(*exp_done(g, n))
                        v.reciprocal(rsi[:, n - 1:n], rs[:, k]).then_inc(rsum_done.sem, 1)
                    if n >= 2:
                        dve.wait_ge(*rsum_done(g, n - 1))
                        dve.wait_ge(*ao_ready(g, n - 1))
                        xi = xc(main)[:, n - 2, :]
                        v.scalar_tensor_tensor(xi, bank[4 + n % 2][:, 0:P], rsi[:, n - 2:n - 1], xi, ALU.mult, ALU.add
                                               ).then_inc(ao_done.sem, 1)

                rows(0)
                normalise(pre, 1, False)
                rows(1)
                rows(2)
                rows(3)
                arrive(st)
                rows(4)
                statistics(st, None, rows=(1,))
                rows(5)
                if main is not None:
                    dve.wait_ge(*ao_done(main.g))
                    v.tensor_copy(tick[:, :], rsi[:, 0:1]).then_inc(x_done.sem, 1)

            dve.wait_ge(*constants(0))
            dve.wait_ge(x0_loaded.sem, 16)
            for stage, (kind, call) in enumerate(STAGES):
                if kind == "l1f":
                    v.tensor_copy(nxt[:, :], region[:, :]).then_inc(routing_reset.sem, 1)
                    dve.wait_ge(*routing_reset(call))
                run_stage(dve, stage, {"l0f": l0_ffn, "l0a": l0_attn, "l1f": route, "l1a": l1_attn})
                if kind == "l1f":
                    tables(call)
                    dve.wait_ge(*tabs_ready(call))
                    dve.wait_ge(late_loaded.sem, 16 * len(late_loads))
                    pipeline(dve, NT, 4, 4, call, stage, expert, first=5)
            if STAGES[-1][0] == "l1f":
                pipeline(dve, NCH, 2, 1, CALLS - 1, stage, arrive)

        @block.gpsimd
        def _(pool):
            pool.memset(ident[:, :], 0.0).then_inc(zeroed.sem, 1)
            pool.wait_ge(zeroed.sem, 1)
            pool.affine_select(out=ident[:, :], in_=ident[:, :], compare_op=ALU.not_equal, fill=1.0, base=0,
                               pattern=[[-1, P]], channel_multiplier=1).then_inc(constants.sem, 1)
            pool.memset(neghalf[:, :], -0.5).then_inc(constants.sem, 1)
            pool.wait_ge(constants.sem, 1)
            pool.tensor_copy(ident_bf[:, :], ident[:, :]).then_inc(constants.sem, 1)
            for e in range(E):
                pool.memset(pri[:, :, e:e + 1], float(E - e)).then_inc(constants.sem, 1)
            for e in range(E):
                pool.memset(region[:, e:e + 1], float(e * REGION)).then_inc(constants.sem, 1)
            pool.memset(one8[:, :], 1.0).then_inc(constants.sem, 1)
            pool.memset(zrow[:, :, 0:P], 0.0).then_inc(constants.sem, 1)
            pool.memset(ones[:, :], 1.0).then_inc(constants.sem, 1)
            pool.memset(lower[:, :], 1.0).then_inc(zeroed.sem, 1)
            pool.wait_ge(zeroed.sem, 2)
            pool.affine_select(out=lower[:, :], in_=lower[:, :], compare_op=ALU.is_gt, fill=0.0, base=0,
                               pattern=[[1, P]], channel_multiplier=-1).then_inc(constants.sem, 1)
            pool.iota(tile_i[:, :], pattern=[[1, NT]], base=0, channel_multiplier=0).then_inc(zeroed.sem, 1)
            pool.wait_ge(zeroed.sem, 3)
            pool.tensor_copy(tile_no[:, :], tile_i[:, :]).then_inc(constants.sem, 1)
            pool.iota(token_i[:, :], pattern=[[P, NCH * T + 2 * E]], base=0, channel_multiplier=1).then_inc(zeroed.sem, 1)
            pool.wait_ge(zeroed.sem, 4)
            pool.tensor_copy(token[:, :], token_i[:, :]).then_inc(constants.sem, 1)
            pool.tensor_copy(zrow[:, :, P:W], token_i[:, NCH * T:].unsqueeze(2)).then_inc(constants.sem, 1)
            pool.wait_ge(*constants(0))

            def scales(st, rows=(1, 3)):
                if st is None:
                    return
                pool.wait_ge(*stats_ready(st.gs))
                pool.wait_ge(*normed(st.gs, ago=2))
                for r in rows:
                    pool.tensor_tensor(sc[st.p % 2][:, r, :], sc[st.p % 2][:, r - 1, :], neghalf[:, :], ALU.pow
                                       ).then_inc(scale_steps.sem, 2 // len(rows))

            def l0_ffn(st, pre, main, tail):
                def total(j):
                    if main is None:
                        return
                    g = main.g
                    pool.wait_ge(*weighted(g, LAST[j]))
                    pool.wait_ge(*hidden_used(g, j - 1))
                    pool.tensor_tensor(out=gsum[j % 2][:, :], in0=gab[0][j % 2][:, :], in1=gab[1][j % 2][:, :], op=ALU.add
                                       ).then_inc(summed.sem, 1)
                if pre is not None:
                    p = pre.p
                    pool.wait_ge(*t_ready(pre.g))
                    pool.wait_ge(*hidden_used(pre.g, ago=2))
                    pool.tensor_tensor(out=ts[p][1], in0=tT[p][:, :], in1=ts[p][0].bitcast(F32), op=ALU.subtract
                                       ).then_inc(t_low.sem, 1)
                total(0)
                total(1)
                if pre is not None:
                    pool.wait_ge(*maskT_saved(pre.g, 2))
                    pool.wait_ge(*u_masked(pre.g, ago=1))
                    pool.tensor_tensor(out=mdT[:, :], in0=mT[pre.p][1][:, :], in1=mT[pre.p][0][:, :], op=ALU.subtract
                                       ).then_inc(mdiff_ready.sem, 1)
                total(2)
                total(3)
                if pre is not None:
                    g, p = pre.g, pre.p
                    for i in range(2):
                        for k, (dst, src) in enumerate(((uas[p][i], ua[i]), (uds[p][i], ud[i]))):
                            pool.wait_ge(*u_high(g, 2 * i + k + 1))
                            pool.tensor_tensor(out=dst[1], in0=src[:, :], in1=dst[0].bitcast(F32), op=ALU.subtract
                                               ).then_inc(u_low.sem, 1)
                scales(st, rows=(3,))
                if pre is not None:
                    pool.wait_ge(*u_masked(pre.g))
                    pool.wait_ge(*maskT_saved(pre.g))
                    for s in range(2):
                        m = mT[pre.p][s]
                        pool.tensor_tensor(out=m[:, :], in0=m[:, :], in1=wT[pre.p][s][:, :], op=ALU.mult
                                           ).then_inc(masks_weighted.sem, 1)

            def l0_attn(st, pre, gat, nrm, up, dn):
                if nrm is not None:
                    g = nrm.g
                    pool.wait_ge(*z_ready(g))
                    pool.tensor_tensor(out=xc(nrm), in0=xc(nrm), in1=z[:, :, :], op=ALU.add).then_inc(z_added.sem, 1)
                    pool.wait_ge(*stats2_ready(g))
                    pool.wait_ge(*normed2(g, ago=1))
                    pool.tensor_tensor(sc2[:, 1, :], sc2[:, 0, :], neghalf[:, :], ALU.pow).then_inc(scale2_steps.sem, 1)
                if gat is not None:
                    g = gat.g
                    pool.wait_ge(*scan_steps(g))
                    pool.wait_ge(*gates_saved(g))
                    pool.wait_ge(*oab_ready(g, ago=1))
                    pool.tensor_tensor(out=oaT[:, :], in0=num[:, :], in1=go[:, :], op=ALU.mult).then_inc(oa_ready.sem, 1)
                scales(st)

            def carry_wait(ready, g, done, n):
                pool.wait_ge(*done(g, ago=1))
                pool.wait_ge(*ready(g))
                pool.tensor_tensor(out=held[:, n:n + 1], in0=one8[:, 0:1], in1=one8[:, 0:1], op=ALU.mult).then_inc(done.sem, 1)

            def route(st, pre, srt):
                scales(st)
                if srt is not None:
                    carry_wait(rows_ready, srt.g, carried_s, 1)
                    for t in range(T):
                        pool.indirect_dma_start(rows_in[:, :], bass.IndirectOffsetOnAxis(slot_i[srt.p][:, t:t + 1], 0),
                                                yw[srt.p][:, t, :], None).then_inc(scattered[srt.p].sem, 16)

            def expert(n0, n1, n2, n3):
                if n3 is not None:
                    carry_wait(ob_ready, n3.g, carried_o, 2)
                    pool.indirect_dma_start(rows_out[:, :], bass.IndirectOffsetOnAxis(ids[n3.p][:, 0:1], 0), ob[n3.p][:, :], None
                                            ).then_inc(tile_out[n3.p].sem, 16)

            def l1_attn(st, pre, main):
                scales(st, rows=(1,))

            for stage, (kind, call) in enumerate(STAGES):
                run_stage(pool, stage, {"l0f": l0_ffn, "l0a": l0_attn, "l1f": route, "l1a": l1_attn})
                if kind == "l1f":
                    pipeline(pool, NT, 4, 4, call, stage, expert, first=5)



def kernel(**inputs):
    import concourse.bacc as bacc
    from concourse.bass_utils import run_bass_kernel_spmd as run

    i = {n: np.asarray(a) for n, a in inputs.items()}
    f, a, m, t = "L0_ffn_", "L0_attn_", "L1_ffn_", "L1_attn_"
    D = P
    lay = {
        "x": i["L0_attn_x"].reshape(-1, D),
        "w1": i[f + "w1"].T, "w3": i[f + "w3"].T,
        "w2": i[f + "w2"].T.reshape(J, P, D).transpose(1, 0, 2),
        "gate": i[f + "gate_w"].T, "normw": i[f + "norm_w"].reshape(D, 1),
        "a1": i[f + "a1"].reshape(E * R, D).T, "a3": i[f + "a3"].reshape(E * R, D).T,
        "a2": i[f + "a2"].reshape(E * R, J, P).transpose(2, 1, 0),
        "b1": i[f + "b1"].transpose(0, 2, 1).reshape(E * R, J * P),
        "b3": i[f + "b3"].transpose(0, 2, 1).reshape(E * R, J * P),
        "b2": i[f + "b2"].transpose(0, 2, 1).reshape(E * R, D),
        "vecs": np.stack([i[a + n] for n in ("ln1_g", "ln1_b", "ln2_g", "ln2_b", "bv", "bo", "b2")], axis=1),
        "bif": np.stack([i[a + "bi"], i[a + "bf"]], axis=1),
        "wif": np.concatenate([i[a + "Wi"], i[a + "Wf"]], axis=1),
        "wv": i[a + "Wv"], "wo": i[a + "Wo"], "wm1": i[a + "W1"],
        "bm1": i[a + "b1"].reshape(JM, P).T, "wm2": i[a + "W2"].reshape(JM, P, D).transpose(1, 0, 2),
        "wk_l1": i[t + "Wk"], "wq_l1": i[t + "Wq"], "wv_l1": i[t + "Wv"], "waT": i[t + "Wa"].T, "wbT": i[t + "Wb"].T,
        "cen": i[m + "centroids"].T, "lng": i[m + "ln_g"].T, "lnb": i[m + "ln_b"].T,
        "e1": i[m + "w1"].transpose(1, 0, 2), "eb1": i[m + "b1"].reshape(1, -1),
        "e2": i[m + "w2"].reshape(E, J, P, D).transpose(2, 0, 1, 3), "eb2": i[m + "b2"].reshape(1, -1),
    }
    lay = {n: np.ascontiguousarray(w) for n, w in lay.items()}
    nc = bacc.Bacc("TRN2", target_bir_lowering=False, num_devices=1)
    d = {n: nc.dram_tensor(n + "_dram", w.shape, mybir.dt.from_np(w.dtype), kind="ExternalInput").ap() for n, w in lay.items()}
    out = nc.dram_tensor("out", i["L0_attn_x"].shape, F32, kind="ExternalOutput").ap()
    build(nc, d, out)
    r = run(nc, [{n + "_dram": w for n, w in lay.items()}], core_ids=[0])
    return r.results[0]["out"]
```
